# Optimizing a Trainium2 kernel written in Bass

```python
import numpy as np
import jax
import jax.numpy as jnp

def _softmax(x, axis=-1):
    return jax.nn.softmax(x, axis=axis)

def _gelu(x):
    return jax.nn.gelu(x, approximate=True)

def _silu(x):
    return jax.nn.silu(x)

def _sigmoid(x):
    return jax.nn.sigmoid(x)

def _layernorm(x, axis=-1, eps=1e-05):
    m = jnp.mean(x, axis=axis, keepdims=True)
    v = jnp.var(x, axis=axis, keepdims=True)
    return (x - m) / jnp.sqrt(v + eps)

def _scatter_add(tgt, idx, src, axis=0):
    return tgt.at[idx].add(src)

def _segment_sum(src, seg, n):
    return jax.ops.segment_sum(src, seg, n)
kernel_name = 'mk_decoder_postln_d2_seqx_r8_329c3f'

def setup_inputs(seed: int=0):
    np.random.seed(seed)
    _w = jnp.asarray

    def _rec_inputs():
        import jax
        import jax.numpy as jnp
        _rk = jax.random.key(seed)
        x = 7.22e-05 + 1 * jax.random.normal(jax.random.fold_in(_rk, 1), (32, 128, 128), jnp.float32)
        _lenS = 128 - jax.random.randint(jax.random.fold_in(_rk, 7), (32,), 0, max(1, 128 // 4) + 1, jnp.int32)
        _lenS2 = 120 - jax.random.randint(jax.random.fold_in(_rk, 8), (32,), 0, max(1, 120 // 4) + 1, jnp.int32)
        _ctx_1024P = jax.random.normal(jax.random.fold_in(_rk, 11), (32, 16, 128), jnp.float32)
        _ctx_1024c = jax.random.dirichlet(jax.random.fold_in(_rk, 511), 0.3 * jnp.ones((16,), jnp.float32), (32, 120))
        _ctx_1024t = jnp.einsum('bsk,bkd->bsd', _ctx_1024c, _ctx_1024P)
        _ctx_1024t = _ctx_1024t * jax.lax.rsqrt(jnp.mean(jnp.square(_ctx_1024t)) + 1e-12) * 0.953939
        ctx_1024 = 4.13588e-05 + 0.999923 * (_ctx_1024t + 0.3 * jax.random.normal(jax.random.fold_in(_rk, 611), (32, 120, 128), jnp.float32))
        _validS = jnp.arange(128)[None, :] < _lenS[:, None]
        _validS2 = jnp.arange(120)[None, :] < _lenS2[:, None]
        _causal = jnp.tril(jnp.ones((128, 128), dtype=bool))
        mask_1x1xSxS2_fk1 = jnp.where(jnp.broadcast_to(_validS2[0:1, None, None, :], (1, 1, 128, 120)), 1.0, 0.0).astype(jnp.float32)
        mask_Bx1xSxS2_ff0 = jnp.where(jnp.ones((32, 1, 128, 120), dtype=bool), 0.0, -1000000000.0).astype(jnp.float32)
        return (x, ctx_1024, mask_1x1xSxS2_fk1, mask_Bx1xSxS2_ff0)
    x, ctx_1024, mask_1x1xSxS2_fk1, mask_Bx1xSxS2_ff0 = _rec_inputs()

    def _L0_attn_setup():
        import jax, jax.numpy as jnp
        import numpy as np
        N_HEADS = 16
        SEG = 64
        D_MODEL = 128
        NOISE_EPS = 1e-05

        def _forward(hidden_states, Wq, Wk, Wv, Wc, terrace_mix, index_decays, mega_decays):
            b, L, d = hidden_states.shape
            H, seg = (N_HEADS, SEG)
            Dh = d // H
            r = L // seg
            q = (hidden_states @ Wq.T).reshape(b, L, H, Dh)
            k = (hidden_states @ Wk.T).reshape(b, L, H, Dh)
            v = (hidden_states @ Wv.T).reshape(b, L, H, Dh)
            scores = jnp.einsum('bnhd,bmhd->bhnm', q, k) / jnp.sqrt(jnp.float32(Dh))
            idx = jnp.arange(L)
            causal = idx[:, None] >= idx[None, :]
            dblk = (idx // seg)[:, None] - (idx // seg)[None, :]
            neg = jnp.float32(-jnp.inf)
            scores = jnp.where(causal, scores, neg)
            terrace_allowed = causal & ((dblk == 0) | (dblk == 1))
            scores_t = jnp.where(terrace_allowed, scores, neg)
            att_t = jax.nn.softmax(scores_t, axis=-1)
            out_t = jnp.einsum('bhnm,bmhd->bhnd', att_t, v).reshape(b, H, r, seg, Dh)
            att = jax.nn.softmax(scores, axis=-1)
            awc = att.reshape(b, H, r, seg, L) * jnp.exp(index_decays)[None, :, None, :, None]
            pcs = awc.sum(axis=-2)
            mega = jnp.clip(jnp.exp(mega_decays * seg), 0.0, 2.0)
            s_seq = jnp.moveaxis(pcs, 2, 0)

            def step(carry, s):
                return (carry * mega[None, :, None] + s, carry)
            _, outs = jax.lax.scan(step, jnp.zeros_like(s_seq[0]), s_seq)
            w = jnp.moveaxis(outs, 0, 2)
            w = w / (w.sum(axis=-1, keepdims=True) + NOISE_EPS)
            kv = jnp.einsum('bhrs,bshd,bshe->brhde', w, k, v)
            qc = q.reshape(b, r, seg, H, Dh)
            out_lin = jnp.einsum('brlhd,brhde->bhrle', qc, kv)
            tw = jax.nn.sigmoid(terrace_mix)[None, None, None, :, None]
            y = tw * out_t + (1.0 - tw) * out_lin
            y = y.reshape(b, H, L, Dh).transpose(0, 2, 1, 3).reshape(b, L, d)
            return y @ Wc.T
        key = jax.random.key(seed)
        ks = jax.random.split(key, 8)
        b, L, d = (1, 256, D_MODEL)
        sc = 0.02
        hidden_states = jax.random.normal(ks[0], (b, L, d), jnp.float32)
        Wq = sc * jax.random.normal(ks[1], (d, d), jnp.float32)
        Wk = sc * jax.random.normal(ks[2], (d, d), jnp.float32)
        Wv = sc * jax.random.normal(ks[3], (d, d), jnp.float32)
        Wc = sc * jax.random.normal(ks[4], (d, d), jnp.float32)
        terrace_mix = 0.5 * jnp.ones((SEG,), jnp.float32)
        index_decays = -0.1 * jnp.ones((N_HEADS, SEG), jnp.float32) + 0.01 * jax.random.normal(ks[5], (N_HEADS, SEG), jnp.float32)
        mega_decays = -0.1 * jnp.ones((N_HEADS,), jnp.float32) + 0.01 * jax.random.normal(ks[6], (N_HEADS,), jnp.float32)
        return dict(hidden_states=hidden_states, Wq=Wq, Wk=Wk, Wv=Wv, Wc=Wc, terrace_mix=terrace_mix, index_decays=index_decays, mega_decays=mega_decays)
    _L0_attn_all = _L0_attn_setup()
    _L0_attn_in = {k: v for k, v in _L0_attn_all.items() if k in ('Wq', 'Wk', 'Wv', 'Wc', 'terrace_mix', 'index_decays', 'mega_decays')}
    del _L0_attn_all

    def _L0_xattn_setup():
        import jax, jax.numpy as jnp
        import numpy as np
        D_MODEL = 128
        NUM_HEADS = 16
        DEPTH = D_MODEL // NUM_HEADS
        B, S = (4, 256)
        NEG = -1000000000.0

        def _split_heads(x):
            b, s, _ = x.shape
            return x.reshape(b, s, NUM_HEADS, DEPTH).transpose(0, 2, 1, 3)
        key = jax.random.key(seed)
        ks = jax.random.split(key, 12)
        q = jax.random.normal(ks[0], (B, S, D_MODEL), dtype=jnp.float32)
        k = jax.random.normal(ks[1], (B, S, D_MODEL), dtype=jnp.float32)
        v = jax.random.normal(ks[2], (B, S, D_MODEL), dtype=jnp.float32)
        mask = (1.0 - jnp.tril(jnp.ones((S, S), dtype=jnp.float32)))[None, None]
        scale = 1.0 / np.sqrt(D_MODEL)
        Wq = jax.random.normal(ks[3], (D_MODEL, D_MODEL), dtype=jnp.float32) * scale
        Wk = jax.random.normal(ks[4], (D_MODEL, D_MODEL), dtype=jnp.float32) * scale
        Wv = jax.random.normal(ks[5], (D_MODEL, D_MODEL), dtype=jnp.float32) * scale
        Wo = jax.random.normal(ks[6], (D_MODEL, D_MODEL), dtype=jnp.float32) * scale
        bq = jnp.zeros((D_MODEL,), jnp.float32)
        bk = jnp.zeros((D_MODEL,), jnp.float32)
        bv = jnp.zeros((D_MODEL,), jnp.float32)
        bo = jnp.zeros((D_MODEL,), jnp.float32)
        return {'query': q, 'key': k, 'value': v, 'mask': mask, 'Wq': Wq, 'bq': bq, 'Wk': Wk, 'bk': bk, 'Wv': Wv, 'bv': bv, 'Wo': Wo, 'bo': bo}
    _L0_xattn_all = _L0_xattn_setup()
    _L0_xattn_in = {k: v for k, v in _L0_xattn_all.items() if k in ('Wq', 'bq', 'Wk', 'bk', 'Wv', 'bv', 'Wo', 'bo')}
    del _L0_xattn_all

    def _L0_ffn_setup():
        import jax, jax.numpy as jnp
        import numpy as np
        D = 128
        F = 352
        E = 8
        TOP_K = 2
        key = jax.random.key(seed)
        ks = jax.random.split(key, 6)
        std = 0.02
        x = jax.random.normal(ks[0], (2, 256, D), dtype=jnp.float32)
        router_w = jax.random.normal(ks[1], (D, E), dtype=jnp.float32) * std
        w1 = jax.random.normal(ks[2], (E, D, F), dtype=jnp.float32) * std
        v1 = jax.random.normal(ks[3], (E, D, F), dtype=jnp.float32) * std
        w2 = jax.random.normal(ks[4], (E, F, D), dtype=jnp.float32) * std
        bias = jnp.zeros((D,), dtype=jnp.float32)
        return {'x': x, 'router_w': router_w, 'w1': w1, 'v1': v1, 'w2': w2, 'bias': bias}
    _L0_ffn_all = _L0_ffn_setup()
    _L0_ffn_in = {k: v for k, v in _L0_ffn_all.items() if k in ('router_w', 'w1', 'v1', 'w2', 'bias')}
    del _L0_ffn_all

    def _L1_attn_setup():
        import jax, jax.numpy as jnp
        import numpy as np
        B, N, C = (8, 512, 128)
        key = jax.random.key(seed)
        k1, k2, k3 = jax.random.split(key, 3)
        x = jax.random.normal(k1, (B, N, C), dtype=jnp.float32)
        w_qkv = jax.random.normal(k2, (3 * C, C), dtype=jnp.float32) * C ** (-0.5)
        w_conv1 = jax.random.normal(k3, (C,), dtype=jnp.float32) * C ** (-0.5)
        return {'x': x, 'w_qkv': w_qkv, 'w_conv1': w_conv1}
    _L1_attn_all = _L1_attn_setup()
    _L1_attn_in = {k: v for k, v in _L1_attn_all.items() if k in ('w_qkv', 'w_conv1')}
    del _L1_attn_all

    def _L1_xattn_setup():
        import jax, jax.numpy as jnp
        import numpy as np
        HIDDEN = 128
        NUM_HEADS = 16
        DEPTH = HIDDEN // NUM_HEADS
        B, F, T = (2, 256, 256)
        key = jax.random.key(seed)
        ks = jax.random.split(key, 6)
        scale = 1.0 / np.sqrt(HIDDEN)
        return {'query_input': jax.random.normal(ks[0], (B, F, HIDDEN), dtype=jnp.float32), 'source_input': jax.random.normal(ks[1], (B, T, HIDDEN), dtype=jnp.float32), 'bias': jnp.zeros((B, 1, F, T), dtype=jnp.float32), 'wq': jax.random.normal(ks[2], (HIDDEN, NUM_HEADS, DEPTH), dtype=jnp.float32) * scale, 'wk': jax.random.normal(ks[3], (HIDDEN, NUM_HEADS, DEPTH), dtype=jnp.float32) * scale, 'wv': jax.random.normal(ks[4], (HIDDEN, NUM_HEADS, DEPTH), dtype=jnp.float32) * scale, 'wo': jax.random.normal(ks[5], (NUM_HEADS, DEPTH, HIDDEN), dtype=jnp.float32) * scale}
    _L1_xattn_all = _L1_xattn_setup()
    _L1_xattn_in = {k: v for k, v in _L1_xattn_all.items() if k in ('wq', 'wk', 'wv', 'wo')}
    del _L1_xattn_all

    def _L1_ffn_setup():
        import jax, jax.numpy as jnp
        import numpy as np
        FP8_MAX = 448.0
        FP8 = jnp.float8_e4m3fn
        key = jax.random.key(seed)
        kx, kw, kb = jax.random.split(key, 3)
        B, S, D_in, D_out = (4, 1024, 128, 128)
        x = jax.random.normal(kx, (B, S, D_in), dtype=jnp.float32)
        w = jax.random.normal(kw, (D_out, D_in), dtype=jnp.float32) * 0.02
        weight_scale = jnp.maximum(jnp.max(jnp.abs(w)), 1e-12) / FP8_MAX
        weight = (w / weight_scale).astype(FP8)
        bias = jax.random.normal(kb, (D_out,), dtype=jnp.float32) * 0.01
        return {'x': x, 'weight': weight, 'weight_scale': weight_scale, 'bias': bias}
    _L1_ffn_all = _L1_ffn_setup()
    _L1_ffn_in = {k: v for k, v in _L1_ffn_all.items() if k in ('weight', 'weight_scale', 'bias')}
    del _L1_ffn_all
    return {'x': x, 'ctx_1024': ctx_1024, 'mask_1x1xSxS2_fk1': mask_1x1xSxS2_fk1, 'mask_Bx1xSxS2_ff0': mask_Bx1xSxS2_ff0, 'L0_attn_Wq': _L0_attn_in['Wq'], 'L0_attn_Wk': _L0_attn_in['Wk'], 'L0_attn_Wv': _L0_attn_in['Wv'], 'L0_attn_Wc': _L0_attn_in['Wc'], 'L0_attn_terrace_mix': _L0_attn_in['terrace_mix'], 'L0_attn_index_decays': _L0_attn_in['index_decays'], 'L0_attn_mega_decays': _L0_attn_in['mega_decays'], 'L0_xattn_Wq': _L0_xattn_in['Wq'], 'L0_xattn_bq': _L0_xattn_in['bq'], 'L0_xattn_Wk': _L0_xattn_in['Wk'], 'L0_xattn_bk': _L0_xattn_in['bk'], 'L0_xattn_Wv': _L0_xattn_in['Wv'], 'L0_xattn_bv': _L0_xattn_in['bv'], 'L0_xattn_Wo': _L0_xattn_in['Wo'], 'L0_xattn_bo': _L0_xattn_in['bo'], 'L0_ffn_router_w': _L0_ffn_in['router_w'], 'L0_ffn_w1': _L0_ffn_in['w1'], 'L0_ffn_v1': _L0_ffn_in['v1'], 'L0_ffn_w2': _L0_ffn_in['w2'], 'L0_ffn_bias': _L0_ffn_in['bias'], 'L1_attn_w_qkv': _L1_attn_in['w_qkv'], 'L1_attn_w_conv1': _L1_attn_in['w_conv1'], 'L1_xattn_wq': _L1_xattn_in['wq'], 'L1_xattn_wk': _L1_xattn_in['wk'], 'L1_xattn_wv': _L1_xattn_in['wv'], 'L1_xattn_wo': _L1_xattn_in['wo'], 'L1_ffn_weight': _L1_ffn_in['weight'], 'L1_ffn_weight_scale': _L1_ffn_in['weight_scale'], 'L1_ffn_bias': _L1_ffn_in['bias']}

def reference(x, ctx_1024, mask_1x1xSxS2_fk1, mask_Bx1xSxS2_ff0, L0_attn_Wq, L0_attn_Wk, L0_attn_Wv, L0_attn_Wc, L0_attn_terrace_mix, L0_attn_index_decays, L0_attn_mega_decays, L0_xattn_Wq, L0_xattn_bq, L0_xattn_Wk, L0_xattn_bk, L0_xattn_Wv, L0_xattn_bv, L0_xattn_Wo, L0_xattn_bo, L0_ffn_router_w, L0_ffn_w1, L0_ffn_v1, L0_ffn_w2, L0_ffn_bias, L1_attn_w_qkv, L1_attn_w_conv1, L1_xattn_wq, L1_xattn_wk, L1_xattn_wv, L1_xattn_wo, L1_ffn_weight, L1_ffn_weight_scale, L1_ffn_bias):
    import jax
    import jax.numpy as jnp

    def _L0_attn_ref(hidden_states, Wq, Wk, Wv, Wc, terrace_mix, index_decays, mega_decays):
        import jax, jax.numpy as jnp
        import numpy as np
        N_HEADS = 16
        SEG = 64
        D_MODEL = 128
        NOISE_EPS = 1e-05

        def _forward(hidden_states, Wq, Wk, Wv, Wc, terrace_mix, index_decays, mega_decays):
            b, L, d = hidden_states.shape
            H, seg = (N_HEADS, SEG)
            Dh = d // H
            r = L // seg
            q = (hidden_states @ Wq.T).reshape(b, L, H, Dh)
            k = (hidden_states @ Wk.T).reshape(b, L, H, Dh)
            v = (hidden_states @ Wv.T).reshape(b, L, H, Dh)
            scores = jnp.einsum('bnhd,bmhd->bhnm', q, k) / jnp.sqrt(jnp.float32(Dh))
            idx = jnp.arange(L)
            causal = idx[:, None] >= idx[None, :]
            dblk = (idx // seg)[:, None] - (idx // seg)[None, :]
            neg = jnp.float32(-jnp.inf)
            scores = jnp.where(causal, scores, neg)
            terrace_allowed = causal & ((dblk == 0) | (dblk == 1))
            scores_t = jnp.where(terrace_allowed, scores, neg)
            att_t = jax.nn.softmax(scores_t, axis=-1)
            out_t = jnp.einsum('bhnm,bmhd->bhnd', att_t, v).reshape(b, H, r, seg, Dh)
            att = jax.nn.softmax(scores, axis=-1)
            awc = att.reshape(b, H, r, seg, L) * jnp.exp(index_decays)[None, :, None, :, None]
            pcs = awc.sum(axis=-2)
            mega = jnp.clip(jnp.exp(mega_decays * seg), 0.0, 2.0)
            s_seq = jnp.moveaxis(pcs, 2, 0)

            def step(carry, s):
                return (carry * mega[None, :, None] + s, carry)
            _, outs = jax.lax.scan(step, jnp.zeros_like(s_seq[0]), s_seq)
            w = jnp.moveaxis(outs, 0, 2)
            w = w / (w.sum(axis=-1, keepdims=True) + NOISE_EPS)
            kv = jnp.einsum('bhrs,bshd,bshe->brhde', w, k, v)
            qc = q.reshape(b, r, seg, H, Dh)
            out_lin = jnp.einsum('brlhd,brhde->bhrle', qc, kv)
            tw = jax.nn.sigmoid(terrace_mix)[None, None, None, :, None]
            y = tw * out_t + (1.0 - tw) * out_lin
            y = y.reshape(b, H, L, Dh).transpose(0, 2, 1, 3).reshape(b, L, d)
            return y @ Wc.T
        return _forward(hidden_states, Wq, Wk, Wv, Wc, terrace_mix, index_decays, mega_decays)

    def _L0_xattn_ref(query, key, value, mask, Wq, bq, Wk, bk, Wv, bv, Wo, bo):
        import jax, jax.numpy as jnp
        import numpy as np
        D_MODEL = 128
        NUM_HEADS = 16
        DEPTH = D_MODEL // NUM_HEADS
        B, S = (4, 256)
        NEG = -1000000000.0

        def _split_heads(x):
            b, s, _ = x.shape
            return x.reshape(b, s, NUM_HEADS, DEPTH).transpose(0, 2, 1, 3)
        q = _split_heads(query @ Wq + bq)
        k = _split_heads(key @ Wk + bk)
        v = _split_heads(value @ Wv + bv)
        scores = jnp.einsum('bhqd,bhkd->bhqk', q, k) / jnp.sqrt(jnp.asarray(DEPTH, q.dtype))
        scores = scores + mask * NEG
        weights = jax.nn.softmax(scores, axis=-1)
        out = jnp.einsum('bhqk,bhkd->bhqd', weights, v)
        out = out.transpose(0, 2, 1, 3).reshape(query.shape[0], -1, D_MODEL)
        return out @ Wo + bo

    def _L0_ffn_ref(x, router_w, w1, v1, w2, bias):
        import jax, jax.numpy as jnp
        import numpy as np
        D = 128
        F = 352
        E = 8
        TOP_K = 2
        B, S, d = x.shape
        xt = x.reshape(B * S, d)
        scores = jax.nn.softmax(xt @ router_w, axis=-1)
        expert_weights, expert_idx = jax.lax.top_k(scores, TOP_K)
        h = jax.nn.gelu(jnp.einsum('td,edf->tef', xt, w1), approximate=False) * jnp.einsum('td,edf->tef', xt, v1)
        y = jnp.einsum('tef,efd->ted', h, w2)
        yk = jnp.take_along_axis(y, expert_idx[:, :, None], axis=1)
        out = jnp.sum(expert_weights[:, :, None] * yk, axis=1) + bias
        return out.reshape(B, S, d)

    def _L1_attn_ref(x, w_qkv, w_conv1):
        import jax, jax.numpy as jnp
        import numpy as np
        B, N, C = (8, 512, 128)
        b, n, c = x.shape
        scale = c ** (-0.5)
        qkv = jnp.einsum('bnc,dc->bnd', x, w_qkv)
        q = qkv[..., :c]
        k = qkv[..., c:2 * c]
        v = qkv[..., 2 * c:]
        agent = jnp.einsum('bnc,c->bn', q, w_conv1)
        agent_attn = jax.nn.softmax(jnp.einsum('bn,bnc->bc', agent * scale, k), axis=-1)
        agent_v = jax.nn.softmax(jnp.einsum('bc,bnc->bn', agent_attn, v), axis=-1)
        agent_v = jnp.einsum('bn,bnc->bc', agent_v, v)
        agent_tok = jax.nn.softmax(agent[:, :, None], axis=-1)
        return agent_tok * agent_v[:, None, :]

    def _L1_xattn_ref(query_input, source_input, bias, wq, wk, wv, wo):
        import jax, jax.numpy as jnp
        import numpy as np
        HIDDEN = 128
        NUM_HEADS = 16
        DEPTH = HIDDEN // NUM_HEADS
        B, F, T = (2, 256, 256)
        q = jnp.einsum('bfh,hnd->bfnd', query_input, wq)
        k = jnp.einsum('bth,hnd->btnd', source_input, wk)
        v = jnp.einsum('bth,hnd->btnd', source_input, wv)
        q = q * DEPTH ** (-0.5)
        logits = jnp.einsum('btnd,bfnd->bnft', k, q) + bias
        weights = jax.nn.softmax(logits, axis=-1)
        attn = jnp.einsum('bnft,btnd->bfnd', weights, v)
        return jnp.einsum('bfnd,ndh->bfh', attn, wo)

    def _L1_ffn_ref(x, weight, weight_scale, bias):
        import jax, jax.numpy as jnp
        import numpy as np
        FP8_MAX = 448.0
        FP8 = jnp.float8_e4m3fn
        amax = jnp.max(jnp.abs(x), axis=-1, keepdims=True)
        x_scale = jnp.maximum(amax, 1e-12) / FP8_MAX
        qinput = (x / x_scale).astype(FP8)
        A = qinput.astype(x.dtype) * x_scale
        Bm = weight.astype(x.dtype) * weight_scale
        out = jnp.einsum('bsk,nk->bsn', A, Bm) + bias
        return out.astype(x.dtype)
    x = _layernorm(x + _L0_attn_ref(x, L0_attn_Wq, L0_attn_Wk, L0_attn_Wv, L0_attn_Wc, L0_attn_terrace_mix, L0_attn_index_decays, L0_attn_mega_decays), axis=-1)
    x = _layernorm(x + _L0_xattn_ref(x, ctx_1024, ctx_1024, mask_1x1xSxS2_fk1, L0_xattn_Wq, L0_xattn_bq, L0_xattn_Wk, L0_xattn_bk, L0_xattn_Wv, L0_xattn_bv, L0_xattn_Wo, L0_xattn_bo), axis=-1)
    x = _layernorm(x + _L0_ffn_ref(x, L0_ffn_router_w, L0_ffn_w1, L0_ffn_v1, L0_ffn_w2, L0_ffn_bias), axis=-1)
    x = _layernorm(x + _L1_attn_ref(x, L1_attn_w_qkv, L1_attn_w_conv1), axis=-1)
    x = _layernorm(x + _L1_xattn_ref(x, ctx_1024, mask_Bx1xSxS2_ff0, L1_xattn_wq, L1_xattn_wk, L1_xattn_wv, L1_xattn_wo), axis=-1)
    x = _layernorm(x + _L1_ffn_ref(x, L1_ffn_weight, L1_ffn_weight_scale, L1_ffn_bias), axis=-1)
    return x

_drawn_inputs = setup_inputs


def setup_inputs(seed=0):
    import zlib

    import numpy as np

    out = dict(_drawn_inputs(seed))
    spreads = {'L0_attn_terrace_mix': (0.5, 0.6),
     'L0_xattn_bq': (0.0, 0.287),
     'L0_xattn_bk': (0.0, 0.8),
     'L0_xattn_bv': (0.0, 0.1),
     'L0_xattn_bo': (0.0, 0.1),
     'L0_ffn_bias': (0.0, 0.1)}
    factors = {'L0_attn_Wq': 8.0,
     'L0_attn_Wk': 8.0,
     'L0_attn_Wv': 8.0,
     'L0_attn_Wc': 8.0,
     'L0_attn_index_decays': 8.0,
     'L0_ffn_router_w': 8.0,
     'L0_ffn_w1': 8.0,
     'L0_ffn_v1': 8.0,
     'L0_ffn_w2': 8.0,
     'L1_ffn_bias': 5.864}
    for name, (base, spread) in spreads.items():
        noise = np.random.default_rng([zlib.crc32(name.encode()), seed]).standard_normal(out[name].shape)
        drawn = base * np.exp(spread * noise) if base else spread * noise
        out[name] = jnp.asarray(drawn.astype(out[name].dtype))
    for name, factor in factors.items():
        out[name] = (out[name] * factor).astype(out[name].dtype)
    return out
```

```python
from contextlib import ExitStack

import numpy as np
import concourse.bass as bass
from concourse import mybir

ALU = mybir.AluOpType
ACT = mybir.ActivationFunctionType
AX = mybir.AxisListType
F32 = mybir.dt.float32
F16 = mybir.dt.float16
I32 = mybir.dt.int32
U8 = mybir.dt.uint8

NSEQ, S, D, S2 = 32, 128, 128, 120
H, DH, SEG = 16, 8, 64
NB = 4
NG = NSEQ // NB
NJ, NQ = 4, 4
TERM = 32
NE, FF = 8, 352
CH = [(e, q, min(128, FF - 128 * q)) for e in range(NE) for q in range(3)]
SLOTS = 3 * NB
NEG = -1000000000.0
EPS = 1e-5
BIG = 4
WQ, WK, WV, WO = range(4)


def reach(eng, sem, value):
    if isinstance(value, int) and value <= 0:
        return
    eng.wait_ge(sem, value)


def decoder(nc, x_d, ctx_d, mask0_d, mask1_d, w_d, bias_d, terrace_d, decay_d, mega_d, rw_d, w1_d, v1_d,
            w2_d, conv_d, w8_d, wscale_d, ident_d, causal_d, block_d, lower_d, out_d):
    with ExitStack() as ctx:
        def sb(name, shape, dt=F32):
            return ctx.enter_context(nc.sbuf_tensor(name, shape, dt))

        def ps(name):
            return ctx.enter_context(nc.psum_tensor(name, [128, 512], F32))

        def sem(name):
            return ctx.enter_context(nc.semaphore(name))

        pS = [ps("pS0"), ps("pS1")]
        pT = ps("pT")
        pM = ps("pM")
        pO = ps("pO")
        pA, pB, pY = ps("pA"), ps("pB"), ps("pY")

        ident = sb("ident", [128, 128])
        ident16 = sb("ident16", [128, 128], F16)
        causal = sb("causal", [128, 128])
        block_diag = sb("block_diag", [128, 128])
        lower = sb("lower", [128, NE * NE + NE])
        ones = sb("ones", [128, 128])
        w = sb("w", [128, 16, 128])
        bias = sb("bias", [128, 6, 128])
        mask0 = sb("mask0", [128, S2])
        mix = sb("mix", [128, 4])
        decay = sb("decay", [SEG, H])
        mega = sb("mega", [SEG, H])
        rw = sb("rw", [128, NE])
        w1h, w1l = sb("w1h", [128, NE, FF], F16), sb("w1l", [128, NE, FF], F16)
        v1h, v1l = sb("v1h", [128, NE, FF], F16), sb("v1l", [128, NE, FF], F16)
        wtmp = sb("wtmp", [128, 2, NE, FF])
        w2 = sb("w2", [128, NE, 3, 128])
        conv = sb("conv", [128, 1])
        u_col = sb("u_col", [128, 1])
        w8raw = sb("w8raw", [128, 128], U8)
        w8i = sb("w8i", [128, 4, 128], I32)
        w8f = sb("w8f", [128, 3, 128])
        w8 = sb("w8", [128, 128], F16)
        wscale = sb("wscale", [128, 1])
        half = sb("half", [128, 4])

        idle = sb("idle", [128, 4])

        xa = sb("xa", [128, NB, 128])
        xb = sb("xb", [128, NB, 128])
        xc = sb("xc", [128, NB, 128])
        yout = sb("yout", [128, NB, 128])
        ctxB = sb("ctxB", [128, NB, 128])
        ctxE = sb("ctxE", [128, NB, 128])
        mask1 = sb("mask1", [128, NB, S2])

        xcT = sb("xcT", [128, 2, 128])
        qk32 = sb("qk32", [128, BIG, 2, 128])
        qT32 = sb("qT32", [128, BIG, SEG])
        vaug = sb("vaug", [128, BIG, H, DH + 1])
        split = sb("split", [128, 2, 2, H, 4, DH], F16)
        splitT = sb("splitT", [128, 2, 2, NQ, 128], F16)
        P = sb("P", [128, BIG, NJ, NQ, 128])
        nmax = sb("nmax", [128, BIG, NJ, NQ])
        PT = sb("PT", [128, 2, NJ, NQ, 128])
        rz = sb("rz", [128, 2, H])
        carry_w = sb("carry_w", [SEG, 2, H])
        yo = sb("yo", [128, 2, 128])
        pcs = sb("pcs", [SEG, H])
        vp = sb("vp", [SEG, 128])
        kvm = sb("kvm", [128, 128])
        rsum = sb("rsum", [128, H])
        ylin = sb("ylin", [128, 128])
        yT = sb("yT", [128, 128])
        res = sb("res", [128, 2, 128])
        st6 = sb("st6", [128, 2, 6])
        mv = sb("mv", [128, 2, 2])
        ve = sb("ve", [128, 2])
        rstd = sb("rstd", [128, 2])

        gT32 = sb("gT32", [128, NB, 128])
        gTh, gTl = sb("gTh", [128, NB * 128], F16), sb("gTl", [128, NB * 128], F16)
        rt = sb("rt", [128, 8, NB, NE])
        rt64 = sb("rt64", [128, 2, NB, NE, NE])
        rts = sb("rts", [128, 4, NB])
        G = sb("G", [128, 2, 512])
        Hh = sb("Hh", [128, 2, 512])
        yw = sb("yw", [128, 2, NB, 128])
        acc = sb("acc", [128, NB, 128])
        gst = sb("gst", [128, NB, 6])
        gmv = sb("gmv", [128, NB, 2])
        gve = sb("gve", [128, NB])
        grs = sb("grs", [128, NB])
        dT = sb("dT", [128, NB, 128])
        dcol = sb("dcol", [128, 8, NB])
        drow = sb("drow", [NB, 4, 128])
        dstat = sb("dstat", [NB, 4])
        fq = sb("fq", [128, 3, NB, 128])
        fsc = sb("fsc", [128, 4, NB])
        f16T = sb("f16T", [128, NB, 128], F16)

        s_const = sem("s_const")
        s_w = sem("s_w")
        s_setup_dve, s_setup_act, s_setup_pe, s_setup_pool = (sem(f"s_setup_{n}") for n in ("dve", "act", "pe", "pool"))
        s_x, s_ctxB, s_ctxE, s_mask1, s_out = sem("s_x"), sem("s_ctxB"), sem("s_ctxE"), sem("s_mask1"), sem("s_out")
        s_xT, s_xT_ev = sem("s_xT"), sem("s_xT_ev")
        s_proj, s_proj_ev, s_qT_ev = sem("s_proj"), sem("s_proj_ev"), sem("s_qT_ev")
        s_split = sem("s_split")
        s_hi = sem("s_hi")
        s_splitT, s_splitT_ev = sem("s_splitT"), sem("s_splitT_ev")
        s_score, s_masked, s_max, s_shift, s_exp = (sem(n) for n in ("s_score", "s_masked", "s_max", "s_shift", "s_exp"))
        s_PT, s_PT_ev, s_pv = sem("s_PT"), sem("s_PT_ev"), sem("s_pv")
        s_rz, s_rzt, s_yo = sem("s_rz"), sem("s_rzt"), sem("s_yo")
        s_rl, s_pcs, s_vp, s_kv, s_kvm, s_lin, s_lin_ev = (sem(n) for n in (
            "s_rl", "s_pcs", "s_vp", "s_kv", "s_kvm", "s_lin", "s_lin_ev"))
        s_y = sem("s_y")
        s_yT, s_yT_ev, s_proj_out = sem("s_yT"), sem("s_yT_ev"), sem("s_proj_out")
        s_res, s_resb, s_st, s_mv, s_ve, s_rstd = (sem(n) for n in ("s_res", "s_resb", "s_st", "s_mv", "s_ve", "s_rstd"))
        s_ln = {"A": sem("s_lnA"), "B": sem("s_lnB"), "E": sem("s_lnE")}
        s_gT, s_gT_ev, s_gTl = sem("s_gT"), sem("s_gT_ev"), sem("s_gTl")
        s_rt, s_rt_dve, s_rt_exp = sem("s_rt"), sem("s_rt_dve"), sem("s_rt_exp")
        s_gate, s_val, s_gelu, s_h, s_y2, s_yw, s_acc = (sem(n) for n in (
            "s_gate", "s_val", "s_gelu", "s_h", "s_y2", "s_yw", "s_acc"))
        s_gst, s_gmv, s_gve, s_grs, s_gln = (sem(n) for n in ("s_gst", "s_gmv", "s_gve", "s_grs", "s_gln"))
        s_dpe, s_ddve, s_dact = sem("s_dpe"), sem("s_ddve"), sem("s_dact")
        s_fpe, s_fdve, s_fact = sem("s_fpe"), sem("s_fdve"), sem("s_fact")

        block = ctx.enter_context(nc.Block())

        def slots_of(n, stages):
            out = []
            for a, st in enumerate("ABE"):
                if st in stages:
                    out += [(st, b, n, n * SLOTS + a * NB + b) for b in range(NB)]
            return out

        def par(slot, m):
            a = "ABE".index(slot[0])
            return (a * NB + slot[1]) % m

        def mw(st):
            return S if st == "A" else S2

        wbase = {"A": 0, "B": 4, "E": 8}
        x_of = {"A": xa, "B": xa, "E": xc}
        dst_of = {"A": xa, "B": xb, "E": xc}

        RTD = 12
        DDVE, DACT = 22, 4
        FDVE = 14


        @block.sync
        def _(sp):
            def load_AB(n):
                reach(sp, s_ln["B"], NB * n)
                sp.dma_start(xa[:], x_d[bass.ds(n * NB, NB)].rearrange("b t d -> t b d")).then_inc(s_x, 16)
                sp.dma_start(ctxB[0:S2], ctx_d[bass.ds(n * NB, NB)].rearrange("b t d -> t b d")).then_inc(s_ctxB, 16)

            def load_E(n):
                reach(sp, s_ln["E"], NB * n)
                sp.dma_start(ctxE[0:S2], ctx_d[bass.ds(n * NB, NB)].rearrange("b t d -> t b d")).then_inc(s_ctxE, 16)
                sp.dma_start(mask1[:], mask1_d[bass.ds(n * NB, NB)].rearrange("b o t m -> t (b o) m")).then_inc(s_mask1, 16)

            def store(n):
                sp.wait_ge(s_gln, NB * 3 * n + 3 * NB)
                sp.dma_start(out_d[bass.ds(n * NB, NB)].rearrange("b t d -> t b d"), yout[:]).then_inc(s_out, 16)

            reach(sp, s_setup_pool, 1)
            sp.dma_start(w[:], w_d.rearrange("m p c -> p m c")).then_inc(s_w, 16)
            for dst, src in (
                (ident[:], ident_d), (causal[:], causal_d), (block_diag[:], block_d), (lower[:], lower_d),
                (bias[:].rearrange("p m c -> p (m c)"), bias_d.partition_broadcast(128)),
                (mask0[:], mask0_d[0, 0]), (mix[0:SEG, 0:1], terrace_d), (mix[SEG:128, 0:1], terrace_d),
                (decay[:], decay_d), (mega[:], mega_d.partition_broadcast(SEG)), (rw[:], rw_d), (conv[:], conv_d),
                (w8raw[:], w8_d), (wscale[:], wscale_d.partition_broadcast(128)),
                (wtmp[:, 0], w1_d.rearrange("e d f -> d e f")), (wtmp[:, 1], v1_d.rearrange("e d f -> d e f")),
                (w2[:, :, 0, :], w2_d[:, 0:128, :].rearrange("e p d -> p e d")),
                (w2[:, :, 1, :], w2_d[:, 128:256, :].rearrange("e p d -> p e d")),
                (w2[0:96, :, 2, :], w2_d[:, 256:352, :].rearrange("e p d -> p e d")),
            ):
                sp.dma_start(dst, src).then_inc(s_const, 16)
            load_AB(0)
            load_E(0)
            with sp.Fori(0, NG - 1) as n:
                load_AB(n + 1)
                load_E(n + 1)
                store(n)
            store(NG - 1)
            sp.wait_ge(s_out, 16 * NG)

        n_const = 16 * 19

        @block.tensor
        def _(pe):
            pe.wait_ge(s_const, n_const)
            pe.wait_ge(s_w, 16)
            pe.matmul(pY[:, 0:1], w[:, 12, :], conv[:], start=True, stop=True).then_inc(s_setup_pe, 1)
            pe.wait_ge(s_setup_dve, 13)
            pe.wait_ge(s_setup_pool, 5)

            def front_xT(slot):
                st, b, n, k = slot
                if st == "A":
                    pe.wait_ge(s_x, (n + 1) * 16)
                elif st == "B":
                    pe.wait_ge(s_ln["A"], n * NB + (b + 1))
                    pe.wait_ge(s_ctxB, (n + 1) * 16)
                else:
                    pe.wait_ge(s_gln, NB * 3 * n + (NB + b + 1))
                    pe.wait_ge(s_ctxE, (n + 1) * 16)
                reach(pe, s_splitT_ev, k)
                last = pe.transpose(pM[:, 0:128], x_of[st][:, b, :], ident[:])
                if st != "A":
                    last = pe.transpose(pM[:, 128:256], (ctxB if st == "B" else ctxE)[:, b, :], ident[:])
                last.then_inc(s_xT, 1)

            def front_proj(slot):
                st, b, n, k = slot
                pe.wait_ge(s_xT_ev, k + 1)
                base = wbase[st]
                wr = w[:].rearrange("p m c -> p (m c)")
                if st == "A":
                    pe.matmul(pM[:, 0:384], xcT[:, 0, :], wr[:, 0:384], start=True, stop=True)
                    last = pe.matmul(pM[:, 384:448], w[:, base + WQ, :], xcT[:, 0, SEG:128], start=True, stop=True)
                else:
                    pe.matmul(pM[:, 0:128], xcT[:, 0, :], w[:, base + WQ, :], start=True, stop=True)
                    last = pe.matmul(pM[:, 128:384], xcT[:, 1, :], wr[:, (base + WK) * 128:(base + WO) * 128],
                                     start=True, stop=True)
                last.then_inc(s_proj, 1)

            def front_split(slot):
                st, b, n, k = slot
                pe.wait_ge(s_split, k + 1)
                pe.wait_ge(s_proj_ev, 2 * k + 2)
                if st == "A":
                    pe.wait_ge(s_qT_ev, n * NB + (b + 1))
                m16 = pM[:].bitcast(F16)
                for r in range(2):
                    for g in range(NQ):
                        c = (r * NQ + g) * 128
                        last = pe.transpose(m16[:, c:c + 128],
                                            split[:, par(slot, 2), r, NQ * g:NQ * g + NQ].rearrange("p j t d -> p (j t d)"),
                                            ident16[:])
                last.then_inc(s_splitT, 1)

            def front_scores(slot, j):
                st, b, n, k = slot
                if j == 0:
                    pe.wait_ge(s_splitT_ev, k + 1)
                reach(pe, s_masked, 4 * k + (j - 1))
                for g in range(NQ):
                    r0 = TERM * j
                    last = pe.matmul(pS[j % 2][:, 128 * g:128 * g + mw(st)],
                                     splitT[r0:r0 + 24, par(slot, 2), 0, g, :],
                                     splitT[r0:r0 + 24, par(slot, 2), 1, g, 0:mw(st)], start=True, stop=True)
                last.then_inc(s_score, 1)

            def mid_transpose(slot, j):
                st, b, n, k = slot
                pe.wait_ge(s_exp, 4 * k + (j + 1))
                reach(pe, s_PT_ev, 4 * k + j)
                for g in range(NQ):
                    last = pe.transpose(pT[0:mw(st), 128 * g:128 * g + 128], P[:, par(slot, BIG), j, g, 0:mw(st)],
                                        ident[:])
                last.then_inc(s_PT, 1)

            def mid_values(slot):
                st, b, n, k = slot
                pe.wait_ge(s_PT_ev, 4 * k + 4)
                reach(pe, s_res, k)
                for h in range(H):
                    last = pe.matmul(pO[:, (DH + 1) * h:(DH + 1) * (h + 1)],
                                     PT[0:mw(st), par(slot, 2), h % NJ, h // NJ, :],
                                     vaug[0:mw(st), par(slot, BIG), h, :], start=True, stop=True)
                last.then_inc(s_pv, 1)

            def back_pcs(slot):
                st, b, n, k = slot
                if st != "A":
                    return
                pe.wait_ge(s_rl, n * NB + (b + 1))
                pe.wait_ge(s_yo, k + 1)
                for h in range(H):
                    last = pe.matmul(pO[:, h:h + 1], P[0:SEG, par(slot, BIG), h % NJ, h // NJ, :],
                                     carry_w[:, par(slot, 2), h:h + 1], start=True, stop=True)
                last.then_inc(s_pcs, 1)

            def back_kv(slot):
                st, b, n, k = slot
                if st != "A":
                    return
                pe.wait_ge(s_vp, 2 * (n * NB + (b + 1)))
                pe.matmul(pO[:, 0:128], qk32[0:SEG, par(slot, BIG), 1, :], vp[:], start=True, stop=True)
                pe.matmul(pO[SEG:128, 128:128 + H], ones[0:SEG, 0:SEG], pcs[:], start=True, stop=True).then_inc(s_kv, 1)

            def back_lin(slot):
                st, b, n, k = slot
                if st != "A":
                    return
                pe.wait_ge(s_kvm, 2 * (n * NB + (b + 1)))
                pe.matmul(pO[SEG:128, 0:128], qT32[:, par(slot, BIG), :], kvm[:], start=True, stop=True)\
                    .then_inc(s_lin, 1)

            def back_yT(slot):
                st, b, n, k = slot
                pe.wait_ge(s_yo, k + 1)
                if st == "A":
                    pe.wait_ge(s_y, n * NB + (b + 1))
                pe.transpose(pO[:, 0:128], yo[:, par(slot, 2), :], ident[:]).then_inc(s_yT, 1)

            def back_out(slot):
                st, b, n, k = slot
                pe.wait_ge(s_yT_ev, k + 1)
                pe.matmul(pO[:, 0:128], yT[:], w[:, wbase[st] + WO, :], start=True, stop=True).then_inc(s_proj_out, 1)

            def attention(slots):
                N = len(slots)
                for s in range(N + 3):
                    f = slots[s] if s < N else None
                    m = slots[s - 2] if 0 <= s - 2 < N else None
                    k = slots[s - 3] if 0 <= s - 3 < N else None
                    if f: front_xT(f)
                    if k: back_pcs(k)
                    if m: mid_transpose(m, 0)
                    if f: front_proj(f)
                    if k: back_kv(k)
                    if m: mid_transpose(m, 1)
                    if k: back_lin(k)
                    if f: front_split(f)
                    if m: mid_transpose(m, 2)
                    if k: back_yT(k)
                    if m: mid_transpose(m, 3)
                    if f:
                        front_scores(f, 0)
                        front_scores(f, 1)
                    if k: back_out(k)
                    if f:
                        front_scores(f, 2)
                        front_scores(f, 3)
                    if m: mid_values(m)

            def ffn(n):
                pe.wait_ge(s_ln["B"], NB * (n + 1))
                reach(pe, s_fdve, FDVE * n)
                for b in range(NB):
                    last = pe.transpose(pA[:, 128 * b:128 * b + 128], xb[:, b, :], ident[:])
                last.then_inc(s_gT, 1)
                pe.wait_ge(s_gT_ev, 2 * n + 1)
                for b in range(NB):
                    last = pe.matmul(pY[:, NE * b:NE * b + NE], gT32[:, b, :], rw[:], start=True, stop=True)
                last.then_inc(s_rt, 1)

                def out_part(c):
                    e, q, m = CH[c]
                    pe.wait_ge(s_h, n * len(CH) + (c + 1))
                    if q == 0:
                        if e == 0:
                            pe.wait_ge(s_rt_dve, RTD * n + 1)
                        else:
                            pe.wait_ge(s_yw, NE * n + e)
                    for b in range(NB):
                        last = pe.matmul(pY[:, 128 * b:128 * b + 128], Hh[0:m, c % 2, 128 * b:128 * b + 128],
                                         w2[0:m, e, q, :], start=(q == 0 and b == 0), stop=(q == 2),
                                         skip_group_check=True)
                    last.then_inc(s_y2, 1)

                for c, (e, q, m) in enumerate(CH):
                    for bank, hi, lo, done, free in ((pA, w1h, w1l, s_gate, s_gelu), (pB, v1h, v1l, s_val, s_h)):
                        if c == 0:
                            pe.wait_ge(s_gT_ev, 2 * n + 2)
                            pe.wait_ge(s_gTl, n + 1)
                        else:
                            pe.wait_ge(free, n * len(CH) + c)
                        fs = slice(128 * q, 128 * q + m)
                        pe.matmul(bank[0:m, :], hi[:, e, fs], gTh[:], start=True, stop=False)
                        pe.matmul(bank[0:m, :], hi[:, e, fs], gTl[:], start=False, stop=False)
                        pe.matmul(bank[0:m, :], lo[:, e, fs], gTh[:], start=False, stop=True).then_inc(done, 1)
                    if c >= 1:
                        out_part(c - 1)
                out_part(len(CH) - 1)

            def agent(n):
                def d_ready(i):
                    pe.wait_ge(s_ddve, DDVE * n + i)

                def done(ins):
                    ins.then_inc(s_dpe, 1)

                pe.wait_ge(s_gln, NB * (3 * n + 1))
                for b in range(NB):
                    last = pe.transpose(pA[:, 128 * b:128 * b + 128], xc[:, b, :], ident[:])
                done(last)
                pe.wait_ge(s_dact, DACT * n + 1)
                for b in range(NB):
                    last = pe.matmul(pY[:, b:b + 1], dT[:, b, :], u_col[:], start=True, stop=True)
                done(last)
                d_ready(1)
                for b in range(NB):
                    last = pe.matmul(pY[:, b:b + 1], xc[:, b, :], dcol[:, 0, b:b + 1], start=True, stop=True)
                done(last)
                d_ready(3)
                done(pe.matmul(pY[0:NB, 0:128], dcol[:, 1, :], w[:, 13, :], start=True, stop=True))
                d_ready(6)
                done(pe.matmul(pY[:, 0:NB], drow[:, 1, :], ident[0:NB, 0:NB], start=True, stop=True))
                d_ready(7)
                done(pe.matmul(pY[:, 0:NB], w[:, 14, :], dcol[:, 2, :], start=True, stop=True))
                d_ready(8)
                for b in range(NB):
                    last = pe.matmul(pY[:, b:b + 1], dT[:, b, :], dcol[:, 3, b:b + 1], start=True, stop=True)
                done(last)
                d_ready(9)
                done(pe.transpose(pY[0:NB, 0:128], dcol[:, 4, :], ident[:]))
                d_ready(12)
                done(pe.matmul(pY[:, 0:NB], drow[:, 3, :], ident[0:NB, 0:NB], start=True, stop=True))
                d_ready(13)
                for b in range(NB):
                    last = pe.matmul(pY[:, b:b + 1], xc[:, b, :], dcol[:, 5, b:b + 1], start=True, stop=True)
                done(last)
                d_ready(14)
                for b in range(NB):
                    last = pe.matmul(pB[:, 128 * b:128 * b + 128], dcol[:, 6, b:b + 1].to_broadcast([128, 128]),
                                     w[:, 15, :], start=True, stop=True)
                done(last)

            def fp8_linear(n):
                pe.wait_ge(s_fdve, FDVE * n + 8)
                for b in range(NB):
                    last = pe.transpose(pA[:, 128 * b:128 * b + 128], fq[:, 2, b, :], ident[:])
                last.then_inc(s_fpe, 1)
                pe.wait_ge(s_fact, n + 1)
                for b in range(NB):
                    last = pe.matmul(pB[:, 128 * b:128 * b + 128], f16T[:, b, :], w8[:], start=True, stop=True)
                last.then_inc(s_fpe, 1)

            def body(n):
                attention(slots_of(n, "AB"))
                ffn(n)
                agent(n)
                attention(slots_of(n, "E"))
                fp8_linear(n)

            body(0)
            with pe.Fori(1, NG) as n:
                body(n)

        @block.scalar
        def _(act):
            act.wait_ge(s_const, n_const)
            act.activation(mix[:, 1:2], mix[:, 0:1], ACT.Exp, scale=-1.0).then_inc(s_setup_act, 1)
            act.activation(decay[:], decay[:], ACT.Exp).then_inc(s_setup_act, 1)
            act.activation(mega[:], mega[:], ACT.Exp, scale=float(SEG)).then_inc(s_setup_act, 1)
            act.activation(ident16[:], ident[:], ACT.Copy).then_inc(s_setup_act, 1)

            def front_xT(slot):
                st, b, n, k = slot
                act.wait_ge(s_xT, k + 1)
                reach(act, s_proj, k)
                width = 1 if st == "A" else 2
                act.activation(xcT[:, 0:width, :], pM[:, 0:128 * width].rearrange("p (a c) -> p a c", a=width),
                               ACT.Copy).then_inc(s_xT_ev, 1)

            def front_proj(slot):
                st, b, n, k = slot
                if st == "B":
                    return
                act.wait_ge(s_proj, k + 1)
                reach(act, s_proj_out, k - BIG + 1)
                act.activation(qk32[:, par(slot, BIG)].rearrange("p a c -> p (a c)"), pM[:, 0:256], ACT.Copy)\
                    .then_inc(s_proj_ev, 1)
                act.activation(vaug[:, par(slot, BIG), :, 0:DH], pM[:, 256:384].rearrange("p (h d) -> p h d", h=H),
                               ACT.Copy).then_inc(s_proj_ev, 1)
                if st == "A":
                    act.activation(qT32[:, par(slot, BIG), :], pM[:, 384:448], ACT.Copy).then_inc(s_qT_ev, 1)

            def front_split(slot):
                st, b, n, k = slot
                act.wait_ge(s_splitT, k + 1)
                reach(act, s_score, 4 * k - 4)
                act.activation(splitT[:, par(slot, 2)].rearrange("p r g c -> p (r g c)"), pM[:].bitcast(F16), ACT.Copy)\
                    .then_inc(s_splitT_ev, 1)

            def exp(slot, j):
                st, b, n, k = slot
                act.wait_ge(s_shift, 4 * k + (j + 1))
                t = P[:, par(slot, BIG), j, :, 0:mw(st)]
                act.activation(t, t, ACT.Exp).then_inc(s_exp, 1)

            def mid_PT(slot, j):
                st, b, n, k = slot
                act.wait_ge(s_PT, 4 * k + (j + 1))
                if j == 0:
                    reach(act, s_pv, k - 1)
                act.activation(PT[0:mw(st), par(slot, 2), j, :, :], pT[0:mw(st), :].rearrange("p (g l) -> p g l", g=NQ),
                               ACT.Copy).then_inc(s_PT_ev, 1)

            def back_yT(slot):
                st, b, n, k = slot
                act.wait_ge(s_yT, k + 1)
                act.activation(yT[:], pO[:, 0:128], ACT.Copy).then_inc(s_yT_ev, 1)

            def attention(slots):
                N = len(slots)
                for s in range(N + 3):
                    f = slots[s] if s < N else None
                    e = slots[s - 1] if 0 <= s - 1 < N else None
                    m = slots[s - 2] if 0 <= s - 2 < N else None
                    k = slots[s - 3] if 0 <= s - 3 < N else None
                    if f: front_xT(f)
                    if m: mid_PT(m, 0)
                    if e: exp(e, 0)
                    if f: front_proj(f)
                    if m: mid_PT(m, 1)
                    if e: exp(e, 1)
                    if f: front_split(f)
                    if m: mid_PT(m, 2)
                    if k: back_yT(k)
                    if e: exp(e, 2)
                    if m: mid_PT(m, 3)
                    if e: exp(e, 3)

            def ffn(n):
                act.wait_ge(s_gT, n + 1)
                act.activation(gT32[:].rearrange("p b c -> p (b c)"), pA[:], ACT.Copy).then_inc(s_gT_ev, 1)
                act.activation(gTh[:], pA[:], ACT.Copy).then_inc(s_gT_ev, 1)
                act.wait_ge(s_rt_dve, RTD * n + 3)
                act.activation(rt[:, 2], rt[:, 1], ACT.Exp).then_inc(s_rt_exp, 1)
                for c, (e, q, m) in enumerate(CH):
                    act.wait_ge(s_gate, n * len(CH) + (c + 1))
                    if c >= 2:
                        act.wait_ge(s_h, n * len(CH) + (c - 1))
                    act.activation(G[0:m, c % 2, :], pA[0:m, :], ACT.Gelu).then_inc(s_gelu, 1)

            def agent(n):
                act.wait_ge(s_dpe, 11 * n + 1)
                act.activation(dT[:].rearrange("p b c -> p (b c)"), pA[:], ACT.Copy).then_inc(s_dact, 1)
                act.wait_ge(s_ddve, DDVE * n + 2)
                act.activation(dcol[:, 7, :], dcol[:, 7, :], ACT.Exp).then_inc(s_dact, 1)
                act.wait_ge(s_ddve, DDVE * n + 4)
                act.activation(drow[:, 0, :], pY[0:NB, 0:128], ACT.Exp, bias=dstat[:, 0:1], accum_out=dstat[:, 1:2])\
                    .then_inc(s_dact, 1)
                act.wait_ge(s_ddve, DDVE * n + 10)
                act.activation(drow[:, 2, :], pY[0:NB, 0:128], ACT.Exp, bias=dstat[:, 2:3], accum_out=dstat[:, 3:4])\
                    .then_inc(s_dact, 1)

            def fp8_linear(n):
                act.wait_ge(s_fpe, 2 * n + 1)
                act.activation(f16T[:].rearrange("p b c -> p (b c)"), pA[:], ACT.Copy).then_inc(s_fact, 1)

            def body(n):
                attention(slots_of(n, "AB"))
                ffn(n)
                agent(n)
                attention(slots_of(n, "E"))
                fp8_linear(n)

            body(0)
            with act.Fori(1, NG) as n:
                body(n)

        @block.gpsimd
        def _(pool):
            for t in (ctxB, ctxE):
                pool.memset(t[:], 0.0)
            pool.memset(split[:], 0.0)
            pool.memset(vaug[:], 1.0)
            pool.memset(half[:], -0.5)
            pool.memset(ones[:], 1.0).then_inc(s_setup_pool, 1)
            pool.wait_ge(s_const, n_const)
            pool.tensor_copy(w1h[:], wtmp[:, 0]).then_inc(s_setup_pool, 1)
            pool.tensor_copy(v1h[:], wtmp[:, 1]).then_inc(s_setup_pool, 1)
            pool.wait_ge(s_setup_pool, 3)
            pool.tensor_tensor(w1l[:], wtmp[:, 0], w1h[:], ALU.subtract).then_inc(s_setup_pool, 1)
            pool.tensor_tensor(v1l[:], wtmp[:, 1], v1h[:], ALU.subtract).then_inc(s_setup_pool, 1)

            def carry_pool():
                pool.tensor_tensor(idle[:, 0:1], half[:, 0:1], half[:, 0:1], ALU.add)

            def front_split(slot):
                st, b, n, k = slot
                pool.wait_ge(s_proj_ev, 2 * k + 2)
                reach(pool, s_splitT, k - 1)
                carry_pool()
                qk = qk32[:, par(slot, BIG)].rearrange("p r (h d) -> p r h d", h=H)
                t = split[:, par(slot, 2)]
                pool.tensor_copy(t[:, :, :, 0, :], qk).then_inc(s_hi, 1)
                pool.tensor_copy(t[:, 0, :, 1, :], qk[:, 0])
                pool.tensor_copy(t[:, 1, :, 2, :], qk[:, 1])
                pool.wait_ge(s_hi, k + 1)
                pool.tensor_tensor(t[:, 0, :, 2, :], qk[:, 0], t[:, 0, :, 0, :], ALU.subtract)
                pool.tensor_tensor(t[:, 1, :, 1, :], qk[:, 1], t[:, 1, :, 0, :], ALU.subtract).then_inc(s_split, 1)

            def shift(slot, j):
                st, b, n, k = slot
                pool.wait_ge(s_max, 4 * k + (j + 1))
                t = P[:, par(slot, BIG), j, :, 0:mw(st)]
                pool.tensor_tensor(t, t, nmax[:, par(slot, BIG), j, :].unsqueeze(2).to_broadcast([128, NQ, mw(st)]),
                                   ALU.add).then_inc(s_shift, 1)

            def back_rstd(slot):
                st, b, n, k = slot
                pool.wait_ge(s_ve, k + 1)
                i = par(slot, 2)
                pool.tensor_tensor(rstd[:, i:i + 1], ve[:, i:i + 1], half[:, 0:1], ALU.pow).then_inc(s_rstd, 1)

            def attention(slots):
                N = len(slots)
                for s in range(N + 3):
                    f = slots[s] if s < N else None
                    k = slots[s - 3] if 0 <= s - 3 < N else None
                    if f:
                        front_split(f)
                        shift(f, 0)
                        shift(f, 1)
                    if k: back_rstd(k)
                    if f:
                        shift(f, 2)
                        shift(f, 3)

            def group_rstd(i):
                pool.wait_ge(s_gve, i)
                pool.tensor_tensor(grs[:], gve[:], half[:], ALU.pow).then_inc(s_grs, 1)

            def ffn(n):
                pool.wait_ge(s_gT_ev, 2 * n + 2)
                pool.tensor_tensor(gTl[:], gT32[:].rearrange("p b c -> p (b c)"), gTh[:], ALU.subtract)\
                    .then_inc(s_gTl, 1)
                reach(pool, s_gln, NB * 3 * n)
                pool.tensor_tensor(acc[:], xb[:], bias[:, 4, :].unsqueeze(1).to_broadcast([128, NB, 128]), ALU.add)\
                    .then_inc(s_acc, 1)
                for e in range(NE):
                    pool.wait_ge(s_acc, (NE + 1) * n + (e + 1))
                    pool.wait_ge(s_yw, NE * n + (e + 1))
                    pool.tensor_tensor(acc[:], acc[:], yw[:, e % 2], ALU.add).then_inc(s_acc, 1)
                group_rstd(3 * n + 1)

            def body(n):
                attention(slots_of(n, "AB"))
                ffn(n)
                group_rstd(3 * n + 2)
                attention(slots_of(n, "E"))
                group_rstd(3 * n + 3)

            body(0)
            with pool.Fori(1, NG) as n:
                body(n)

        @block.vector
        def _(dve):
            def carry_dve(c):
                dve.memset(idle[:, c:c + 1], 0.0)

            done_setup = [0]

            def step(ins):
                done_setup[0] += 1
                ins.then_inc(s_setup_dve, 1)
                dve.wait_ge(s_setup_dve, done_setup[0])

            dve.wait_ge(s_const, n_const)
            dve.wait_ge(s_w, 16)
            dve.wait_ge(s_setup_act, 4)
            rs8 = 1.0 / float(np.sqrt(DH))
            for a in (0, 4, 8):
                dve.tensor_scalar(w[:, a, :], w[:, a, :], rs8, None, ALU.mult)
            dve.tensor_scalar(bias[:, 0, :], bias[:, 0, :], rs8, None, ALU.mult)
            step(dve.tensor_scalar(mask0[:], mask0[:], NEG, None, ALU.mult))
            step(dve.tensor_scalar(mix[:, 1:2], mix[:, 1:2], 1.0, None, ALU.add))
            step(dve.reciprocal(mix[:, 2:3], mix[:, 1:2]))
            step(dve.tensor_scalar(mix[:, 3:4], mix[:, 2:3], -1.0, 1.0, ALU.mult, ALU.add))
            step(dve.tensor_scalar(mega[:], mega[:], 0.0, 2.0, ALU.max, ALU.min))
            step(dve.tensor_scalar(mega[:], mega[:], 0.0, None, ALU.mult))
            step(dve.tensor_tensor(decay[:], decay[:], mega[:], ALU.add))
            step(dve.tensor_copy(w8i[:, 0, :], w8raw[:]))
            dve.tensor_scalar(w8i[:, 1, :], w8i[:, 0, :], 3, 15, ALU.logical_shift_right, ALU.bitwise_and)
            dve.tensor_scalar(w8i[:, 2, :], w8i[:, 0, :], 7, None, ALU.bitwise_and)
            step(dve.tensor_scalar(w8i[:, 3, :], w8i[:, 0, :], 7, None, ALU.logical_shift_right))
            dve.tensor_scalar(w8f[:, 0, :], w8i[:, 1, :], 0.0, 8.0, ALU.is_gt, ALU.mult)
            dve.tensor_scalar(w8i[:, 1, :], w8i[:, 1, :], 1.0, 117.0, ALU.max, ALU.add)
            step(dve.tensor_scalar(w8f[:, 1, :], w8i[:, 3, :], -2.0, 1.0, ALU.mult, ALU.add))
            dve.tensor_scalar(w8i[:, 1, :], w8i[:, 1, :], 23, None, ALU.logical_shift_left)
            step(dve.tensor_tensor(w8f[:, 0, :], w8f[:, 0, :], w8i[:, 2, :], ALU.add))
            step(dve.tensor_tensor(w8f[:, 0, :], w8f[:, 0, :], w8f[:, 1, :], ALU.mult))
            dve.tensor_tensor(w8[:], w8f[:, 0, :], w8i[:, 1, :].bitcast(F32), ALU.mult)
            dve.wait_ge(s_setup_pe, 1)
            step(dve.tensor_copy(u_col[:], pY[:, 0:1]))

            def front_proj(slot):
                st, b, n, k = slot
                if st != "B":
                    return
                dve.wait_ge(s_proj, k + 1)
                reach(dve, s_proj_out, k - BIG + 1)
                dve.tensor_tensor(qk32[:, par(slot, BIG)].rearrange("p a c -> p (a c)"), pM[:, 0:256],
                                  bias[:, 0:2, :].rearrange("p a c -> p (a c)"), ALU.add).then_inc(s_proj_ev, 1)
                dve.tensor_tensor(vaug[:, par(slot, BIG), :, 0:DH], pM[:, 256:384].rearrange("p (h d) -> p h d", h=H),
                                  bias[:, 2, :].rearrange("p (h d) -> p h d", h=H), ALU.add).then_inc(s_proj_ev, 1)

            def front_mask(slot, j):
                st, b, n, k = slot
                m = mw(st)
                dve.wait_ge(s_score, 4 * k + (j + 1))
                if j == 0:
                    reach(dve, s_proj_out, k - BIG + 1)
                if st == "E" and j == 0:
                    dve.wait_ge(s_mask1, (n + 1) * 16)
                mask = {"A": causal[:], "B": mask0[:], "E": mask1[:, b, :]}[st]
                dve.tensor_tensor(P[:, par(slot, BIG), j, :, 0:m], pS[j % 2][:].rearrange("p (g c) -> p g c", g=NQ)[:, :, 0:m],
                                  mask.unsqueeze(1).to_broadcast([128, NQ, m]), ALU.add).then_inc(s_masked, 1)

            def front_max(slot, j):
                st, b, n, k = slot
                dve.wait_ge(s_masked, 4 * k + (j + 1))
                dve.tensor_reduce(nmax[:, par(slot, BIG), j, :], P[:, par(slot, BIG), j, :, 0:mw(st)], AX.X, ALU.max,
                                  negate=True).then_inc(s_max, 1)

            def oview():
                return pO[:, 0:H * (DH + 1)].rearrange("p (h d) -> p h d", h=H)

            def mid_y(slot):
                st, b, n, k = slot
                i = par(slot, 2)
                na = n * NB + (b + 1)
                dve.wait_ge(s_pv, k + 1)
                dve.reciprocal(rz[:, i, :], oview()[:, :, DH]).then_inc(s_rz, 1)
                dve.wait_ge(s_rz, k + 1)
                if st == "A":
                    dve.tensor_tensor(carry_w[:, i, :], rz[0:SEG, i, :], decay[:], ALU.mult).then_inc(s_rl, 1)
                    dve.wait_ge(s_rl, na)
                    dve.tensor_scalar(rz[:, i, :], rz[:, i, :], mix[:, 2:3], None, ALU.mult).then_inc(s_rzt, 1)
                    dve.wait_ge(s_rzt, na)
                last = dve.tensor_tensor(yo[:, i, :].rearrange("p (h d) -> p h d", h=H), oview()[:, :, 0:DH],
                                         rz[:, i, :].unsqueeze(2).to_broadcast([128, H, DH]), ALU.mult)
                last.then_inc(s_yo, 1)

            def back_vp(slot):
                st, b, n, k = slot
                if st != "A":
                    return
                dve.wait_ge(s_pcs, n * NB + (b + 1))
                dve.tensor_tensor(vp[:].rearrange("p (h d) -> p h d", h=H), vaug[0:SEG, par(slot, BIG), :, 0:DH],
                                  pO[0:SEG, 0:H].unsqueeze(2).to_broadcast([SEG, H, DH]), ALU.mult).then_inc(s_vp, 1)
                dve.tensor_copy(pcs[:], pO[0:SEG, 0:H]).then_inc(s_vp, 1)

            def back_kvm(slot):
                st, b, n, k = slot
                if st != "A":
                    return
                dve.wait_ge(s_kv, n * NB + (b + 1))
                dve.tensor_scalar(rsum[SEG:128, :], pO[SEG:128, 128:128 + H], EPS, None, ALU.add)\
                    .then_inc(s_kvm, 1)
                dve.tensor_tensor(kvm[:], pO[:, 0:128], block_diag[:], ALU.mult).then_inc(s_kvm, 1)

            def back_ylin(slot):
                st, b, n, k = slot
                if st != "A":
                    return
                na = n * NB + b
                dve.wait_ge(s_kvm, 2 * na + 2)
                dve.reciprocal(rsum[SEG:128, :], rsum[SEG:128, :]).then_inc(s_lin_ev, 1)
                dve.wait_ge(s_lin_ev, 3 * na + 1)
                dve.tensor_scalar(rsum[SEG:128, :], rsum[SEG:128, :], mix[SEG:128, 3:4], None, ALU.mult)\
                    .then_inc(s_lin_ev, 1)
                dve.wait_ge(s_lin_ev, 3 * na + 2)
                dve.wait_ge(s_lin, na + 1)
                dve.tensor_tensor(ylin[SEG:128, :].rearrange("p (h d) -> p h d", h=H),
                                  pO[SEG:128, 0:128].rearrange("p (h d) -> p h d", h=H),
                                  rsum[SEG:128, :].unsqueeze(2).to_broadcast([SEG, H, DH]), ALU.mult)\
                    .then_inc(s_lin_ev, 1)
                dve.wait_ge(s_lin_ev, 3 * na + 3)
                i = par(slot, 2)
                dve.tensor_tensor(yo[SEG:128, i, :], yo[SEG:128, i, :], ylin[SEG:128, :], ALU.add).then_inc(s_y, 1)

            def back_res(slot):
                st, b, n, k = slot
                i = par(slot, 2)
                dve.wait_ge(s_proj_out, k + 1)
                dve.tensor_tensor(res[:, i, :], pO[:, 0:128], x_of[st][:, b, :], ALU.add).then_inc(s_res, 1)
                if st == "B":
                    dve.wait_ge(s_res, k + 1)
                    dve.tensor_tensor(res[:, i, :], res[:, i, :], bias[:, 3, :], ALU.add).then_inc(s_resb, 1)

            def back_stats(slot):
                st, b, n, k = slot
                i = par(slot, 2)
                if st == "B":
                    dve.wait_ge(s_resb, n * NB + (b + 1))
                dve.wait_ge(s_res, k + 1)
                dve.bn_stats(st6[:, i, :], res[:, i, :]).then_inc(s_st, 1)

            def back_aggr(slot):
                st, b, n, k = slot
                i = par(slot, 2)
                dve.wait_ge(s_st, k + 1)
                carry_dve(1)
                dve.bn_aggr(mv[:, i, :], st6[:, i, :]).then_inc(s_mv, 1)
                dve.wait_ge(s_mv, k + 1)
                dve.tensor_scalar(ve[:, i:i + 1], mv[:, i, 1:2], EPS, None, ALU.add).then_inc(s_ve, 1)

            def back_norm(slot):
                st, b, n, k = slot
                i = par(slot, 2)
                dve.wait_ge(s_rstd, k + 1)
                if st == "B":
                    reach(dve, s_acc, (NE + 1) * (n - 1) + 1)
                    reach(dve, s_gT, n)
                dve.tensor_scalar(dst_of[st][:, b, :], res[:, i, :], mv[:, i, 0:1], rstd[:, i:i + 1],
                                  ALU.subtract, ALU.mult).then_inc(s_ln[st], 1)

            def attention(slots):
                N = len(slots)
                for s in range(N + 3):
                    f = slots[s] if s < N else None
                    m = slots[s - 2] if 0 <= s - 2 < N else None
                    k = slots[s - 3] if 0 <= s - 3 < N else None
                    if k: back_vp(k)
                    if f: front_proj(f)
                    if k: back_kvm(k)
                    if k: back_ylin(k)
                    if f:
                        front_mask(f, 0)
                        front_mask(f, 1)
                        front_max(f, 0)
                        front_max(f, 1)
                    if k: back_res(k)
                    if f: front_mask(f, 2)
                    if k: back_stats(k)
                    if f: front_mask(f, 3)
                    if k: back_aggr(k)
                    if f:
                        front_max(f, 2)
                        front_max(f, 3)
                    if m: mid_y(m)
                    if k: back_norm(k)

            def group_norm(i, src, dst):
                for b in range(NB):
                    dve.bn_stats(gst[:, b, :], src[:, b, :]).then_inc(s_gst, 1)
                dve.wait_ge(s_gst, NB * i + NB)
                carry_dve(2)
                for b in range(NB):
                    dve.bn_aggr(gmv[:, b, :], gst[:, b, :]).then_inc(s_gmv, 1)
                dve.wait_ge(s_gmv, NB * (i + 1))
                dve.tensor_scalar(gve[:], gmv[:, :, 1], EPS, None, ALU.add).then_inc(s_gve, 1)
                dve.wait_ge(s_grs, i + 1)
                for b in range(NB):
                    dve.tensor_scalar(dst[:, b, :], src[:, b, :], gmv[:, b, 0:1], grs[:, b:b + 1],
                                      ALU.subtract, ALU.mult).then_inc(s_gln, 1)

            def router(n):
                count = [0]

                def step(ins):
                    count[0] += 1
                    ins.then_inc(s_rt_dve, 1)
                    dve.wait_ge(s_rt_dve, RTD * n + count[0])

                def over(t, a):
                    return t.unsqueeze(a).to_broadcast([128, NB, NE, NE])

                dve.wait_ge(s_rt, n + 1)
                step(dve.tensor_copy(rt[:, 0].rearrange("p b e -> p (b e)"), pY[:, 0:NB * NE]))
                step(dve.tensor_reduce(rts[:, 0, :], rt[:, 0], AX.X, ALU.max))
                step(dve.tensor_tensor(rt[:, 1], rt[:, 0], rts[:, 0, :].unsqueeze(2).to_broadcast([128, NB, NE]),
                                       ALU.subtract))
                dve.wait_ge(s_rt_exp, n + 1)
                step(dve.tensor_reduce(rts[:, 1, :], rt[:, 2], AX.X, ALU.add))
                step(dve.reciprocal(rts[:, 2, :], rts[:, 1, :]))
                step(dve.tensor_tensor(rt[:, 3], rt[:, 2], rts[:, 2, :].unsqueeze(2).to_broadcast([128, NB, NE]),
                                       ALU.mult))
                step(dve.tensor_tensor(rt64[:, 0], over(rt[:, 3], 2), over(rt[:, 3], 3), ALU.is_ge))
                step(dve.tensor_tensor(rt64[:, 1], rt64[:, 0],
                                       lower[:, 0:NE * NE].rearrange("p (a c) -> p a c", a=NE).unsqueeze(1)
                                       .to_broadcast([128, NB, NE, NE]), ALU.mult))
                dve.tensor_reduce(rt[:, 4], rt64[:, 1], AX.X, ALU.add)
                step(dve.tensor_reduce(rt[:, 5], rt64[:, 1].rearrange("p b a c -> p b c a"), AX.X, ALU.add))
                step(dve.tensor_tensor(rt[:, 6], rt[:, 4], rt[:, 5], ALU.subtract))
                step(dve.tensor_tensor(rt[:, 6], rt[:, 6], above(), ALU.add))
                step(dve.scalar_tensor_tensor(out=rt[:, 7], in0=rt[:, 6], scalar=1.5, in1=rt[:, 3],
                                              op0=ALU.is_lt, op1=ALU.mult))

            def above():
                return lower[:, NE * NE:].unsqueeze(1).to_broadcast([128, NB, NE])

            def ffn(n):
                router(n)
                for c, (e, q, m) in enumerate(CH):
                    dve.wait_ge(s_gelu, n * len(CH) + (c + 1))
                    dve.wait_ge(s_val, n * len(CH) + (c + 1))
                    if c >= 2:
                        dve.wait_ge(s_y2, n * len(CH) + (c - 1))
                    dve.tensor_tensor(Hh[0:m, c % 2, :], pB[0:m, :], G[0:m, c % 2, :], ALU.mult).then_inc(s_h, 1)
                    if q == 0 and e >= 1:
                        weigh(n, e - 1)
                weigh(n, NE - 1)
                dve.wait_ge(s_acc, (NE + 1) * (n + 1))
                group_norm(3 * n, acc, xc)

            def weigh(n, e):
                dve.wait_ge(s_y2, n * len(CH) + 3 * (e + 1))
                if e >= 2:
                    dve.wait_ge(s_acc, (NE + 1) * n + e)
                dve.tensor_tensor(yw[:, e % 2], pY[:].rearrange("p (b c) -> p b c", b=NB),
                                  rt[:, 7, :, e].unsqueeze(2).to_broadcast([128, NB, 128]), ALU.mult)\
                    .then_inc(s_yw, 1)

            def agent(n):
                count = [0]

                def step(ins):
                    count[0] += 1
                    ins.then_inc(s_ddve, 1)
                    dve.wait_ge(s_ddve, DDVE * n + count[0])

                def product(i):
                    dve.wait_ge(s_dpe, 11 * n + i)

                def exped(i):
                    dve.wait_ge(s_dact, DACT * n + i)

                product(2)
                step(dve.tensor_scalar(dcol[:, 0, :], pY[:, 0:NB], float(D) ** -0.5, None, ALU.mult))
                step(dve.tensor_tensor(dcol[:, 7, :], dcol[:, 0, :], dcol[:, 0, :], ALU.subtract))
                product(3)
                step(dve.tensor_copy(dcol[:, 1, :], pY[:, 0:NB]))
                product(4)
                step(dve.tensor_reduce(dstat[:, 0:1], pY[0:NB, 0:128], AX.X, ALU.max, negate=True))
                exped(3)
                step(dve.reciprocal(dstat[:, 1:2], dstat[:, 1:2]))
                step(dve.tensor_scalar(drow[:, 1, :], drow[:, 0, :], dstat[:, 1:2], None, ALU.mult))
                product(5)
                step(dve.tensor_copy(dcol[:, 2, :], pY[:, 0:NB]))
                product(6)
                step(dve.tensor_copy(dcol[:, 3, :], pY[:, 0:NB]))
                product(7)
                step(dve.tensor_copy(dcol[:, 4, :], pY[:, 0:NB]))
                product(8)
                step(dve.tensor_reduce(dstat[:, 2:3], pY[0:NB, 0:128], AX.X, ALU.max, negate=True))
                exped(4)
                step(dve.reciprocal(dstat[:, 3:4], dstat[:, 3:4]))
                step(dve.tensor_scalar(drow[:, 3, :], drow[:, 2, :], dstat[:, 3:4], None, ALU.mult))
                product(9)
                step(dve.tensor_copy(dcol[:, 5, :], pY[:, 0:NB]))
                product(10)
                step(dve.tensor_copy(dcol[:, 6, :], pY[:, 0:NB]))
                product(11)
                for b in range(NB):
                    step(dve.tensor_scalar(acc[:, b, :], pB[:, 128 * b:128 * b + 128], dcol[:, 7, b:b + 1], None,
                                           ALU.mult))
                for b in range(NB):
                    step(dve.tensor_tensor(acc[:, b, :], acc[:, b, :], xc[:, b, :], ALU.add))
                group_norm(3 * n + 1, acc, xc)

            def fp8_linear(n):
                count = [0]

                def step(ins):
                    count[0] += 1
                    ins.then_inc(s_fdve, 1)
                    dve.wait_ge(s_fdve, FDVE * n + count[0])

                dve.wait_ge(s_ln["E"], NB * (n + 1))
                step(dve.tensor_reduce(fsc[:, 0, :], xc[:], AX.X, ALU.max, apply_absolute_value=True))
                step(dve.tensor_scalar(fsc[:, 1, :], fsc[:, 0, :], 1e-12, 1.0 / 448.0, ALU.max, ALU.mult))
                dve.tensor_scalar(fsc[:, 3, :], fsc[:, 1, :], wscale[:, 0:1], None, ALU.mult)
                step(dve.reciprocal(fsc[:, 2, :], fsc[:, 1, :]))
                step(dve.tensor_tensor(fq[:, 0], xc[:], fsc[:, 2, :].unsqueeze(2).to_broadcast([128, NB, 128]),
                                       ALU.mult))
                step(dve.tensor_scalar(fq[:, 1].bitcast(I32), fq[:, 0].bitcast(I32), 0x7F800000, None,
                                       ALU.bitwise_and))
                step(dve.tensor_scalar(fq[:, 1], fq[:, 1], 2.0 ** -6, 1.5 * 2.0 ** 20, ALU.max, ALU.mult))
                step(dve.tensor_tensor(fq[:, 0], fq[:, 0], fq[:, 1], ALU.add))
                step(dve.tensor_tensor(fq[:, 2], fq[:, 0], fq[:, 1], ALU.subtract))
                dve.wait_ge(s_fpe, 2 * n + 2)
                step(dve.tensor_tensor(acc[:], pB[:].rearrange("p (b c) -> p b c", b=NB),
                                       fsc[:, 3, :].unsqueeze(2).to_broadcast([128, NB, 128]), ALU.mult))
                step(dve.tensor_tensor(acc[:], acc[:], bias[:, 5, :].unsqueeze(1).to_broadcast([128, NB, 128]),
                                       ALU.add))
                for b in range(NB):
                    step(dve.tensor_tensor(acc[:, b, :], acc[:, b, :], xc[:, b, :], ALU.add))
                reach(dve, s_out, 16 * n)
                group_norm(3 * n + 2, acc, yout)

            def body(n):
                attention(slots_of(n, "AB"))
                ffn(n)
                agent(n)
                attention(slots_of(n, "E"))
                fp8_linear(n)

            dve.wait_ge(s_setup_pool, 5)
            body(0)
            with dve.Fori(1, NG) as n:
                body(n)


def kernel(**inputs):
    import concourse.bacc as bacc
    from concourse.bass_utils import run_bass_kernel_spmd

    a = {k: np.ascontiguousarray(v) for k, v in inputs.items()}
    flat = lambda t: t.reshape(128, 128)
    l1 = a["L1_attn_w_qkv"]
    mats = [a["L0_attn_Wq"].T, a["L0_attn_Wk"].T, a["L0_attn_Wv"].T, a["L0_attn_Wc"].T,
            a["L0_xattn_Wq"], a["L0_xattn_Wk"], a["L0_xattn_Wv"], a["L0_xattn_Wo"],
            flat(a["L1_xattn_wq"]), flat(a["L1_xattn_wk"]), flat(a["L1_xattn_wv"]), flat(a["L1_xattn_wo"]),
            l1[0:128], l1[128:256].T, l1[256:384], l1[256:384].T]
    arrays = {
        "x": a["x"], "ctx": a["ctx_1024"], "mask0": a["mask_1x1xSxS2_fk1"], "mask1": a["mask_Bx1xSxS2_ff0"],
        "w": np.stack(mats),
        "bias": np.concatenate([a["L0_xattn_bq"], a["L0_xattn_bk"], a["L0_xattn_bv"], a["L0_xattn_bo"],
                                a["L0_ffn_bias"], a["L1_ffn_bias"]]),
        "terrace": a["L0_attn_terrace_mix"].reshape(SEG, 1),
        "decay": a["L0_attn_index_decays"].T, "mega": a["L0_attn_mega_decays"],
        "rw": a["L0_ffn_router_w"], "w1": a["L0_ffn_w1"], "v1": a["L0_ffn_v1"], "w2": a["L0_ffn_w2"],
        "conv": a["L1_attn_w_conv1"].reshape(128, 1),
        "w8": a["L1_ffn_weight"].view(np.uint8).T, "wscale": a["L1_ffn_weight_scale"].reshape(1),
        "ident": np.eye(128, dtype=np.float32),
        "causal": np.where(np.tril(np.ones((128, 128), bool)), 0.0, -1e30).astype(np.float32),
        "block": (np.kron(np.eye(H), np.ones((DH, DH))) * np.sqrt(DH)).astype(np.float32),
        "lower": np.tile(np.concatenate([np.tril(np.ones((NE, NE)), -1).ravel(), NE - 1.0 - np.arange(NE)]), (128, 1))
        .astype(np.float32),
    }
    nc = bacc.Bacc("TRN2", target_bir_lowering=False, num_devices=1)
    feeds, args = {}, []
    for name, t in arrays.items():
        t = np.ascontiguousarray(t)
        feeds[f"in_{name}"] = t
        args.append(nc.dram_tensor(f"in_{name}", t.shape, mybir.dt.from_np(t.dtype), kind="ExternalInput").ap())
    args.append(nc.dram_tensor("out_0", (NSEQ, S, D), F32, kind="ExternalOutput").ap())
    decoder(nc, *args)
    r = run_bass_kernel_spmd(nc, [feeds], core_ids=[0])
    return r.results[0]["out_0"]
```

```python
from contextlib import ExitStack

import numpy as np
import concourse.bass as bass
from concourse import mybir

ALU = mybir.AluOpType
ACT = mybir.ActivationFunctionType
AX = mybir.AxisListType
F32 = mybir.dt.float32
F16 = mybir.dt.float16
I32 = mybir.dt.int32
U8 = mybir.dt.uint8

NSEQ, S, D, S2 = 32, 128, 128, 120
H, DH, SEG = 16, 8, 64
NB = 4
NG = NSEQ // NB
NJ, NQ = 4, 4
TERM = 32
NE, FF = 8, 352
CH = [(e, q, min(128, FF - 128 * q)) for e in range(NE) for q in range(3)]
POSITIONS = [("A", 0), ("A", 1), ("A", 2), ("A", 3), ("E", 0), ("E", 1), ("B", 0), ("E", 2), ("B", 1), ("E", 3),
             ("B", 2), ("B", 3)]
STEPS = len(POSITIONS)
E_LATE = 2
LAST = NG + E_LATE
TAIL = 6
CHUNKS_AT = {}
for _c, _at in enumerate([(5, p) for p in (1, 2, 3)] +
                         [(s, p) for s in range(6, 12) for p in ((0, 1, 2, 3) if s % 2 == 0 else (1, 2, 3))]):
    CHUNKS_AT[_at] = _c
assert len(CHUNKS_AT) == len(CH)
AGENT_PE = {(0, 2): (1,), (0, 3): (2,), (1, 0): (3,), (1, 1): (4,), (1, 3): (5,), (2, 0): (6,), (2, 1): (7,),
            (2, 2): (8,), (3, 0): (9,), (3, 1): (10,), (3, 2): (11,)}
AGENT_DVE = {(0, 3): (2,), (1, 0): (3,), (1, 1): (4,), (1, 2): ("softmax c",), (1, 3): (5,), (2, 0): (6,),
             (2, 1): (7,), (2, 2): (8,), (2, 3): ("softmax n",), (3, 0): (9,), (3, 1): (10,), (3, 2): (11,)}
NEG = -1000000000.0
EPS = 1e-5
DEEP = 6
PBUF = 3
WQ, WK, WV, WO = range(4)


def reach(eng, sem, value):
    if isinstance(value, int) and value <= 0:
        return
    eng.wait_ge(sem, value)


def turn_of(i):
    if not isinstance(i, int):
        return True, True, STEPS * i - 2 * NB, 4
    ab, e = 0 <= i < NG, E_LATE <= i < NG + E_LATE
    before = 2 * NB * min(i, NG) + NB * max(0, i - E_LATE)
    return ab, e, before, before % STEPS


def slot_at(i, p):
    if i_has_no_step(i, p):
        return None
    if p < 0:
        return slot_at(i - 1, p + STEPS)
    ab, e, before, mod = turn_of(i)
    here = {"A": ab, "B": ab, "E": e}
    st, b = POSITIONS[p]
    if not here[st]:
        return None
    rank = sum(here[s] for s, _ in POSITIONS[:p])
    return st, b, (i - E_LATE if st == "E" else i), before + rank, (mod + rank) % STEPS


def slot_before(i, p, count):
    while count:
        p -= 1
        if i_has_no_step(i, p):
            return None
        count -= slot_at(i, p) is not None
    return slot_at(i, p)


def i_has_no_step(i, p):
    return isinstance(i, int) and STEPS * i + p < 0


def others_of(i):
    if not isinstance(i, int):
        return i - 1, i - 2, i - 3
    return [i - late if 0 <= i - late < NG else None for late in (1, 2, 3)]


def program(eng, step):
    for i in range(3):
        for p in range(STEPS):
            step(i, p)
    with eng.Fori(3, NG) as i:
        for p in range(STEPS):
            step(i, p)
    for i in range(NG, LAST + 1):
        for p in range(STEPS if i < LAST else TAIL):
            step(i, p)


def decoder(nc, x_d, ctx_d, mask0_d, mask1_d, w_d, bias_d, terrace_d, decay_d, mega_d, rw_d, w1_d, v1_d,
            w2_d, conv_d, w8_d, wscale_d, ident_d, causal_d, block_d, lower_d, out_d):
    with ExitStack() as ctx:
        def sb(name, shape, dt=F32):
            return ctx.enter_context(nc.sbuf_tensor(name, shape, dt))

        def ps(name):
            return ctx.enter_context(nc.psum_tensor(name, [128, 512], F32))

        def sem(name):
            return ctx.enter_context(nc.semaphore(name))

        pS = [ps("pS0"), ps("pS1")]
        pT = ps("pT")
        pM = ps("pM")
        pO = ps("pO")
        pA, pB, pY = ps("pA"), ps("pB"), ps("pY")

        ident = sb("ident", [128, 128])
        ident16 = sb("ident16", [128, 128], F16)
        causal = sb("causal", [128, 128])
        block_diag = sb("block_diag", [128, 128])
        lower = sb("lower", [128, NE * NE + NE])
        ones = sb("ones", [128, 128])
        w = sb("w", [128, 16, 128])
        bias = sb("bias", [128, 6, 128])
        mask0 = sb("mask0", [128, S2])
        mix = sb("mix", [128, 4])
        decay = sb("decay", [SEG, H])
        mega = sb("mega", [SEG, H])
        rw = sb("rw", [128, NE])
        w1h, w1l = sb("w1h", [128, NE, FF], F16), sb("w1l", [128, NE, FF], F16)
        v1h, v1l = sb("v1h", [128, NE, FF], F16), sb("v1l", [128, NE, FF], F16)
        w2 = sb("w2", [128, NE, 3, 128])
        conv = sb("conv", [128, 1])
        u_col = sb("u_col", [128, 1])
        w8raw = sb("w8raw", [128, 128], U8)
        w8i = sb("w8i", [128, 4, 128], I32)
        w8f = sb("w8f", [128, 3, 128])
        w8 = sb("w8", [128, 128], F16)
        wscale = sb("wscale", [128, 1])
        half = sb("half", [128, 4])

        idle = sb("idle", [128, 6])
        idle_pool = sb("idle_pool", [128, 1])

        x0 = sb("x0", [128, NB, 128])
        xa = sb("xa", [128, NB, 128])
        xb = sb("xb", [128, NB, 128])
        xc = sb("xc", [128, NB, 128])
        xd = sb("xd", [128, NB, 128])
        xe = sb("xe", [128, NB, 128])
        yout = sb("yout", [128, NB, 128])
        ctxB = sb("ctxB", [128, NB, 128])
        ctxE = sb("ctxE", [128, NB, 128])
        mask1 = sb("mask1", [128, NB, S2])

        xcT = sb("xcT", [128, 2, 128])
        qk32 = sb("qk32", [128, DEEP, 2, 128])
        qT32 = sb("qT32", [128, DEEP, SEG])
        v32 = sb("v32", [128, DEEP, 128])
        vh = sb("vh", [128, DEEP, H, DH + 1], F16)
        vl = sb("vl", [128, DEEP, H, DH + 1], F16)
        split = sb("split", [128, 2, 2, H, 4, DH], F16)
        splitT = sb("splitT", [128, 2, 2, NQ, 128], F16)
        P = sb("P", [128, PBUF, NJ, NQ, 128])
        smax = sb("smax", [128, PBUF, NJ, NQ])
        PTh = sb("PTh", [128, 2, NJ, NQ, 128], F16)
        PTl = sb("PTl", [128, 2, NJ, NQ, 128], F16)
        pch = sb("pch", [SEG, 2, H + 1, SEG], F16)
        pcl = sb("pcl", [SEG, 2, H + 1, SEG], F16)
        rz = sb("rz", [128, 2, H])
        carry_w = sb("carry_w", [SEG, H])
        carry_h = sb("carry_h", [SEG, H], F16)
        carry_l = sb("carry_l", [SEG, H], F16)
        yo = sb("yo", [128, 2, 128])
        pcs = sb("pcs", [SEG, H])
        vp = sb("vp", [SEG, 128])
        kvm = sb("kvm", [128, 128])
        rsum = sb("rsum", [128, H])
        ylin = sb("ylin", [128, 128])
        yT = sb("yT", [128, 128])
        res = sb("res", [128, 2, 128])
        st6 = sb("st6", [128, 2, 6])
        mv = sb("mv", [128, 2, 2])
        ve = sb("ve", [128, 2])
        rstd = sb("rstd", [128, 2])

        gT32 = sb("gT32", [128, NB, 128])
        gTh, gTl = sb("gTh", [128, NB * 128], F16), sb("gTl", [128, NB * 128], F16)
        rt = sb("rt", [128, 8, NB, NE])
        rt64 = sb("rt64", [128, 2, NB, NE, NE])
        rts = sb("rts", [128, 4, NB])
        ffn_buf = sb("ffn_buf", [128, 3, 2, 512])
        G, Hh = ffn_buf[:, 0], ffn_buf[:, 1]
        yw = ffn_buf[:, 2].rearrange("p a (b c) -> p a b c", b=NB)
        wtmp = ffn_buf[:].rearrange("p a b c -> p (a b c)")[:, 0:NE * FF].rearrange("p (e f) -> p e f", e=NE)
        acc = sb("acc", [128, NB, 128])
        facc = sb("facc", [128, NB, 128])
        gst = {s: sb(f"gst{s}", [128, NB, 6]) for s in "CDF"}
        gmv = {s: sb(f"gmv{s}", [128, NB, 2]) for s in "CDF"}
        gve = {s: sb(f"gve{s}", [128, NB]) for s in "CDF"}
        grs = {s: sb(f"grs{s}", [128, NB]) for s in "CDF"}
        dT = sb("dT", [128, NB, 128])
        dcol = sb("dcol", [128, 8, NB])
        drow = sb("drow", [NB, 4, 128])
        dstat = sb("dstat", [NB, 4])
        fq = sb("fq", [128, 3, NB, 128])
        fsc = sb("fsc", [128, 4, NB])
        f16T = sb("f16T", [128, NB, 128], F16)

        s_const = sem("s_const")
        s_wtmp, s_ffn_w, s_ffn_split = sem("s_wtmp"), sem("s_ffn_w"), sem("s_ffn_split")
        s_w = sem("s_w")
        s_setup_dve, s_setup_act, s_setup_pe, s_setup_pool = (sem(f"s_setup_{n}") for n in ("dve", "act", "pe", "pool"))
        s_x, s_ctxB, s_ctxE, s_mask1, s_out = sem("s_x"), sem("s_ctxB"), sem("s_ctxE"), sem("s_mask1"), sem("s_out")
        s_xT, s_xT_ev = sem("s_xT"), sem("s_xT_ev")
        s_proj, s_proj_ev, s_qT_ev = sem("s_proj"), sem("s_proj_ev"), sem("s_qT_ev")
        s_hi, s_split, s_vhi, s_vsplit = sem("s_hi"), sem("s_split"), sem("s_vhi"), sem("s_vsplit")
        s_splitT, s_splitT_ev = sem("s_splitT"), sem("s_splitT_ev")
        s_score, s_max, s_shift, s_exp = (sem(n) for n in ("s_score", "s_max", "s_shift", "s_exp"))
        s_PT, s_PTh, s_PTl, s_pv = sem("s_PT"), sem("s_PTh"), sem("s_PTl"), sem("s_pv")
        s_pch, s_pcl = sem("s_pch"), sem("s_pcl")
        s_rz, s_rzt, s_yo = sem("s_rz"), sem("s_rzt"), sem("s_yo")
        s_rl, s_rlh, s_rll, s_pcs, s_vp, s_kv, s_kvm, s_lin, s_lin_ev = (sem(n) for n in (
            "s_rl", "s_rlh", "s_rll", "s_pcs", "s_vp", "s_kv", "s_kvm", "s_lin", "s_lin_ev"))
        s_y = sem("s_y")
        s_yT, s_yT_ev, s_proj_out = sem("s_yT"), sem("s_yT_ev"), sem("s_proj_out")
        s_res, s_resb, s_st, s_mv, s_ve, s_rstd = (sem(n) for n in ("s_res", "s_resb", "s_st", "s_mv", "s_ve", "s_rstd"))
        s_ln = {"A": sem("s_lnA"), "B": sem("s_lnB"), "E": sem("s_lnE")}
        s_gT, s_gT_ev, s_gTl = sem("s_gT"), sem("s_gT_ev"), sem("s_gTl")
        s_rt, s_rt_dve, s_rt_exp = sem("s_rt"), sem("s_rt_dve"), sem("s_rt_exp")
        s_gate, s_val, s_gelu, s_h, s_y2, s_yw, s_acc = (sem(n) for n in (
            "s_gate", "s_val", "s_gelu", "s_h", "s_y2", "s_yw", "s_acc"))
        s_gst, s_gmv, s_gve, s_grs, s_gln = ({s: sem(f"s_{n}{s}") for s in "CDF"}
                                             for n in ("gst", "gmv", "gve", "grs", "gln"))
        s_dpe, s_ddve, s_dact = sem("s_dpe"), sem("s_ddve"), sem("s_dact")
        s_fpe, s_fdve, s_fact = sem("s_fpe"), sem("s_fdve"), sem("s_fact")

        block = ctx.enter_context(nc.Block())

        def mw(st):
            return S if st == "A" else S2

        wbase = {"A": 0, "B": 4, "E": 8}
        x_of = {"A": x0, "B": xa, "E": xd}
        dst_of = {"A": xa, "B": xb, "E": xe}

        RTD = 12
        DPE, DDVE, DACT = 11, 18, 4
        FDVE = 13

        @block.sync
        def _(sp):
            def load_x(n):
                reach(sp, s_ln["A"], NB * n)
                sp.dma_start(x0[:], x_d[bass.ds(n * NB, NB)].rearrange("b t d -> t b d")).then_inc(s_x, 16)

            def load_ctxB(n):
                reach(sp, s_ln["B"], NB * n)
                sp.dma_start(ctxB[0:S2], ctx_d[bass.ds(n * NB, NB)].rearrange("b t d -> t b d")).then_inc(s_ctxB, 16)

            def load_E(n):
                reach(sp, s_ln["E"], NB * n)
                sp.dma_start(ctxE[0:S2], ctx_d[bass.ds(n * NB, NB)].rearrange("b t d -> t b d")).then_inc(s_ctxE, 16)
                sp.dma_start(mask1[:], mask1_d[bass.ds(n * NB, NB)].rearrange("b o t m -> t (b o) m")).then_inc(s_mask1, 16)

            def store(n):
                sp.wait_ge(s_gln["F"], NB * n + NB)
                sp.dma_start(out_d[bass.ds(n * NB, NB)].rearrange("b t d -> t b d"), yout[:]).then_inc(s_out, 16)

            sp.dma_start(w[:, 0:4, :], w_d[0:4].rearrange("m p c -> p m c")).then_inc(s_w, 16)
            load_x(0)
            for dst, src in (
                (ident[:], ident_d), (causal[:], causal_d), (mix[0:SEG, 0:1], terrace_d), (mix[SEG:128, 0:1], terrace_d),
                (decay[:], decay_d), (mega[:], mega_d.partition_broadcast(SEG)), (mask0[:], mask0_d[0, 0]),
                (bias[:].rearrange("p m c -> p (m c)"), bias_d.partition_broadcast(128)),
            ):
                sp.dma_start(dst, src).then_inc(s_const, 16)
            sp.dma_start(wtmp, w1_d.rearrange("e d f -> d e f")).then_inc(s_wtmp, 16)
            for dst, src in (
                (w2[:, :, 0, :], w2_d[:, 0:128, :].rearrange("e p d -> p e d")),
                (w2[:, :, 1, :], w2_d[:, 128:256, :].rearrange("e p d -> p e d")),
                (w2[0:96, :, 2, :], w2_d[:, 256:352, :].rearrange("e p d -> p e d")),
            ):
                sp.dma_start(dst, src).then_inc(s_ffn_w, 16)
            sp.wait_ge(s_setup_pool, 1)
            load_ctxB(0)
            load_x(1)
            sp.wait_ge(s_ffn_split, 4)
            sp.dma_start(wtmp, v1_d.rearrange("e d f -> d e f")).then_inc(s_wtmp, 16)
            for i in range(1, 3):
                if i == E_LATE:
                    load_E(0)
                load_ctxB(i)
                load_x(i + 1)
            with sp.Fori(3, NG - 1) as i:
                load_E(i - E_LATE)
                load_ctxB(i)
                store(i - 3)
                load_x(i + 1)
            load_E(NG - 3)
            load_ctxB(NG - 1)
            store(NG - 4)
            for i in range(NG, LAST + 1):
                if i < LAST:
                    load_E(i - E_LATE)
                store(i - 3)
            sp.wait_ge(s_out, 16 * NG)

        n_const = 16 * 14

        @block.tensor
        def _(pe):
            pe.wait_ge(s_const, n_const)
            pe.wait_ge(s_w, 32)
            pe.matmul(pY[:, 0:1], w[:, 12, :], conv[:], start=True, stop=True).then_inc(s_setup_pe, 1)
            pe.wait_ge(s_setup_dve, 13)
            pe.wait_ge(s_setup_pool, 1)

            m16 = pM[:].bitcast(F16)

            def front_xT(slot):
                st, b, n, k, u = slot
                if st == "A":
                    pe.wait_ge(s_x, (n + 1) * 16)
                elif st == "B":
                    pe.wait_ge(s_ln["A"], n * NB + (b + 1))
                    pe.wait_ge(s_ctxB, (n + 1) * 16)
                else:
                    pe.wait_ge(s_gln["D"], n * NB + (b + 1))
                    pe.wait_ge(s_ctxE, (n + 1) * 16)
                reach(pe, s_splitT_ev, k)
                last = pe.transpose(pM[:, 0:128], x_of[st][:, b, :], ident[:])
                if st != "A":
                    last = pe.transpose(pM[:, 128:256], (ctxB if st == "B" else ctxE)[:, b, :], ident[:])
                last.then_inc(s_xT, 1)

            def front_proj(slot):
                st, b, n, k, u = slot
                pe.wait_ge(s_xT_ev, k + 1)
                base = wbase[st]
                wr = w[:].rearrange("p m c -> p (m c)")
                if st == "A":
                    pe.matmul(pM[:, 0:384], xcT[:, 0, :], wr[:, 0:384], start=True, stop=True)
                    last = pe.matmul(pM[:, 384:448], w[:, base + WQ, :], xcT[:, 0, SEG:128], start=True, stop=True)
                else:
                    pe.matmul(pM[:, 0:128], xcT[:, 0, :], w[:, base + WQ, :], start=True, stop=True)
                    last = pe.matmul(pM[:, 128:384], xcT[:, 1, :], wr[:, (base + WK) * 128:(base + WO) * 128],
                                     start=True, stop=True)
                last.then_inc(s_proj, 1)

            def scores_split(slot):
                st, b, n, k, u = slot
                pe.wait_ge(s_split, k + 1)
                pe.wait_ge(s_proj_ev, 2 * k + 2)
                if st == "A":
                    pe.wait_ge(s_qT_ev, n * NB + (b + 1))
                for r in range(2):
                    for g in range(NQ):
                        c = (r * NQ + g) * 128
                        last = pe.transpose(m16[:, c:c + 128],
                                            split[:, u % 2, r, NQ * g:NQ * g + NQ].rearrange("p j t d -> p (j t d)"),
                                            ident16[:])
                last.then_inc(s_splitT, 1)

            def scores(slot, j):
                st, b, n, k, u = slot
                if j == 0:
                    pe.wait_ge(s_splitT_ev, k + 1)
                reach(pe, s_max, 4 * k + (j - 1))
                r0 = TERM * j
                for g in range(NQ):
                    last = pe.matmul(pS[j % 2][:, 128 * g:128 * g + mw(st)], splitT[r0:r0 + 24, u % 2, 0, g, :],
                                     splitT[r0:r0 + 24, u % 2, 1, g, 0:mw(st)], start=True, stop=True)
                last.then_inc(s_score, 1)

            def probs_T(slot, j):
                st, b, n, k, u = slot
                pe.wait_ge(s_exp, 4 * k + (j + 1))
                reach(pe, s_PTl, 4 * k + j)
                for g in range(NQ):
                    last = pe.transpose(pT[0:mw(st), 128 * g:128 * g + 128], P[:, u % PBUF, j, g, 0:mw(st)], ident[:])
                last.then_inc(s_PT, 1)

            def values(slot):
                st, b, n, k, u = slot
                pe.wait_ge(s_PTl, 4 * k + 4)
                pe.wait_ge(s_vsplit, k + 1)
                reach(pe, s_res, k)
                for h in range(H):
                    o = pO[:, (DH + 1) * h:(DH + 1) * (h + 1)]
                    hi, lo = (t[0:mw(st), h % NJ, h // NJ, :] for t in (PTh[:, u % 2], PTl[:, u % 2]))
                    pe.matmul(o, hi, vh[0:mw(st), u % DEEP, h, :], start=True, stop=False)
                    pe.matmul(o, hi, vl[0:mw(st), u % DEEP, h, :], start=False, stop=False)
                    last = pe.matmul(o, lo, vh[0:mw(st), u % DEEP, h, :], start=False, stop=True)
                last.then_inc(s_pv, 1)

            def back_pcs(slot):
                st, b, n, k, u = slot
                if st != "A":
                    return
                pe.wait_ge(s_rll, n * NB + (b + 1))
                pe.wait_ge(s_pcl, n * NB + (b + 1))
                pe.wait_ge(s_yo, k + 1)
                for h in range(H):
                    x = NQ * (h % NJ) + h // NJ
                    hi, lo = (t[:, b % 2, x:x + 2, :].rearrange("p x c -> p (x c)") for t in (pch, pcl))
                    pe.matmul(pO[:, h:h + 1], hi, carry_h[:, h:h + 1], start=True, stop=False)
                    pe.matmul(pO[:, h:h + 1], hi, carry_l[:, h:h + 1], start=False, stop=False)
                    last = pe.matmul(pO[:, h:h + 1], lo, carry_h[:, h:h + 1], start=False, stop=True)
                last.then_inc(s_pcs, 1)

            def back_kv(slot):
                st, b, n, k, u = slot
                if st != "A":
                    return
                pe.wait_ge(s_vp, 2 * (n * NB + (b + 1)))
                pe.matmul(pO[:, 0:128], qk32[0:SEG, u % DEEP, 1, :], vp[:], start=True, stop=True)
                pe.matmul(pO[SEG:128, 128:128 + H], ones[0:SEG, 0:SEG], pcs[:], start=True, stop=True).then_inc(s_kv, 1)

            def back_lin(slot):
                st, b, n, k, u = slot
                if st != "A":
                    return
                pe.wait_ge(s_kvm, 2 * (n * NB + (b + 1)))
                pe.matmul(pO[SEG:128, 0:128], qT32[:, u % DEEP, :], kvm[:], start=True, stop=True).then_inc(s_lin, 1)

            def back_yT(slot):
                st, b, n, k, u = slot
                pe.wait_ge(s_yo, k + 1)
                if st == "A":
                    pe.wait_ge(s_y, n * NB + (b + 1))
                pe.transpose(pO[:, 0:128], yo[:, u % 2, :], ident[:]).then_inc(s_yT, 1)

            def back_out(slot):
                st, b, n, k, u = slot
                pe.wait_ge(s_yT_ev, k + 1)
                pe.matmul(pO[:, 0:128], yT[:], w[:, wbase[st] + WO, :], start=True, stop=True).then_inc(s_proj_out, 1)

            def ffn_xT(n):
                pe.wait_ge(s_ln["B"], NB * (n + 1))
                for b in range(NB):
                    last = pe.transpose(pA[:, 128 * b:128 * b + 128], xb[:, b, :], ident[:])
                last.then_inc(s_gT, 1)

            def ffn_router(n):
                pe.wait_ge(s_gT_ev, 2 * n + 1)
                if isinstance(n, int) and n == 0:
                    pe.wait_ge(s_ffn_w, 16 * 3)
                    pe.wait_ge(s_ffn_split, 8)
                for b in range(NB):
                    last = pe.matmul(pY[:, NE * b:NE * b + NE], gT32[:, b, :], rw[:], start=True, stop=True)
                last.then_inc(s_rt, 1)

            def ffn_out(n, c):
                e, q, m = CH[c]
                pe.wait_ge(s_h, n * len(CH) + (c + 1))
                if q == 0:
                    if e == 0:
                        pe.wait_ge(s_rt_dve, RTD * n + 1)
                    else:
                        pe.wait_ge(s_yw, NE * n + e)
                for b in range(NB):
                    last = pe.matmul(pY[:, 128 * b:128 * b + 128], Hh[0:m, c % 2, 128 * b:128 * b + 128],
                                     w2[0:m, e, q, :], start=(q == 0 and b == 0), stop=(q == 2),
                                     skip_group_check=True)
                last.then_inc(s_y2, 1)

            def ffn_chunk(n, c):
                e, q, m = CH[c]
                for bank, hi, lo, done, free in ((pA, w1h, w1l, s_gate, s_gelu), (pB, v1h, v1l, s_val, s_h)):
                    if c == 0:
                        pe.wait_ge(s_gT_ev, 2 * n + 2)
                        pe.wait_ge(s_gTl, n + 1)
                        if bank is pB:
                            reach(pe, s_ddve, DDVE * n)
                            reach(pe, s_fdve, FDVE * (n - 2) + 12)
                    else:
                        pe.wait_ge(free, n * len(CH) + c)
                    fs = slice(128 * q, 128 * q + m)
                    pe.matmul(bank[0:m, :], hi[:, e, fs], gTh[:], start=True, stop=False)
                    pe.matmul(bank[0:m, :], hi[:, e, fs], gTl[:], start=False, stop=False)
                    pe.matmul(bank[0:m, :], lo[:, e, fs], gTh[:], start=False, stop=True).then_inc(done, 1)
                if c >= 1:
                    ffn_out(n, c - 1)

            def agent(n, part):
                def each(out, lhs, rhs):
                    for b in range(NB):
                        last = pe.matmul(out(b), lhs(b), rhs(b), start=True, stop=True)
                    last.then_inc(s_dpe, 1)

                needs = {2: None, 3: 1, 4: 3, 5: 6, 6: 7, 7: 8, 8: 9, 9: 12, 10: 13, 11: 14}
                col = lambda b: pY[:, b:b + 1]
                if part == 1:
                    pe.wait_ge(s_gln["C"], NB * (n + 1))
                    for b in range(NB):
                        last = pe.transpose(pA[:, 128 * b:128 * b + 128], xc[:, b, :], ident[:])
                    last.then_inc(s_dpe, 1)
                    return
                if part == 2:
                    pe.wait_ge(s_dact, DACT * n + 1)
                else:
                    pe.wait_ge(s_ddve, DDVE * n + needs[part])
                if part == 2:
                    each(col, lambda b: dT[:, b, :], lambda b: u_col[:])
                elif part == 3:
                    each(col, lambda b: xc[:, b, :], lambda b: dcol[:, 0, b:b + 1])
                elif part == 4:
                    pe.matmul(pY[0:NB, 0:128], dcol[:, 1, :], w[:, 13, :], start=True, stop=True).then_inc(s_dpe, 1)
                elif part == 5:
                    pe.matmul(pY[:, 0:NB], drow[:, 1, :], ident[0:NB, 0:NB], start=True, stop=True).then_inc(s_dpe, 1)
                elif part == 6:
                    pe.matmul(pY[:, 0:NB], w[:, 14, :], dcol[:, 2, :], start=True, stop=True).then_inc(s_dpe, 1)
                elif part == 7:
                    each(col, lambda b: dT[:, b, :], lambda b: dcol[:, 3, b:b + 1])
                elif part == 8:
                    pe.transpose(pY[0:NB, 0:128], dcol[:, 4, :], ident[:]).then_inc(s_dpe, 1)
                elif part == 9:
                    pe.matmul(pY[:, 0:NB], drow[:, 3, :], ident[0:NB, 0:NB], start=True, stop=True).then_inc(s_dpe, 1)
                elif part == 10:
                    each(col, lambda b: xc[:, b, :], lambda b: dcol[:, 5, b:b + 1])
                elif part == 11:
                    each(lambda b: pB[:, 128 * b:128 * b + 128],
                         lambda b: dcol[:, 6, b:b + 1].to_broadcast([128, 128]), lambda b: w[:, 15, :])

            def fp8_xT(n):
                pe.wait_ge(s_fdve, FDVE * n + 8)
                for b in range(NB):
                    last = pe.transpose(pA[:, 128 * b:128 * b + 128], fq[:, 2, b, :], ident[:])
                last.then_inc(s_fpe, 1)

            def fp8_product(n, after_agent):
                pe.wait_ge(s_fact, n + 1)
                if after_agent:
                    pe.wait_ge(s_ddve, DDVE * (n + 2))
                for b in range(NB):
                    last = pe.matmul(pB[:, 128 * b:128 * b + 128], f16T[:, b, :], w8[:], start=True, stop=True)
                last.then_inc(s_fpe, 1)

            def between(i, p, place):
                nC, nD, nF = others_of(i)
                at = (p, place)
                if nD is not None:
                    if at == (0, 0):
                        ffn_out(nD, len(CH) - 1)
                    if at in AGENT_PE:
                        for part in AGENT_PE[at]:
                            agent(nD, part)
                if nF is not None:
                    if at == (4, 0):
                        fp8_xT(nF)
                    if at == (4, 1):
                        fp8_product(nF, nD is not None)
                if nC is not None:
                    if at == (4, 3):
                        ffn_xT(nC)
                    if at == (5, 0):
                        ffn_router(nC)
                    if at in CHUNKS_AT:
                        ffn_chunk(nC, CHUNKS_AT[at])

            def step(i, p):
                f, g, v, b = (slot_at(i, p - lag) for lag in (0, 1, 3, 4))
                if g: scores_split(g)
                if v: probs_T(v, 0)
                if b: values(b)
                if f: front_xT(f)
                between(i, p, 0)
                if g:
                    scores(g, 0)
                    scores(g, 1)
                if b: back_pcs(b)
                if v: probs_T(v, 1)
                between(i, p, 1)
                if b: back_kv(b)
                if f: front_proj(f)
                if v: probs_T(v, 2)
                if b: back_lin(b)
                if g: scores(g, 2)
                between(i, p, 2)
                if b: back_yT(b)
                if g: scores(g, 3)
                if v: probs_T(v, 3)
                if b: back_out(b)
                between(i, p, 3)

            program(pe, step)

        @block.scalar
        def _(act):
            for dst, src in (
                (w[:, 4:16, :], w_d[4:16].rearrange("m p c -> p m c")), (conv[:], conv_d),
                (block_diag[:], block_d), (lower[:], lower_d), (rw[:], rw_d),
                (w8raw[:], w8_d), (wscale[:], wscale_d.partition_broadcast(128)),
            ):
                act.dma_start(dst, src).then_inc(s_w if dst.shape == w[:, 4:16, :].shape else s_const, 16)
            act.wait_ge(s_const, n_const)
            act.activation(mix[:, 1:2], mix[:, 0:1], ACT.Exp, scale=-1.0).then_inc(s_setup_act, 1)
            act.activation(decay[:], decay[:], ACT.Exp).then_inc(s_setup_act, 1)
            act.activation(mega[:], mega[:], ACT.Exp, scale=float(SEG)).then_inc(s_setup_act, 1)
            act.activation(ident16[:], ident[:], ACT.Copy).then_inc(s_setup_act, 1)

            def front_xT(slot):
                st, b, n, k, u = slot
                act.wait_ge(s_xT, k + 1)
                reach(act, s_proj, k)
                width = 1 if st == "A" else 2
                act.activation(xcT[:, 0:width, :], pM[:, 0:128 * width].rearrange("p (a c) -> p a c", a=width),
                               ACT.Copy).then_inc(s_xT_ev, 1)

            def front_proj(slot):
                st, b, n, k, u = slot
                if st == "B":
                    return
                act.wait_ge(s_proj, k + 1)
                reach(act, s_proj_out, k - DEEP + 1)
                act.activation(qk32[:, u % DEEP].rearrange("p a c -> p (a c)"), pM[:, 0:256], ACT.Copy)\
                    .then_inc(s_proj_ev, 1)
                act.activation(v32[:, u % DEEP, :], pM[:, 256:384], ACT.Copy).then_inc(s_proj_ev, 1)
                if st == "A":
                    act.activation(qT32[:, u % DEEP, :], pM[:, 384:448], ACT.Copy).then_inc(s_qT_ev, 1)

            def scores_split(slot):
                st, b, n, k, u = slot
                act.wait_ge(s_splitT, k + 1)
                reach(act, s_score, 4 * k - 4)
                act.activation(splitT[:, u % 2].rearrange("p r g c -> p (r g c)"), m16, ACT.Copy)\
                    .then_inc(s_splitT_ev, 1)

            def exp(slot):
                st, b, n, k, u = slot
                for j in range(NJ):
                    act.wait_ge(s_shift, 4 * k + (j + 1))
                    t = P[:, u % PBUF, j, :, 0:mw(st)]
                    act.activation(t, t, ACT.Exp).then_inc(s_exp, 1)

            def probs_hi(slot, j):
                st, b, n, k, u = slot
                act.wait_ge(s_PT, 4 * k + (j + 1))
                if j == 0:
                    reach(act, s_pv, k - 1)
                act.activation(PTh[0:mw(st), u % 2, j, :, :], pT[0:mw(st), :].rearrange("p (g l) -> p g l", g=NQ), ACT.Copy)\
                    .then_inc(s_PTh, 1)

            def carry_hi(slot):
                st, b, n, k, u = slot
                if st != "A":
                    return
                act.wait_ge(s_exp, 4 * k + 4)
                reach(act, s_pcs, n * NB + (b - 1))
                act.activation(pch[:, b % 2, 0:H, :], P[0:SEG, u % PBUF, :, :, 0:SEG].rearrange("p j g c -> p (j g) c"),
                               ACT.Copy).then_inc(s_pch, 1)

            def back_yT(slot):
                st, b, n, k, u = slot
                act.wait_ge(s_yT, k + 1)
                act.activation(yT[:], pO[:, 0:128], ACT.Copy).then_inc(s_yT_ev, 1)

            def ffn_xT(n):
                act.wait_ge(s_gT, n + 1)
                act.activation(gT32[:].rearrange("p b c -> p (b c)"), pA[:], ACT.Copy).then_inc(s_gT_ev, 1)
                act.activation(gTh[:], pA[:], ACT.Copy).then_inc(s_gT_ev, 1)

            def ffn_router(n):
                act.wait_ge(s_rt_dve, RTD * n + 3)
                act.activation(rt[:, 2], rt[:, 1], ACT.Exp).then_inc(s_rt_exp, 1)

            def ffn_chunk(n, c):
                e, q, m = CH[c]
                act.wait_ge(s_gate, n * len(CH) + (c + 1))
                if c >= 2:
                    act.wait_ge(s_h, n * len(CH) + (c - 1))
                act.activation(G[0:m, c % 2, :], pA[0:m, :], ACT.Gelu).then_inc(s_gelu, 1)

            def agent_xT(n):
                act.wait_ge(s_dpe, DPE * n + 1)
                act.activation(dT[:].rearrange("p b c -> p (b c)"), pA[:], ACT.Copy).then_inc(s_dact, 1)

            def agent_token(n):
                act.wait_ge(s_ddve, DDVE * n + 2)
                act.activation(dcol[:, 7, :], dcol[:, 7, :], ACT.Exp).then_inc(s_dact, 1)

            def agent_exp(n, dve_step, row, stat):
                act.wait_ge(s_ddve, DDVE * n + dve_step)
                act.activation(drow[:, row, :], pY[0:NB, 0:128], ACT.Exp, bias=dstat[:, stat:stat + 1],
                               accum_out=dstat[:, stat + 1:stat + 2]).then_inc(s_dact, 1)

            def fp8_xT(n):
                act.wait_ge(s_fpe, 2 * n + 1)
                act.activation(f16T[:].rearrange("p b c -> p (b c)"), pA[:], ACT.Copy).then_inc(s_fact, 1)

            def between(i, p, place):
                nC, nD, nF = others_of(i)
                at = (p, place)
                if nD is not None:
                    for part in AGENT_PE.get(at, ()):
                        if part == 1: agent_xT(nD)
                        if part == 2: agent_token(nD)
                        if part == 4: agent_exp(nD, 4, 0, 0)
                        if part == 8: agent_exp(nD, 10, 2, 2)
                if nF is not None and at == (4, 0):
                    fp8_xT(nF)
                if nC is not None:
                    if at == (4, 3):
                        ffn_xT(nC)
                    if at == (5, 0):
                        ffn_router(nC)
                    if at in CHUNKS_AT:
                        ffn_chunk(nC, CHUNKS_AT[at])

            def step(i, p):
                f, g, m, v, b = (slot_at(i, p - lag) for lag in (0, 1, 2, 3, 4))
                if g: scores_split(g)
                if v: probs_hi(v, 0)
                if f: front_xT(f)
                between(i, p, 0)
                if v: probs_hi(v, 1)
                between(i, p, 1)
                if m: exp(m)
                if f: front_proj(f)
                if v: probs_hi(v, 2)
                between(i, p, 2)
                if b: back_yT(b)
                if v: probs_hi(v, 3)
                between(i, p, 3)
                if v: carry_hi(v)

            m16 = pM[:].bitcast(F16)
            program(act, step)

        @block.gpsimd
        def _(pool):
            for t in (ctxB, ctxE, split, vl, pch, pcl):
                pool.memset(t[:], 0.0)
            pool.memset(vh[:], 1.0)
            pool.memset(half[:], -0.5)
            pool.memset(ones[:], 1.0).then_inc(s_setup_pool, 1)
            pool.wait_ge(s_const, n_const)

            def carry_pool(c):
                pool.tensor_tensor(idle_pool[:, c:c + 1], half[:, 0:1], half[:, 0:1], ALU.add)

            def halves(out, in_):
                return pool.tensor_scalar(out, in_, 1.0, 1.0, ALU.mult, ALU.mult)

            def front_split(slot):
                st, b, n, k, u = slot
                pool.wait_ge(s_proj_ev, 2 * k + 2)
                reach(pool, s_splitT, k - 1)
                carry_pool(0)
                qk = qk32[:, u % DEEP].rearrange("p r (h d) -> p r h d", h=H)
                v = v32[:, u % DEEP].rearrange("p (h d) -> p h d", h=H)
                t = split[:, u % 2]
                halves(t[:, :, :, 0, :], qk)
                halves(t[:, 0, :, 1, :], qk[:, 0])
                halves(t[:, 1, :, 2, :], qk[:, 1]).then_inc(s_hi, 1)
                halves(vh[:, u % DEEP, :, 0:DH], v).then_inc(s_vhi, 1)
                pool.wait_ge(s_hi, k + 1)
                pool.tensor_tensor(t[:, 0, :, 2, :], qk[:, 0], t[:, 0, :, 0, :], ALU.subtract)
                pool.tensor_tensor(t[:, 1, :, 1, :], qk[:, 1], t[:, 1, :, 0, :], ALU.subtract).then_inc(s_split, 1)
                pool.wait_ge(s_vhi, k + 1)
                pool.tensor_tensor(vl[:, u % DEEP, :, 0:DH], v, vh[:, u % DEEP, :, 0:DH], ALU.subtract)\
                    .then_inc(s_vsplit, 1)

            def shift(slot, j):
                st, b, n, k, u = slot
                pool.wait_ge(s_max, 4 * k + (j + 1))
                t = P[:, u % PBUF, j, :, 0:mw(st)]
                pool.tensor_tensor(t, t, smax[:, u % PBUF, j, :].unsqueeze(2).to_broadcast([128, NQ, mw(st)]),
                                   ALU.subtract).then_inc(s_shift, 1)

            def carry_lo(slot):
                st, b, n, k, u = slot
                if st != "A":
                    return
                pool.wait_ge(s_pch, n * NB + (b + 1))
                pool.tensor_tensor(pcl[:, b % 2, 0:H, :],
                                   P[0:SEG, u % PBUF, :, :, 0:SEG].rearrange("p j g c -> p (j g) c"),
                                   pch[:, b % 2, 0:H, :], ALU.subtract).then_inc(s_pcl, 1)

            def back_rstd(slot):
                st, b, n, k, u = slot
                pool.wait_ge(s_ve, k + 1)
                pool.tensor_tensor(rstd[:, u % 2:u % 2 + 1], ve[:, u % 2:u % 2 + 1], half[:, 0:1], ALU.pow)\
                    .then_inc(s_rstd, 1)

            def group_rstd(s, n):
                pool.wait_ge(s_gve[s], n + 1)
                pool.tensor_tensor(grs[s][:], gve[s][:], half[:], ALU.pow).then_inc(s_grs[s], 1)

            def split_weights(hi, lo, a):
                t = ffn_buf[:].rearrange("p a b c -> p (a b c)")[:, 0:NE * FF]
                pool.wait_ge(s_wtmp, 16 * (a + 1))
                flat = lambda w: w[:].rearrange("p e f -> p (e f)")
                halves(flat(hi), t).then_inc(s_ffn_split, 2)
                pool.wait_ge(s_ffn_split, 4 * a + 2)
                pool.tensor_tensor(flat(lo), t, flat(hi), ALU.subtract).then_inc(s_ffn_split, 2)

            def ffn_start(n):
                pool.wait_ge(s_gT_ev, 2 * n + 2)
                pool.tensor_tensor(gTl[:], gT32[:].rearrange("p b c -> p (b c)"), gTh[:], ALU.subtract)\
                    .then_inc(s_gTl, 1)
                reach(pool, s_gln["D"], NB * n)
                pool.tensor_tensor(acc[:], xb[:], bias[:, 4, :].unsqueeze(1).to_broadcast([128, NB, 128]), ALU.add)\
                    .then_inc(s_acc, 1)

            def ffn_add(n, e):
                pool.wait_ge(s_acc, (NE + 1) * n + (e + 1))
                pool.wait_ge(s_yw, NE * n + (e + 1))
                pool.tensor_tensor(acc[:], acc[:], yw[:, e % 2], ALU.add).then_inc(s_acc, 1)

            def between(i, p, place):
                nC, nD, nF = others_of(i)
                at = (p, place)
                if isinstance(i, int) and i == 0 and place == 0:
                    if p == 4: split_weights(w1h, w1l, 0)
                    if p == 9: split_weights(v1h, v1l, 1)
                if nD is not None:
                    if at == (0, 0):
                        ffn_add(nD, NE - 1)
                        group_rstd("C", nD)
                    if at == (3, 3):
                        group_rstd("D", nD)
                if nF is not None and at == (4, 3):
                    group_rstd("F", nF)
                if nC is not None:
                    if at == (4, 3):
                        ffn_start(nC)
                    c = CHUNKS_AT.get(at, 0)
                    if c > 0 and c % 3 == 0:
                        ffn_add(nC, c // 3 - 1)

            def step(i, p):
                f, g, v, b = (slot_at(i, p - lag) for lag in (0, 1, 3, 4))
                between(i, p, 0)
                if g:
                    shift(g, 0)
                    shift(g, 1)
                between(i, p, 1)
                if f: front_split(f)
                between(i, p, 2)
                if g:
                    shift(g, 2)
                    shift(g, 3)
                if b: back_rstd(b)
                if v: carry_lo(v)
                between(i, p, 3)

            program(pool, step)

        @block.vector
        def _(dve):
            def carry_dve(c):
                dve.memset(idle[:, c:c + 1], 0.0)

            done_setup = [0]

            def step(ins):
                done_setup[0] += 1
                ins.then_inc(s_setup_dve, 1)
                dve.wait_ge(s_setup_dve, done_setup[0])

            dve.wait_ge(s_const, n_const)
            dve.wait_ge(s_w, 32)
            dve.wait_ge(s_setup_act, 4)
            rs8 = 1.0 / float(np.sqrt(DH))
            for a in (0, 4, 8):
                dve.tensor_scalar(w[:, a, :], w[:, a, :], rs8, None, ALU.mult)
            dve.tensor_scalar(bias[:, 0, :], bias[:, 0, :], rs8, None, ALU.mult)
            step(dve.tensor_scalar(mask0[:], mask0[:], NEG, None, ALU.mult))
            step(dve.tensor_scalar(mix[:, 1:2], mix[:, 1:2], 1.0, None, ALU.add))
            step(dve.reciprocal(mix[:, 2:3], mix[:, 1:2]))
            step(dve.tensor_scalar(mix[:, 3:4], mix[:, 2:3], -1.0, 1.0, ALU.mult, ALU.add))
            step(dve.tensor_scalar(mega[:], mega[:], 0.0, 2.0, ALU.max, ALU.min))
            step(dve.tensor_scalar(mega[:], mega[:], 0.0, None, ALU.mult))
            step(dve.tensor_tensor(decay[:], decay[:], mega[:], ALU.add))
            step(dve.tensor_copy(w8i[:, 0, :], w8raw[:]))
            dve.tensor_scalar(w8i[:, 1, :], w8i[:, 0, :], 3, 15, ALU.logical_shift_right, ALU.bitwise_and)
            dve.tensor_scalar(w8i[:, 2, :], w8i[:, 0, :], 7, None, ALU.bitwise_and)
            step(dve.tensor_scalar(w8i[:, 3, :], w8i[:, 0, :], 7, None, ALU.logical_shift_right))
            dve.tensor_scalar(w8f[:, 0, :], w8i[:, 1, :], 0.0, 8.0, ALU.is_gt, ALU.mult)
            dve.tensor_scalar(w8i[:, 1, :], w8i[:, 1, :], 1.0, 117.0, ALU.max, ALU.add)
            step(dve.tensor_scalar(w8f[:, 1, :], w8i[:, 3, :], -2.0, 1.0, ALU.mult, ALU.add))
            dve.tensor_scalar(w8i[:, 1, :], w8i[:, 1, :], 23, None, ALU.logical_shift_left)
            step(dve.tensor_tensor(w8f[:, 0, :], w8f[:, 0, :], w8i[:, 2, :], ALU.add))
            step(dve.tensor_tensor(w8f[:, 0, :], w8f[:, 0, :], w8f[:, 1, :], ALU.mult))
            dve.tensor_tensor(w8[:], w8f[:, 0, :], w8i[:, 1, :].bitcast(F32), ALU.mult)
            dve.wait_ge(s_setup_pe, 1)
            step(dve.tensor_copy(u_col[:], pY[:, 0:1]))

            def front_proj(slot):
                st, b, n, k, u = slot
                if st != "B":
                    return
                dve.wait_ge(s_proj, k + 1)
                reach(dve, s_proj_out, k - DEEP + 1)
                dve.tensor_tensor(qk32[:, u % DEEP].rearrange("p a c -> p (a c)"), pM[:, 0:256],
                                  bias[:, 0:2, :].rearrange("p a c -> p (a c)"), ALU.add).then_inc(s_proj_ev, 1)
                dve.tensor_tensor(v32[:, u % DEEP, :], pM[:, 256:384], bias[:, 2, :], ALU.add).then_inc(s_proj_ev, 1)

            def scores(slot, j, old=None):
                st, b, n, k, u = slot
                m = mw(st)
                dve.wait_ge(s_score, 4 * k + (j + 1))
                if j == 0:
                    reach(dve, s_PTl, 4 * (k - PBUF + 1))
                    if old and old[0] == "A":
                        dve.wait_ge(s_pcl, old[2] * NB + (old[1] + 1))
                if st == "E" and j == 0:
                    dve.wait_ge(s_mask1, (n + 1) * 16)
                carry_dve(j % 2)
                mask = {"A": causal[:], "B": mask0[:], "E": mask1[:, b, :]}[st]
                for g in range(NQ):
                    last = dve.tensor_tensor_reduce(P[:, u % PBUF, j, g, 0:m], pS[j % 2][:, 128 * g:128 * g + m], mask,
                                                    1.0, -3e38, ALU.add, ALU.max, smax[:, u % PBUF, j, g:g + 1])
                last.then_inc(s_max, 1)

            def probs_lo(slot, j):
                st, b, n, k, u = slot
                dve.wait_ge(s_PTh, 4 * k + (j + 1))
                if j == 0:
                    reach(dve, s_pv, k - 1)
                dve.tensor_tensor(PTl[0:mw(st), u % 2, j, :, :], pT[0:mw(st), :].rearrange("p (g l) -> p g l", g=NQ),
                                  PTh[0:mw(st), u % 2, j, :, :], ALU.subtract).then_inc(s_PTl, 1)

            def oview():
                return pO[:, 0:H * (DH + 1)].rearrange("p (h d) -> p h d", h=H)

            def back_y(slot):
                st, b, n, k, u = slot
                i = u % 2
                na = n * NB + (b + 1)
                dve.wait_ge(s_pv, k + 1)
                dve.reciprocal(rz[:, i, :], oview()[:, :, DH]).then_inc(s_rz, 1)
                dve.wait_ge(s_rz, k + 1)
                if st == "A":
                    dve.tensor_tensor(carry_w[:], rz[0:SEG, i, :], decay[:], ALU.mult).then_inc(s_rl, 1)
                    dve.wait_ge(s_rl, na)
                    dve.tensor_scalar(rz[:, i, :], rz[:, i, :], mix[:, 2:3], None, ALU.mult).then_inc(s_rzt, 1)
                    dve.tensor_copy(carry_h[:], carry_w[:]).then_inc(s_rlh, 1)
                    dve.wait_ge(s_rzt, na)
                last = dve.tensor_tensor(yo[:, i, :].rearrange("p (h d) -> p h d", h=H), oview()[:, :, 0:DH],
                                         rz[:, i, :].unsqueeze(2).to_broadcast([128, H, DH]), ALU.mult)
                last.then_inc(s_yo, 1)
                if st == "A":
                    dve.wait_ge(s_rlh, na)
                    dve.tensor_tensor(carry_l[:], carry_w[:], carry_h[:], ALU.subtract).then_inc(s_rll, 1)

            def back_vp(slot):
                st, b, n, k, u = slot
                if st != "A":
                    return
                dve.wait_ge(s_pcs, n * NB + (b + 1))
                dve.tensor_tensor(vp[:].rearrange("p (h d) -> p h d", h=H),
                                  v32[0:SEG, u % DEEP, :].rearrange("p (h d) -> p h d", h=H),
                                  pO[0:SEG, 0:H].unsqueeze(2).to_broadcast([SEG, H, DH]), ALU.mult).then_inc(s_vp, 1)
                dve.tensor_copy(pcs[:], pO[0:SEG, 0:H]).then_inc(s_vp, 1)

            def back_kvm(slot):
                st, b, n, k, u = slot
                if st != "A":
                    return
                dve.wait_ge(s_kv, n * NB + (b + 1))
                dve.tensor_scalar(rsum[SEG:128, :], pO[SEG:128, 128:128 + H], EPS, None, ALU.add)\
                    .then_inc(s_kvm, 1)
                dve.tensor_tensor(kvm[:], pO[:, 0:128], block_diag[:], ALU.mult).then_inc(s_kvm, 1)

            def back_ylin(slot):
                st, b, n, k, u = slot
                if st != "A":
                    return
                na = n * NB + b
                dve.wait_ge(s_kvm, 2 * na + 2)
                dve.reciprocal(rsum[SEG:128, :], rsum[SEG:128, :]).then_inc(s_lin_ev, 1)
                dve.wait_ge(s_lin_ev, 3 * na + 1)
                dve.tensor_scalar(rsum[SEG:128, :], rsum[SEG:128, :], mix[SEG:128, 3:4], None, ALU.mult)\
                    .then_inc(s_lin_ev, 1)
                dve.wait_ge(s_lin_ev, 3 * na + 2)
                dve.wait_ge(s_lin, na + 1)
                dve.tensor_tensor(ylin[SEG:128, :].rearrange("p (h d) -> p h d", h=H),
                                  pO[SEG:128, 0:128].rearrange("p (h d) -> p h d", h=H),
                                  rsum[SEG:128, :].unsqueeze(2).to_broadcast([SEG, H, DH]), ALU.mult)\
                    .then_inc(s_lin_ev, 1)
                dve.wait_ge(s_lin_ev, 3 * na + 3)
                dve.tensor_tensor(yo[SEG:128, u % 2, :], yo[SEG:128, u % 2, :], ylin[SEG:128, :], ALU.add)\
                    .then_inc(s_y, 1)

            def back_res(slot):
                st, b, n, k, u = slot
                i = u % 2
                dve.wait_ge(s_proj_out, k + 1)
                dve.tensor_tensor(res[:, i, :], pO[:, 0:128], x_of[st][:, b, :], ALU.add).then_inc(s_res, 1)
                dve.wait_ge(s_res, k + 1)
                if st == "B":
                    dve.tensor_tensor(res[:, i, :], res[:, i, :], bias[:, 3, :], ALU.add).then_inc(s_resb, 1)
                    dve.wait_ge(s_resb, n * NB + (b + 1))
                dve.bn_stats(st6[:, i, :], res[:, i, :]).then_inc(s_st, 1)
                dve.wait_ge(s_st, k + 1)
                carry_dve(2)
                dve.bn_aggr(mv[:, i, :], st6[:, i, :]).then_inc(s_mv, 1)
                dve.wait_ge(s_mv, k + 1)
                dve.tensor_scalar(ve[:, i:i + 1], mv[:, i, 1:2], EPS, None, ALU.add).then_inc(s_ve, 1)

            def last_norm(slot):
                st, b, n, k, u = slot
                i = u % 2
                dve.wait_ge(s_rstd, k + 1)
                if st == "B":
                    reach(dve, s_acc, (NE + 1) * (n - 1) + 1)
                    reach(dve, s_gT, n)
                dve.tensor_scalar(dst_of[st][:, b, :], res[:, i, :], mv[:, i, 0:1], rstd[:, i:i + 1],
                                  ALU.subtract, ALU.mult).then_inc(s_ln[st], 1)

            def group_stats(s, n, src):
                for b in range(NB):
                    dve.bn_stats(gst[s][:, b, :], src[:, b, :]).then_inc(s_gst[s], 1)
                dve.wait_ge(s_gst[s], NB * n + NB)
                carry_dve(3)
                for b in range(NB):
                    dve.bn_aggr(gmv[s][:, b, :], gst[s][:, b, :]).then_inc(s_gmv[s], 1)
                dve.wait_ge(s_gmv[s], NB * n + NB)
                dve.tensor_scalar(gve[s][:], gmv[s][:, :, 1], EPS, None, ALU.add).then_inc(s_gve[s], 1)

            def group_norm(s, n, src, dst):
                dve.wait_ge(s_grs[s], n + 1)
                for b in range(NB):
                    dve.tensor_scalar(dst[:, b, :], src[:, b, :], gmv[s][:, b, 0:1], grs[s][:, b:b + 1],
                                      ALU.subtract, ALU.mult).then_inc(s_gln[s], 1)

            def router_step(n, number, ins):
                ins.then_inc(s_rt_dve, 1)
                dve.wait_ge(s_rt_dve, RTD * n + number)

            def router_logits(n):
                dve.wait_ge(s_rt, n + 1)
                router_step(n, 1, dve.tensor_copy(rt[:, 0].rearrange("p b e -> p (b e)"), pY[:, 0:NB * NE]))
                router_step(n, 2, dve.tensor_reduce(rts[:, 0, :], rt[:, 0], AX.X, ALU.max))
                router_step(n, 3, dve.tensor_tensor(rt[:, 1], rt[:, 0],
                                                    rts[:, 0, :].unsqueeze(2).to_broadcast([128, NB, NE]), ALU.subtract))

            def router_gates(n):
                def over(t, a):
                    return t.unsqueeze(a).to_broadcast([128, NB, NE, NE])

                above = lower[:, NE * NE:].unsqueeze(1).to_broadcast([128, NB, NE])
                dve.wait_ge(s_rt_exp, n + 1)
                router_step(n, 4, dve.tensor_reduce(rts[:, 1, :], rt[:, 2], AX.X, ALU.add))
                router_step(n, 5, dve.reciprocal(rts[:, 2, :], rts[:, 1, :]))
                router_step(n, 6, dve.tensor_tensor(rt[:, 3], rt[:, 2],
                                                    rts[:, 2, :].unsqueeze(2).to_broadcast([128, NB, NE]), ALU.mult))
                router_step(n, 7, dve.tensor_tensor(rt64[:, 0], over(rt[:, 3], 2), over(rt[:, 3], 3), ALU.is_ge))
                router_step(n, 8, dve.tensor_tensor(rt64[:, 1], rt64[:, 0],
                                                    lower[:, 0:NE * NE].rearrange("p (a c) -> p a c", a=NE).unsqueeze(1)
                                                    .to_broadcast([128, NB, NE, NE]), ALU.mult))
                dve.tensor_reduce(rt[:, 4], rt64[:, 1], AX.X, ALU.add)
                router_step(n, 9, dve.tensor_reduce(rt[:, 5], rt64[:, 1].rearrange("p b a c -> p b c a"), AX.X, ALU.add))
                router_step(n, 10, dve.tensor_tensor(rt[:, 6], rt[:, 4], rt[:, 5], ALU.subtract))
                router_step(n, 11, dve.tensor_tensor(rt[:, 6], rt[:, 6], above, ALU.add))
                router_step(n, 12, dve.scalar_tensor_tensor(out=rt[:, 7], in0=rt[:, 6], scalar=1.5, in1=rt[:, 3],
                                                            op0=ALU.is_lt, op1=ALU.mult))

            def ffn_weigh(n, e):
                dve.wait_ge(s_y2, n * len(CH) + 3 * (e + 1))
                if e >= 2:
                    dve.wait_ge(s_acc, (NE + 1) * n + e)
                dve.tensor_tensor(yw[:, e % 2], pY[:].rearrange("p (b c) -> p b c", b=NB),
                                  rt[:, 7, :, e].unsqueeze(2).to_broadcast([128, NB, 128]), ALU.mult)\
                    .then_inc(s_yw, 1)

            def ffn_chunk(n, c):
                e, q, m = CH[c]
                dve.wait_ge(s_gelu, n * len(CH) + (c + 1))
                dve.wait_ge(s_val, n * len(CH) + (c + 1))
                if c >= 2:
                    dve.wait_ge(s_y2, n * len(CH) + (c - 1))
                dve.tensor_tensor(Hh[0:m, c % 2, :], pB[0:m, :], G[0:m, c % 2, :], ALU.mult).then_inc(s_h, 1)
                if q == 0 and e >= 1:
                    ffn_weigh(n, e - 1)

            def agent(n, part):
                def step(number, ins):
                    ins.then_inc(s_ddve, 1)
                    dve.wait_ge(s_ddve, DDVE * n + number)

                def product(i):
                    dve.wait_ge(s_dpe, DPE * n + i)

                def exped(i):
                    dve.wait_ge(s_dact, DACT * n + i)

                if part == 2:
                    product(2)
                    step(1, dve.tensor_scalar(dcol[:, 0, :], pY[:, 0:NB], float(D) ** -0.5, None, ALU.mult))
                    step(2, dve.tensor_tensor(dcol[:, 7, :], dcol[:, 0, :], dcol[:, 0, :], ALU.subtract))
                elif part == 3:
                    product(3)
                    step(3, dve.tensor_copy(dcol[:, 1, :], pY[:, 0:NB]))
                elif part == 4:
                    product(4)
                    step(4, dve.tensor_reduce(dstat[:, 0:1], pY[0:NB, 0:128], AX.X, ALU.max, negate=True))
                elif part == "softmax c":
                    exped(3)
                    step(5, dve.reciprocal(dstat[:, 1:2], dstat[:, 1:2]))
                    step(6, dve.tensor_scalar(drow[:, 1, :], drow[:, 0, :], dstat[:, 1:2], None, ALU.mult))
                elif part in (5, 6, 7):
                    product(part)
                    step(part + 2, dve.tensor_copy(dcol[:, part - 3, :], pY[:, 0:NB]))
                elif part == 8:
                    product(8)
                    step(10, dve.tensor_reduce(dstat[:, 2:3], pY[0:NB, 0:128], AX.X, ALU.max, negate=True))
                elif part == "softmax n":
                    exped(4)
                    step(11, dve.reciprocal(dstat[:, 3:4], dstat[:, 3:4]))
                    step(12, dve.tensor_scalar(drow[:, 3, :], drow[:, 2, :], dstat[:, 3:4], None, ALU.mult))
                elif part in (9, 10):
                    product(part)
                    step(part + 4, dve.tensor_copy(dcol[:, part - 4, :], pY[:, 0:NB]))
                elif part == 11:
                    product(11)
                    for b in range(NB):
                        dve.scalar_tensor_tensor(out=acc[:, b, :], in0=pB[:, 128 * b:128 * b + 128],
                                                 scalar=dcol[:, 7, b:b + 1], in1=xc[:, b, :], op0=ALU.mult,
                                                 op1=ALU.add).then_inc(s_ddve, 1)
                    dve.wait_ge(s_ddve, DDVE * (n + 1))
                    group_stats("D", n, acc)

            def fp8_step(n, number, ins):
                ins.then_inc(s_fdve, 1)
                dve.wait_ge(s_fdve, FDVE * n + number)

            def fp8_scale(n):
                dve.wait_ge(s_ln["E"], NB * (n + 1))
                fp8_step(n, 1, dve.tensor_reduce(fsc[:, 0, :], xe[:], AX.X, ALU.max, apply_absolute_value=True))
                fp8_step(n, 2, dve.tensor_scalar(fsc[:, 1, :], fsc[:, 0, :], 1e-12, 1.0 / 448.0, ALU.max, ALU.mult))
                dve.tensor_scalar(fsc[:, 3, :], fsc[:, 1, :], wscale[:, 0:1], None, ALU.mult)
                fp8_step(n, 3, dve.reciprocal(fsc[:, 2, :], fsc[:, 1, :]))
                fp8_step(n, 4, dve.tensor_tensor(fq[:, 0], xe[:], fsc[:, 2, :].unsqueeze(2).to_broadcast([128, NB, 128]),
                                                 ALU.mult))

            def fp8_round(n):
                fp8_step(n, 5, dve.tensor_scalar(fq[:, 1].bitcast(I32), fq[:, 0].bitcast(I32), 0x7F800000, None,
                                                 ALU.bitwise_and))
                fp8_step(n, 6, dve.tensor_scalar(fq[:, 1], fq[:, 1], 2.0 ** -6, 1.5 * 2.0 ** 20, ALU.max, ALU.mult))
                fp8_step(n, 7, dve.tensor_tensor(fq[:, 0], fq[:, 0], fq[:, 1], ALU.add))
                fp8_step(n, 8, dve.tensor_tensor(fq[:, 2], fq[:, 0], fq[:, 1], ALU.subtract))

            def fp8_finish(n):
                dve.wait_ge(s_fpe, 2 * n + 2)
                for b in range(NB):
                    dve.scalar_tensor_tensor(out=facc[:, b, :], in0=pB[:, 128 * b:128 * b + 128],
                                             scalar=fsc[:, 3, b:b + 1], in1=bias[:, 5, :], op0=ALU.mult,
                                             op1=ALU.add).then_inc(s_fdve, 1)
                dve.wait_ge(s_fdve, FDVE * n + 12)
                fp8_step(n, 13, dve.tensor_tensor(facc[:], facc[:], xe[:], ALU.add))
                group_stats("F", n, facc)

            def between(i, p, place):
                nC, nD, nF = others_of(i)
                at = (p, place)
                if nD is not None:
                    if at == (0, 0):
                        ffn_weigh(nD, NE - 1)
                        dve.wait_ge(s_acc, (NE + 1) * (nD + 1))
                        group_stats("C", nD, acc)
                    if at == (0, 1):
                        group_norm("C", nD, acc, xc)
                    for part in AGENT_DVE.get(at, ()):
                        agent(nD, part)
                    if at == (3, 3):
                        group_norm("D", nD, acc, xd)
                if nF is not None:
                    if at == (3, 0):
                        fp8_scale(nF)
                    if at == (3, 1):
                        fp8_round(nF)
                    if at == (4, 2):
                        fp8_finish(nF)
                    if at == (5, 0):
                        reach(dve, s_out, 16 * nF)
                        group_norm("F", nF, facc, yout)
                if nC is not None:
                    if at == (5, 0):
                        router_logits(nC)
                    if at == (5, 1):
                        router_gates(nC)
                    if at in CHUNKS_AT:
                        ffn_chunk(nC, CHUNKS_AT[at])

            def step(i, p):
                f, g, v, b, c = (slot_at(i, p - lag) for lag in (0, 1, 3, 4, 5))
                if v: probs_lo(v, 0)
                if b: back_y(b)
                between(i, p, 0)
                if g:
                    scores(g, 0, slot_before(i, p - 1, PBUF))
                    scores(g, 1)
                if b: back_vp(b)
                if v: probs_lo(v, 1)
                if c: last_norm(c)
                between(i, p, 1)
                if b: back_kvm(b)
                if f: front_proj(f)
                if v: probs_lo(v, 2)
                if b: back_ylin(b)
                if g: scores(g, 2)
                between(i, p, 2)
                if g: scores(g, 3)
                if v: probs_lo(v, 3)
                if b: back_res(b)
                between(i, p, 3)

            dve.wait_ge(s_setup_pool, 1)
            program(dve, step)


def kernel(**inputs):
    import concourse.bacc as bacc
    from concourse.bass_utils import run_bass_kernel_spmd

    a = {k: np.ascontiguousarray(v) for k, v in inputs.items()}
    flat = lambda t: t.reshape(128, 128)
    l1 = a["L1_attn_w_qkv"]
    mats = [a["L0_attn_Wq"].T, a["L0_attn_Wk"].T, a["L0_attn_Wv"].T, a["L0_attn_Wc"].T,
            a["L0_xattn_Wq"], a["L0_xattn_Wk"], a["L0_xattn_Wv"], a["L0_xattn_Wo"],
            flat(a["L1_xattn_wq"]), flat(a["L1_xattn_wk"]), flat(a["L1_xattn_wv"]), flat(a["L1_xattn_wo"]),
            l1[0:128], l1[128:256].T, l1[256:384], l1[256:384].T]
    arrays = {
        "x": a["x"], "ctx": a["ctx_1024"], "mask0": a["mask_1x1xSxS2_fk1"], "mask1": a["mask_Bx1xSxS2_ff0"],
        "w": np.stack(mats),
        "bias": np.concatenate([a["L0_xattn_bq"], a["L0_xattn_bk"], a["L0_xattn_bv"], a["L0_xattn_bo"],
                                a["L0_ffn_bias"], a["L1_ffn_bias"]]),
        "terrace": a["L0_attn_terrace_mix"].reshape(SEG, 1),
        "decay": a["L0_attn_index_decays"].T, "mega": a["L0_attn_mega_decays"],
        "rw": a["L0_ffn_router_w"], "w1": a["L0_ffn_w1"], "v1": a["L0_ffn_v1"], "w2": a["L0_ffn_w2"],
        "conv": a["L1_attn_w_conv1"].reshape(128, 1),
        "w8": a["L1_ffn_weight"].view(np.uint8).T, "wscale": a["L1_ffn_weight_scale"].reshape(1),
        "ident": np.eye(128, dtype=np.float32),
        "causal": np.where(np.tril(np.ones((128, 128), bool)), 0.0, -1e30).astype(np.float32),
        "block": (np.kron(np.eye(H), np.ones((DH, DH))) * np.sqrt(DH)).astype(np.float32),
        "lower": np.tile(np.concatenate([np.tril(np.ones((NE, NE)), -1).ravel(), NE - 1.0 - np.arange(NE)]), (128, 1))
        .astype(np.float32),
    }
    nc = bacc.Bacc("TRN2", target_bir_lowering=False, num_devices=1)
    feeds, args = {}, []
    for name, t in arrays.items():
        t = np.ascontiguousarray(t)
        feeds[f"in_{name}"] = t
        args.append(nc.dram_tensor(f"in_{name}", t.shape, mybir.dt.from_np(t.dtype), kind="ExternalInput").ap())
    args.append(nc.dram_tensor("out_0", (NSEQ, S, D), F32, kind="ExternalOutput").ap())
    decoder(nc, *args)
    r = run_bass_kernel_spmd(nc, [feeds], core_ids=[0])
    return r.results[0]["out_0"]
```

```python
from contextlib import ExitStack

import numpy as np
import concourse.bass as bass
from concourse import mybir

ALU = mybir.AluOpType
ACT = mybir.ActivationFunctionType
AX = mybir.AxisListType
F32 = mybir.dt.float32
F16 = mybir.dt.float16
I32 = mybir.dt.int32
U8 = mybir.dt.uint8

NSEQ, S, D, S2 = 32, 128, 128, 120
H, DH, SEG = 16, 8, 64
NB = 4
NG = NSEQ // NB
NJ, NQ = 4, 4
TERM = 32
NE, FF = 8, 352
CH = [(e, q, min(128, FF - 128 * q)) for e in range(NE) for q in range(3)]
POSITIONS = [("A", 0, 0), ("A", 1, 0), ("A", 2, 0), ("A", 3, 0), ("E", 2, 3), ("E", 3, 3), ("B", 0, 0), ("E", 0, 2),
             ("B", 1, 0), ("E", 1, 2), ("B", 2, 0), ("B", 3, 0)]
STEPS = len(POSITIONS)
E_LAST = 5
FIRST_FULL = 4
LAST = NG + 3
TAIL = 5
_places = [(s % STEPS, p) for s in range(6, 14) for p in (0, 2, 3)]
CHUNKS_AT = {_at: (_c,) for _c, _at in enumerate(_places)}
assert len(_places) == len(CH)
AGENT_PE = {(2, 2): (1,), (2, 3): (2,), (3, 0): (3,), (3, 1): (4,), (3, 3): (5,), (4, 0): (6,), (4, 1): (7,),
            (4, 2): (8,), (5, 0): (9,), (5, 1): (10,), (5, 2): (11,)}
AGENT_DVE = {(2, 3): (2,), (3, 0): (3,), (3, 1): (4,), (3, 2): ("softmax c",), (3, 3): (5,), (4, 0): (6,),
             (4, 1): (7,), (4, 2): (8,), (4, 3): ("softmax n",), (5, 0): (9,), (5, 1): (10,), (5, 2): (11,)}
NEG = -1000000000.0
EPS = 1e-5
DEEP = 6
PBUF = 4
WQ, WK, WV, WO = range(4)


def reach(eng, sem, value):
    if isinstance(value, int) and value <= 0:
        return
    eng.wait_ge(sem, value)


def slot_at(i, p):
    if i_has_no_step(i, p):
        return None
    if p < 0:
        return slot_at(i - 1, p + STEPS)
    st, b, late = POSITIONS[p]
    if not isinstance(i, int):
        return st, b, i - late, STEPS * i - 10 + p, (p + 2) % STEPS
    steps = [(t, q) for t in range(i + 1) for q in range(STEPS) if t < i or q < p]
    k = sum(is_slot(t, q) for t, q in steps)
    if not is_slot(i, p):
        return None
    if 0 <= i - late < NG:
        return st, b, i - late, k, k % STEPS
    return "E", p - (STEPS - NB), NG - 1, k, k % STEPS


def is_slot(i, p):
    late = POSITIONS[p][2]
    if p >= STEPS - 2 and i == NG + 1:
        return True
    return 0 <= i - late < NG and not (late == 3 and i == NG + 2)


def slot_before(i, p, count):
    while count:
        p -= 1
        if i_has_no_step(i, p):
            return None
        count -= slot_at(i, p) is not None
    return slot_at(i, p)


def i_has_no_step(i, p):
    return isinstance(i, int) and STEPS * i + p < 0


def others_of(i):
    if not isinstance(i, int):
        return i - 1, i - 2, i - 3, i - 4
    return [i - late if 0 <= i - late < NG else None for late in (1, 2, 3, 4)]


def program(eng, step):
    for i in range(FIRST_FULL):
        for p in range(STEPS):
            step(i, p)
    with eng.Fori(FIRST_FULL, NG) as i:
        for p in range(STEPS):
            step(i, p)
    for i in range(NG, LAST + 1):
        for p in range(STEPS if i < LAST else TAIL):
            step(i, p)


def decoder(nc, x_d, ctx_d, mask0_d, mask1_d, w_d, bias_d, terrace_d, decay_d, mega_d, rw_d, w1_d, v1_d,
            w2_d, conv_d, w8_d, wscale_d, ident_d, causal_d, block_d, lower_d, out_d):
    with ExitStack() as ctx:
        def sb(name, shape, dt=F32):
            return ctx.enter_context(nc.sbuf_tensor(name, shape, dt))

        def ps(name):
            return ctx.enter_context(nc.psum_tensor(name, [128, 512], F32))

        def sem(name):
            return ctx.enter_context(nc.semaphore(name))

        pS = [ps("pS0"), ps("pS1")]
        pT = ps("pT")
        pM = ps("pM")
        pO = ps("pO")
        pA, pB, pY = ps("pA"), ps("pB"), ps("pY")

        ident = sb("ident", [128, 128])
        ident16 = sb("ident16", [128, 128], F16)
        causal = sb("causal", [128, 128])
        block_diag = sb("block_diag", [128, 128])
        lower = sb("lower", [128, NE * NE + NE])
        ones = sb("ones", [128, 128])
        w = sb("w", [128, 16, 128])
        bias = sb("bias", [128, 6, 128])
        mask0 = sb("mask0", [128, S2])
        mix = sb("mix", [128, 4])
        decay = sb("decay", [SEG, H])
        mega = sb("mega", [SEG, H])
        rw = sb("rw", [128, NE])
        w1h, w1l = sb("w1h", [128, NE, FF], F16), sb("w1l", [128, NE, FF], F16)
        v1h, v1l = sb("v1h", [128, NE, FF], F16), sb("v1l", [128, NE, FF], F16)
        w2 = sb("w2", [128, NE, 3, 128])
        conv = sb("conv", [128, 1])
        u_col = sb("u_col", [128, 1])
        w8raw = sb("w8raw", [128, 128], U8)
        w8i = sb("w8i", [128, 4, 128], I32)
        w8f = sb("w8f", [128, 3, 128])
        w8 = sb("w8", [128, 128], F16)
        wscale = sb("wscale", [128, 1])
        half = sb("half", [128, 4])

        idle = sb("idle", [128, 6])
        idle_pool = sb("idle_pool", [128, 2])

        x0 = sb("x0", [128, NB, 128])
        xa = sb("xa", [128, NB, 128])
        xb = sb("xb", [128, NB, 128])
        xc = sb("xc", [128, NB, 128])
        xd = sb("xd", [128, NB, 128])
        xe = sb("xe", [128, NB, 128])
        xf = sb("xf", [128, NB, 128])
        yout = sb("yout", [128, NB, 128])
        ctxB = sb("ctxB", [128, NB, 128])
        ctxE = sb("ctxE", [128, NB, 128])
        mask1 = sb("mask1", [128, NB, S2])

        xcT = sb("xcT", [128, 2, 128])
        qk32 = sb("qk32", [128, DEEP, 2, 128])
        qT32 = sb("qT32", [128, DEEP, SEG])
        v32 = sb("v32", [128, DEEP, 128])
        vh = sb("vh", [128, DEEP, H, DH + 1], F16)
        vl = sb("vl", [128, DEEP, H, DH + 1], F16)
        split = sb("split", [128, 2, 2, H, 4, DH], F16)
        splitT = sb("splitT", [128, 2, 2, NQ, 128], F16)
        P = sb("P", [128, PBUF, NJ, NQ, 128])
        smax = sb("smax", [128, PBUF, NJ, NQ])
        PTh = sb("PTh", [128, 2, NJ, NQ, 128], F16)
        PTl = sb("PTl", [128, 2, NJ, NQ, 128], F16)
        pch = sb("pch", [SEG, 2, H + 1, SEG], F16)
        pcl = sb("pcl", [SEG, 2, H + 1, SEG], F16)
        rz = sb("rz", [128, 2, H])
        carry_w = sb("carry_w", [SEG, H])
        carry_h = sb("carry_h", [SEG, H], F16)
        carry_l = sb("carry_l", [SEG, H], F16)
        yo = sb("yo", [128, 2, 128])
        pcs = sb("pcs", [SEG, H])
        vp = sb("vp", [SEG, 128])
        kvm = sb("kvm", [128, 128])
        rsum = sb("rsum", [128, H])
        ylin = sb("ylin", [128, 128])
        yT = sb("yT", [128, 128])
        res = sb("res", [128, 2, 128])
        st6 = sb("st6", [128, 2, 6])
        mv = sb("mv", [128, 2, 2])
        ve = sb("ve", [128, 2])
        rstd = sb("rstd", [128, 2])

        gT32 = sb("gT32", [128, NB, 128])
        gTh, gTl = sb("gTh", [128, NB * 128], F16), sb("gTl", [128, NB * 128], F16)
        rt = sb("rt", [128, 8, NB, NE])
        rt64 = sb("rt64", [128, 2, NB, NE, NE])
        rts = sb("rts", [128, 4, NB])
        ffn_buf = sb("ffn_buf", [128, 3, 2, 512])
        G, Hh = ffn_buf[:, 0], ffn_buf[:, 1]
        yw = ffn_buf[:, 2].rearrange("p a (b c) -> p a b c", b=NB)
        wtmp = ffn_buf[:].rearrange("p a b c -> p (a b c)")[:, 0:NE * FF].rearrange("p (e f) -> p e f", e=NE)
        acc = sb("acc", [128, NB, 128])
        dacc = sb("dacc", [128, NB, 128])
        facc = sb("facc", [128, NB, 128])
        gst = {s: sb(f"gst{s}", [128, NB, 6]) for s in "CDF"}
        gmv = {s: sb(f"gmv{s}", [128, NB, 2]) for s in "CDF"}
        gve = {s: sb(f"gve{s}", [128, NB]) for s in "CDF"}
        grs = {s: sb(f"grs{s}", [128, NB]) for s in "CDF"}
        dT = sb("dT", [128, NB, 128])
        dcol = sb("dcol", [128, 8, NB])
        drow = sb("drow", [NB, 4, 128])
        dstat = sb("dstat", [NB, 4])
        fq = sb("fq", [128, 3, NB, 128])
        fsc = sb("fsc", [128, 4, NB])
        f16T = sb("f16T", [128, NB, 128], F16)

        s_const = sem("s_const")
        s_wtmp, s_ffn_w, s_ffn_split = sem("s_wtmp"), sem("s_ffn_w"), sem("s_ffn_split")
        s_w = sem("s_w")
        s_setup_dve, s_setup_act, s_setup_pe, s_setup_pool = (sem(f"s_setup_{n}") for n in ("dve", "act", "pe", "pool"))
        s_x, s_ctxB, s_ctxE, s_mask1, s_yout_free = sem("s_x"), sem("s_ctxB"), sem("s_ctxE"), sem("s_mask1"), sem("s_yout_free")
        s_xT, s_xT_ev = sem("s_xT"), sem("s_xT_ev")
        s_proj, s_proj_ev, s_qT_ev = sem("s_proj"), sem("s_proj_ev"), sem("s_qT_ev")
        s_hi, s_split, s_vhi, s_vsplit = sem("s_hi"), sem("s_split"), sem("s_vhi"), sem("s_vsplit")
        s_splitT, s_splitT_ev = sem("s_splitT"), sem("s_splitT_ev")
        s_score, s_max, s_shift, s_exp = (sem(n) for n in ("s_score", "s_max", "s_shift", "s_exp"))
        s_PT, s_PTh, s_PTl, s_pv = sem("s_PT"), sem("s_PTh"), sem("s_PTl"), sem("s_pv")
        s_pch, s_pcl = sem("s_pch"), sem("s_pcl")
        s_rz, s_rzt, s_yo = sem("s_rz"), sem("s_rzt"), sem("s_yo")
        s_rl, s_rlh, s_rll, s_pcs, s_vp, s_kv, s_kvm, s_lin, s_lin_ev = (sem(n) for n in (
            "s_rl", "s_rlh", "s_rll", "s_pcs", "s_vp", "s_kv", "s_kvm", "s_lin", "s_lin_ev"))
        s_y = sem("s_y")
        s_yT, s_yT_ev, s_proj_out = sem("s_yT"), sem("s_yT_ev"), sem("s_proj_out")
        s_res, s_resb, s_st, s_mv, s_ve, s_rstd = (sem(n) for n in ("s_res", "s_resb", "s_st", "s_mv", "s_ve", "s_rstd"))
        s_ln = {"A": sem("s_lnA"), "B": sem("s_lnB"), "E": sem("s_lnE")}
        s_gT, s_gT_ev, s_gTl = sem("s_gT"), sem("s_gT_ev"), sem("s_gTl")
        s_rt, s_rt_dve, s_rt_exp = sem("s_rt"), sem("s_rt_dve"), sem("s_rt_exp")
        s_gate, s_val, s_gelu, s_h, s_y2, s_yw, s_acc = (sem(n) for n in (
            "s_gate", "s_val", "s_gelu", "s_h", "s_y2", "s_yw", "s_acc"))
        s_gst, s_gmv, s_gve, s_grs, s_gln = ({s: sem(f"s_{n}{s}") for s in "CDF"}
                                             for n in ("gst", "gmv", "gve", "grs", "gln"))
        s_dpe, s_ddve, s_dact = sem("s_dpe"), sem("s_ddve"), sem("s_dact")
        s_fpool, s_fcopy = sem("s_fpool"), sem("s_fcopy")
        s_fpe, s_fdve, s_fact = sem("s_fpe"), sem("s_fdve"), sem("s_fact")

        block = ctx.enter_context(nc.Block())

        def mw(st):
            return S if st == "A" else S2

        wbase = {"A": 0, "B": 4, "E": 8}
        x_of = {"A": x0, "B": xa, "E": xd}
        dst_of = {"A": xa, "B": xb, "E": xe}

        RTD = 12
        DPE, DDVE, DACT = 11, 18, 4
        FDVE = 10

        @block.sync
        def _(sp):
            def load_x(n):
                reach(sp, s_ln["A"], NB * n)
                sp.dma_start(x0[:], x_d[bass.ds(n * NB, NB)].rearrange("b t d -> t b d")).then_inc(s_x, 16)

            def load_ctxB(n):
                reach(sp, s_ln["B"], NB * n)
                sp.dma_start(ctxB[0:S2], ctx_d[bass.ds(n * NB, NB)].rearrange("b t d -> t b d")).then_inc(s_ctxB, 16)

            def load_E(n, last):
                if last:
                    sp.wait_ge(s_xT, last[3] + 1)
                sp.dma_start(ctxE[0:S2], ctx_d[bass.ds(n * NB, NB)].rearrange("b t d -> t b d")).then_inc(s_ctxE, 16)
                if last:
                    sp.wait_ge(s_max, 4 * last[3] + 4)
                sp.dma_start(mask1[:], mask1_d[bass.ds(n * NB, NB)].rearrange("b o t m -> t (b o) m")).then_inc(s_mask1, 16)

            def store(n):
                sp.wait_ge(s_gln["F"], NB * n + NB)
                sp.dma_start(out_d[bass.ds(n * NB, NB)].rearrange("b t d -> t b d"), yout[:]).then_inc(s_yout_free, 16)

            sp.dma_start(w[:, 0:4, :], w_d[0:4].rearrange("m p c -> p m c")).then_inc(s_w, 16)
            load_x(0)
            for dst, src in (
                (ident[:], ident_d), (causal[:], causal_d), (mix[0:SEG, 0:1], terrace_d), (mix[SEG:128, 0:1], terrace_d),
                (decay[:], decay_d), (mega[:], mega_d.partition_broadcast(SEG)), (mask0[:], mask0_d[0, 0]),
                (bias[:].rearrange("p m c -> p (m c)"), bias_d.partition_broadcast(128)),
            ):
                sp.dma_start(dst, src).then_inc(s_const, 16)
            sp.dma_start(wtmp, w1_d.rearrange("e d f -> d e f")).then_inc(s_wtmp, 16)
            for dst, src in (
                (w2[:, :, 0, :], w2_d[:, 0:128, :].rearrange("e p d -> p e d")),
                (w2[:, :, 1, :], w2_d[:, 128:256, :].rearrange("e p d -> p e d")),
                (w2[0:96, :, 2, :], w2_d[:, 256:352, :].rearrange("e p d -> p e d")),
            ):
                sp.dma_start(dst, src).then_inc(s_ffn_w, 16)
            sp.wait_ge(s_setup_pool, 1)
            load_ctxB(0)
            load_x(1)
            sp.wait_ge(s_ffn_split, 4)
            sp.dma_start(wtmp, v1_d.rearrange("e d f -> d e f")).then_inc(s_wtmp, 16)
            for i in range(1, FIRST_FULL):
                load_ctxB(i)
                if i >= 2:
                    load_E(i - 2, slot_at(i, E_LAST))
                load_x(i + 1)
            with sp.Fori(FIRST_FULL, NG - 1) as i:
                load_ctxB(i)
                store(i - 4)
                load_E(i - 2, slot_at(i, E_LAST))
                load_x(i + 1)
            load_ctxB(NG - 1)
            for i in range(NG - 1, LAST + 1):
                store(i - 4)
                if i < NG + 2:
                    load_E(i - 2, slot_at(i, E_LAST))
            sp.wait_ge(s_yout_free, 16 * (NG + 1))

        n_const = 16 * 14

        @block.tensor
        def _(pe):
            pe.wait_ge(s_const, n_const)
            pe.wait_ge(s_w, 32)
            pe.matmul(pY[:, 0:1], w[:, 12, :], conv[:], start=True, stop=True).then_inc(s_setup_pe, 1)
            pe.wait_ge(s_setup_dve, 13)
            pe.wait_ge(s_setup_pool, 1)

            m16 = pM[:].bitcast(F16)

            def front_xT(slot):
                st, b, n, k, u = slot
                if st == "A":
                    pe.wait_ge(s_x, (n + 1) * 16)
                elif st == "B":
                    pe.wait_ge(s_ln["A"], n * NB + (b + 1))
                    pe.wait_ge(s_ctxB, (n + 1) * 16)
                else:
                    pe.wait_ge(s_gln["D"], n * NB + (b + 1))
                    pe.wait_ge(s_ctxE, (n + 1) * 16)
                reach(pe, s_splitT_ev, k)
                last = pe.transpose(pM[:, 0:128], x_of[st][:, b, :], ident[:])
                if st != "A":
                    last = pe.transpose(pM[:, 128:256], (ctxB if st == "B" else ctxE)[:, b, :], ident[:])
                last.then_inc(s_xT, 1)

            def front_proj(slot):
                st, b, n, k, u = slot
                pe.wait_ge(s_xT_ev, k + 1)
                base = wbase[st]
                wr = w[:].rearrange("p m c -> p (m c)")
                if st == "A":
                    pe.matmul(pM[:, 0:384], xcT[:, 0, :], wr[:, 0:384], start=True, stop=True)
                    last = pe.matmul(pM[:, 384:448], w[:, base + WQ, :], xcT[:, 0, SEG:128], start=True, stop=True)
                else:
                    pe.matmul(pM[:, 0:128], xcT[:, 0, :], w[:, base + WQ, :], start=True, stop=True)
                    last = pe.matmul(pM[:, 128:384], xcT[:, 1, :], wr[:, (base + WK) * 128:(base + WO) * 128],
                                     start=True, stop=True)
                last.then_inc(s_proj, 1)

            def scores_split(slot):
                st, b, n, k, u = slot
                pe.wait_ge(s_split, k + 1)
                pe.wait_ge(s_proj_ev, 2 * k + 2)
                if st == "A":
                    pe.wait_ge(s_qT_ev, n * NB + (b + 1))
                for r in range(2):
                    for g in range(NQ):
                        c = (r * NQ + g) * 128
                        last = pe.transpose(m16[:, c:c + 128],
                                            split[:, u % 2, r, NQ * g:NQ * g + NQ].rearrange("p j t d -> p (j t d)"),
                                            ident16[:])
                last.then_inc(s_splitT, 1)

            def scores(slot, j):
                st, b, n, k, u = slot
                if j == 0:
                    pe.wait_ge(s_splitT_ev, k + 1)
                reach(pe, s_max, 4 * k + (j - 1))
                r0 = TERM * j
                for g in range(NQ):
                    last = pe.matmul(pS[j % 2][:, 128 * g:128 * g + mw(st)], splitT[r0:r0 + 24, u % 2, 0, g, :],
                                     splitT[r0:r0 + 24, u % 2, 1, g, 0:mw(st)], start=True, stop=True)
                last.then_inc(s_score, 1)

            def probs_T(slot, j):
                st, b, n, k, u = slot
                pe.wait_ge(s_exp, 4 * k + (j + 1))
                reach(pe, s_PTl, 4 * k + j)
                for g in range(NQ):
                    last = pe.transpose(pT[0:mw(st), 128 * g:128 * g + 128], P[:, u % PBUF, j, g, 0:mw(st)], ident[:])
                last.then_inc(s_PT, 1)

            def values(slot):
                st, b, n, k, u = slot
                pe.wait_ge(s_PTl, 4 * k + 4)
                pe.wait_ge(s_vsplit, k + 1)
                reach(pe, s_res, k)
                for h in range(H):
                    o = pO[:, (DH + 1) * h:(DH + 1) * (h + 1)]
                    hi, lo = (t[0:mw(st), h % NJ, h // NJ, :] for t in (PTh[:, u % 2], PTl[:, u % 2]))
                    pe.matmul(o, hi, vh[0:mw(st), u % DEEP, h, :], start=True, stop=False)
                    pe.matmul(o, hi, vl[0:mw(st), u % DEEP, h, :], start=False, stop=False)
                    last = pe.matmul(o, lo, vh[0:mw(st), u % DEEP, h, :], start=False, stop=True)
                last.then_inc(s_pv, 1)

            def back_pcs(slot):
                st, b, n, k, u = slot
                if st != "A":
                    return
                pe.wait_ge(s_rll, n * NB + (b + 1))
                pe.wait_ge(s_pcl, n * NB + (b + 1))
                pe.wait_ge(s_yo, k + 1)
                for h in range(H):
                    x = NQ * (h % NJ) + h // NJ
                    hi, lo = (t[:, b % 2, x:x + 2, :].rearrange("p x c -> p (x c)") for t in (pch, pcl))
                    pe.matmul(pO[:, h:h + 1], hi, carry_h[:, h:h + 1], start=True, stop=False)
                    pe.matmul(pO[:, h:h + 1], hi, carry_l[:, h:h + 1], start=False, stop=False)
                    last = pe.matmul(pO[:, h:h + 1], lo, carry_h[:, h:h + 1], start=False, stop=True)
                last.then_inc(s_pcs, 1)

            def back_kv(slot):
                st, b, n, k, u = slot
                if st != "A":
                    return
                pe.wait_ge(s_vp, 2 * (n * NB + (b + 1)))
                pe.matmul(pO[:, 0:128], qk32[0:SEG, u % DEEP, 1, :], vp[:], start=True, stop=True)
                pe.matmul(pO[SEG:128, 128:128 + H], ones[0:SEG, 0:SEG], pcs[:], start=True, stop=True).then_inc(s_kv, 1)

            def back_lin(slot):
                st, b, n, k, u = slot
                if st != "A":
                    return
                pe.wait_ge(s_kvm, 2 * (n * NB + (b + 1)))
                pe.matmul(pO[SEG:128, 0:128], qT32[:, u % DEEP, :], kvm[:], start=True, stop=True).then_inc(s_lin, 1)

            def back_yT(slot):
                st, b, n, k, u = slot
                pe.wait_ge(s_yo, k + 1)
                if st == "A":
                    pe.wait_ge(s_y, n * NB + (b + 1))
                pe.transpose(pO[:, 0:128], yo[:, u % 2, :], ident[:]).then_inc(s_yT, 1)

            def back_out(slot):
                st, b, n, k, u = slot
                pe.wait_ge(s_yT_ev, k + 1)
                pe.matmul(pO[:, 0:128], yT[:], w[:, wbase[st] + WO, :], start=True, stop=True).then_inc(s_proj_out, 1)

            def ffn_xT(n):
                pe.wait_ge(s_ln["B"], NB * (n + 1))
                reach(pe, s_fdve, FDVE * (n - 3) + 9)
                for b in range(NB):
                    last = pe.transpose(pA[:, 128 * b:128 * b + 128], xb[:, b, :], ident[:])
                last.then_inc(s_gT, 1)

            def ffn_router(n):
                pe.wait_ge(s_gT_ev, 2 * n + 1)
                if isinstance(n, int) and n == 0:
                    pe.wait_ge(s_ffn_w, 16 * 3)
                    pe.wait_ge(s_ffn_split, 8)
                for b in range(NB):
                    last = pe.matmul(pY[:, NE * b:NE * b + NE], gT32[:, b, :], rw[:], start=True, stop=True)
                last.then_inc(s_rt, 1)

            def ffn_out(n, c):
                e, q, m = CH[c]
                pe.wait_ge(s_h, n * len(CH) + (c + 1))
                if q == 0:
                    if e == 0:
                        pe.wait_ge(s_rt_dve, RTD * n + 1)
                    else:
                        pe.wait_ge(s_yw, NE * n + e)
                for b in range(NB):
                    last = pe.matmul(pY[:, 128 * b:128 * b + 128], Hh[0:m, c % 2, 128 * b:128 * b + 128],
                                     w2[0:m, e, q, :], start=(q == 0 and b == 0), stop=(q == 2),
                                     skip_group_check=True)
                last.then_inc(s_y2, 1)

            def ffn_chunk(n, c):
                e, q, m = CH[c]
                for bank, hi, lo, done, free in ((pA, w1h, w1l, s_gate, s_gelu), (pB, v1h, v1l, s_val, s_h)):
                    if c == 0:
                        pe.wait_ge(s_gT_ev, 2 * n + 2)
                        pe.wait_ge(s_gTl, n + 1)
                        if bank is pB:
                            reach(pe, s_ddve, DDVE * n)
                    else:
                        pe.wait_ge(free, n * len(CH) + c)
                    fs = slice(128 * q, 128 * q + m)
                    pe.matmul(bank[0:m, :], hi[:, e, fs], gTh[:], start=True, stop=False)
                    pe.matmul(bank[0:m, :], hi[:, e, fs], gTl[:], start=False, stop=False)
                    pe.matmul(bank[0:m, :], lo[:, e, fs], gTh[:], start=False, stop=True).then_inc(done, 1)
                if c >= 1:
                    ffn_out(n, c - 1)

            def agent(n, part):
                def each(out, lhs, rhs):
                    for b in range(NB):
                        last = pe.matmul(out(b), lhs(b), rhs(b), start=True, stop=True)
                    last.then_inc(s_dpe, 1)

                needs = {2: None, 3: 1, 4: 3, 5: 6, 6: 7, 7: 8, 8: 9, 9: 12, 10: 13, 11: 14}
                col = lambda b: pY[:, b:b + 1]
                if part == 1:
                    pe.wait_ge(s_gln["C"], NB * (n + 1))
                    for b in range(NB):
                        last = pe.transpose(pY[:, 128 * b:128 * b + 128], xc[:, b, :], ident[:])
                    last.then_inc(s_dpe, 1)
                    return
                if part == 2:
                    pe.wait_ge(s_dact, DACT * n + 1)
                else:
                    pe.wait_ge(s_ddve, DDVE * n + needs[part])
                if part == 2:
                    each(col, lambda b: dT[:, b, :], lambda b: u_col[:])
                elif part == 3:
                    each(col, lambda b: xc[:, b, :], lambda b: dcol[:, 0, b:b + 1])
                elif part == 4:
                    pe.matmul(pY[0:NB, 0:128], dcol[:, 1, :], w[:, 13, :], start=True, stop=True).then_inc(s_dpe, 1)
                elif part == 5:
                    pe.matmul(pY[:, 0:NB], drow[:, 1, :], ident[0:NB, 0:NB], start=True, stop=True).then_inc(s_dpe, 1)
                elif part == 6:
                    pe.matmul(pY[:, 0:NB], w[:, 14, :], dcol[:, 2, :], start=True, stop=True).then_inc(s_dpe, 1)
                elif part == 7:
                    each(col, lambda b: dT[:, b, :], lambda b: dcol[:, 3, b:b + 1])
                elif part == 8:
                    pe.transpose(pY[0:NB, 0:128], dcol[:, 4, :], ident[:]).then_inc(s_dpe, 1)
                elif part == 9:
                    pe.matmul(pY[:, 0:NB], drow[:, 3, :], ident[0:NB, 0:NB], start=True, stop=True).then_inc(s_dpe, 1)
                elif part == 10:
                    each(col, lambda b: xc[:, b, :], lambda b: dcol[:, 5, b:b + 1])
                elif part == 11:
                    each(lambda b: pB[:, 128 * b:128 * b + 128],
                         lambda b: dcol[:, 6, b:b + 1].to_broadcast([128, 128]), lambda b: w[:, 15, :])

            def fp8_xT(n):
                pe.wait_ge(s_fpool, 3 * n + 3)
                pe.wait_ge(s_gelu, len(CH) * (min(n + 3, NG) if isinstance(n, int) else n + 3))
                for b in range(NB):
                    last = pe.transpose(pA[:, 128 * b:128 * b + 128], fq[:, 2, b, :], ident[:])
                last.then_inc(s_fpe, 1)

            def fp8_product(n):
                pe.wait_ge(s_fact, n + 1)
                for b in range(NB):
                    last = pe.matmul(pA[:, 128 * b:128 * b + 128], f16T[:, b, :], w8[:], start=True, stop=True)
                last.then_inc(s_fpe, 1)

            def between(i, p, place):
                nC, nD, _, nF = others_of(i)
                ending = nD if p <= 2 else nC
                at = (p, place)
                if nD is not None:
                    if at == (2, 0):
                        ffn_out(nD, len(CH) - 1)
                    if at in AGENT_PE:
                        for part in AGENT_PE[at]:
                            agent(nD, part)
                if nF is not None:
                    if at == (2, 0):
                        fp8_xT(nF)
                    if at == (2, 1):
                        fp8_product(nF)
                if nC is not None:
                    if at == (5, 1):
                        ffn_xT(nC)
                    if at == (5, 3):
                        ffn_router(nC)
                if ending is not None:
                    for c in CHUNKS_AT.get(at, ()):
                        ffn_chunk(ending, c)

            def step(i, p):
                f, g, v, b = (slot_at(i, p - lag) for lag in (0, 1, 3, 4))
                early = b and b[0] != "A"
                if g: scores_split(g)
                if v: probs_T(v, 0)
                if b: values(b)
                if f: front_xT(f)
                between(i, p, 0)
                if g: scores(g, 0)
                if g: scores(g, 1)
                if b: back_pcs(b)
                if early: back_yT(b)
                if v: probs_T(v, 1)
                between(i, p, 1)
                if early: back_out(b)
                if b: back_kv(b)
                if f: front_proj(f)
                if v: probs_T(v, 2)
                if b: back_lin(b)
                between(i, p, 2)
                if g: scores(g, 2)
                if b and not early: back_yT(b)
                if g: scores(g, 3)
                if v: probs_T(v, 3)
                if b and not early: back_out(b)
                between(i, p, 3)

            program(pe, step)

        @block.scalar
        def _(act):
            for dst, src in (
                (w[:, 4:16, :], w_d[4:16].rearrange("m p c -> p m c")), (conv[:], conv_d),
                (block_diag[:], block_d), (lower[:], lower_d), (rw[:], rw_d),
                (w8raw[:], w8_d), (wscale[:], wscale_d.partition_broadcast(128)),
            ):
                act.dma_start(dst, src).then_inc(s_w if dst.shape == w[:, 4:16, :].shape else s_const, 16)
            act.wait_ge(s_const, n_const)
            act.activation(mix[:, 1:2], mix[:, 0:1], ACT.Exp, scale=-1.0).then_inc(s_setup_act, 1)
            act.activation(decay[:], decay[:], ACT.Exp).then_inc(s_setup_act, 1)
            act.activation(mega[:], mega[:], ACT.Exp, scale=float(SEG)).then_inc(s_setup_act, 1)
            act.activation(ident16[:], ident[:], ACT.Copy).then_inc(s_setup_act, 1)

            def front_xT(slot):
                st, b, n, k, u = slot
                act.wait_ge(s_xT, k + 1)
                reach(act, s_proj, k)
                width = 1 if st == "A" else 2
                act.activation(xcT[:, 0:width, :], pM[:, 0:128 * width].rearrange("p (a c) -> p a c", a=width),
                               ACT.Copy).then_inc(s_xT_ev, 1)

            def front_proj(slot):
                st, b, n, k, u = slot
                if st == "B":
                    return
                act.wait_ge(s_proj, k + 1)
                reach(act, s_proj_out, k - DEEP + 1)
                act.activation(qk32[:, u % DEEP].rearrange("p a c -> p (a c)"), pM[:, 0:256], ACT.Copy)\
                    .then_inc(s_proj_ev, 1)
                act.activation(v32[:, u % DEEP, :], pM[:, 256:384], ACT.Copy).then_inc(s_proj_ev, 1)
                if st == "A":
                    act.activation(qT32[:, u % DEEP, :], pM[:, 384:448], ACT.Copy).then_inc(s_qT_ev, 1)

            def scores_split(slot):
                st, b, n, k, u = slot
                act.wait_ge(s_splitT, k + 1)
                reach(act, s_score, 4 * k - 4)
                act.activation(splitT[:, u % 2].rearrange("p r g c -> p (r g c)"), m16, ACT.Copy)\
                    .then_inc(s_splitT_ev, 1)

            def exp(slot, j):
                st, b, n, k, u = slot
                act.wait_ge(s_shift, 4 * k + (j + 1))
                t = P[:, u % PBUF, j, :, 0:mw(st)]
                act.activation(t, t, ACT.Exp).then_inc(s_exp, 1)

            def probs_hi(slot, j):
                st, b, n, k, u = slot
                act.wait_ge(s_PT, 4 * k + (j + 1))
                if j == 0:
                    reach(act, s_pv, k - 1)
                act.activation(PTh[0:mw(st), u % 2, j, :, :], pT[0:mw(st), :].rearrange("p (g l) -> p g l", g=NQ), ACT.Copy)\
                    .then_inc(s_PTh, 1)

            def carry_hi(slot):
                st, b, n, k, u = slot
                if st != "A":
                    return
                act.wait_ge(s_exp, 4 * k + 4)
                reach(act, s_pcs, n * NB + (b - 1))
                act.activation(pch[:, b % 2, 0:H, :], P[0:SEG, u % PBUF, :, :, 0:SEG].rearrange("p j g c -> p (j g) c"),
                               ACT.Copy).then_inc(s_pch, 1)

            def back_yT(slot):
                st, b, n, k, u = slot
                act.wait_ge(s_yT, k + 1)
                act.activation(yT[:], pO[:, 0:128], ACT.Copy).then_inc(s_yT_ev, 1)

            def ffn_xT(n):
                act.wait_ge(s_gT, n + 1)
                act.activation(gT32[:].rearrange("p b c -> p (b c)"), pA[:], ACT.Copy).then_inc(s_gT_ev, 1)
                act.activation(gTh[:], pA[:], ACT.Copy).then_inc(s_gT_ev, 1)

            def ffn_router(n):
                act.wait_ge(s_rt_dve, RTD * n + 3)
                act.activation(rt[:, 2], rt[:, 1], ACT.Exp).then_inc(s_rt_exp, 1)

            def ffn_chunk(n, c):
                e, q, m = CH[c]
                act.wait_ge(s_gate, n * len(CH) + (c + 1))
                if c >= 2:
                    act.wait_ge(s_h, n * len(CH) + (c - 1))
                act.activation(G[0:m, c % 2, :], pA[0:m, :], ACT.Gelu).then_inc(s_gelu, 1)

            def agent_xT(n):
                act.wait_ge(s_dpe, DPE * n + 1)
                act.activation(dT[:].rearrange("p b c -> p (b c)"), pY[:], ACT.Copy).then_inc(s_dact, 1)

            def agent_token(n):
                act.wait_ge(s_ddve, DDVE * n + 2)
                act.activation(dcol[:, 7, :], dcol[:, 7, :], ACT.Exp).then_inc(s_dact, 1)

            def agent_exp(n, dve_step, row, stat):
                act.wait_ge(s_ddve, DDVE * n + dve_step)
                act.activation(drow[:, row, :], pY[0:NB, 0:128], ACT.Exp, bias=dstat[:, stat:stat + 1],
                               accum_out=dstat[:, stat + 1:stat + 2]).then_inc(s_dact, 1)

            def fp8_xT(n):
                act.wait_ge(s_fpe, 2 * n + 1)
                act.activation(f16T[:].rearrange("p b c -> p (b c)"), pA[:], ACT.Copy).then_inc(s_fact, 1)

            def between(i, p, place):
                nC, nD, _, nF = others_of(i)
                ending = nD if p <= 2 else nC
                at = (p, place)
                if nD is not None:
                    for part in AGENT_PE.get(at, ()):
                        if part == 1: agent_xT(nD)
                        if part == 2: agent_token(nD)
                        if part == 4: agent_exp(nD, 4, 0, 0)
                        if part == 8: agent_exp(nD, 10, 2, 2)
                if nF is not None and at == (2, 0):
                    fp8_xT(nF)
                if nC is not None:
                    if at == (5, 1):
                        ffn_xT(nC)
                    if at == (6, 1):
                        ffn_router(nC)
                if ending is not None:
                    for c in CHUNKS_AT.get(at, ()):
                        ffn_chunk(ending, c)

            def step(i, p):
                f, g, m, v, b = (slot_at(i, p - lag) for lag in (0, 1, 2, 3, 4))
                early = b and b[0] != "A"
                if g: scores_split(g)
                if v: probs_hi(v, 0)
                if f: front_xT(f)
                between(i, p, 0)
                if m: exp(m, 0)
                if early: back_yT(b)
                if v: probs_hi(v, 1)
                if m: exp(m, 1)
                between(i, p, 1)
                if f: front_proj(f)
                if m: exp(m, 2)
                if v: probs_hi(v, 2)
                between(i, p, 2)
                if m: exp(m, 3)
                if b and not early: back_yT(b)
                if v: probs_hi(v, 3)
                between(i, p, 3)
                if v: carry_hi(v)

            m16 = pM[:].bitcast(F16)
            program(act, step)

        @block.gpsimd
        def _(pool):
            for t in (ctxB, ctxE, split, vl, pch, pcl):
                pool.memset(t[:], 0.0)
            pool.memset(vh[:], 1.0)
            pool.memset(half[:], -0.5)
            pool.memset(ones[:], 1.0).then_inc(s_setup_pool, 1)
            pool.wait_ge(s_const, n_const)

            def carry_pool(c):
                pool.tensor_tensor(idle_pool[:, c:c + 1], half[:, 0:1], half[:, 0:1], ALU.add)

            def halves(out, in_):
                return pool.tensor_scalar(out, in_, 1.0, 1.0, ALU.mult, ALU.mult)

            def front_split(slot):
                st, b, n, k, u = slot
                pool.wait_ge(s_proj_ev, 2 * k + 2)
                reach(pool, s_splitT, k - 1)
                carry_pool(0)
                qk = qk32[:, u % DEEP].rearrange("p r (h d) -> p r h d", h=H)
                v = v32[:, u % DEEP].rearrange("p (h d) -> p h d", h=H)
                t = split[:, u % 2]
                halves(t[:, :, :, 0, :], qk)
                halves(t[:, 0, :, 1, :], qk[:, 0])
                halves(t[:, 1, :, 2, :], qk[:, 1]).then_inc(s_hi, 1)
                halves(vh[:, u % DEEP, :, 0:DH], v).then_inc(s_vhi, 1)
                pool.wait_ge(s_hi, k + 1)
                pool.tensor_tensor(t[:, 0, :, 2, :], qk[:, 0], t[:, 0, :, 0, :], ALU.subtract)
                pool.tensor_tensor(t[:, 1, :, 1, :], qk[:, 1], t[:, 1, :, 0, :], ALU.subtract).then_inc(s_split, 1)
                pool.wait_ge(s_vhi, k + 1)
                pool.tensor_tensor(vl[:, u % DEEP, :, 0:DH], v, vh[:, u % DEEP, :, 0:DH], ALU.subtract)\
                    .then_inc(s_vsplit, 1)

            def shift(slot, j):
                st, b, n, k, u = slot
                pool.wait_ge(s_max, 4 * k + (j + 1))
                t = P[:, u % PBUF, j, :, 0:mw(st)]
                pool.tensor_tensor(t, t, smax[:, u % PBUF, j, :].unsqueeze(2).to_broadcast([128, NQ, mw(st)]),
                                   ALU.subtract).then_inc(s_shift, 1)

            def carry_lo(slot):
                st, b, n, k, u = slot
                if st != "A":
                    return
                pool.wait_ge(s_pch, n * NB + (b + 1))
                pool.tensor_tensor(pcl[:, b % 2, 0:H, :],
                                   P[0:SEG, u % PBUF, :, :, 0:SEG].rearrange("p j g c -> p (j g) c"),
                                   pch[:, b % 2, 0:H, :], ALU.subtract).then_inc(s_pcl, 1)

            def back_rstd(slot):
                st, b, n, k, u = slot
                pool.wait_ge(s_ve, k + 1)
                pool.tensor_tensor(rstd[:, u % 2:u % 2 + 1], ve[:, u % 2:u % 2 + 1], half[:, 0:1], ALU.pow)\
                    .then_inc(s_rstd, 1)

            def group_rstd(s, n):
                pool.wait_ge(s_gve[s], n + 1)
                pool.tensor_tensor(grs[s][:], gve[s][:], half[:], ALU.pow).then_inc(s_grs[s], 1)

            def split_weights(hi, lo, a):
                t = ffn_buf[:].rearrange("p a b c -> p (a b c)")[:, 0:NE * FF]
                pool.wait_ge(s_wtmp, 16 * (a + 1))
                flat = lambda w: w[:].rearrange("p e f -> p (e f)")
                halves(flat(hi), t).then_inc(s_ffn_split, 2)
                pool.wait_ge(s_ffn_split, 4 * a + 2)
                pool.tensor_tensor(flat(lo), t, flat(hi), ALU.subtract).then_inc(s_ffn_split, 2)

            def ffn_start(n):
                pool.wait_ge(s_gT_ev, 2 * n + 2)
                pool.tensor_tensor(gTl[:], gT32[:].rearrange("p b c -> p (b c)"), gTh[:], ALU.subtract)\
                    .then_inc(s_gTl, 1)

            def ffn_acc(n):
                reach(pool, s_gln["C"], NB * n)
                pool.tensor_tensor(acc[:], xb[:], bias[:, 4, :].unsqueeze(1).to_broadcast([128, NB, 128]), ALU.add)\
                    .then_inc(s_acc, 1)

            def ffn_add(n, e):
                pool.wait_ge(s_acc, (NE + 1) * n + (e + 1))
                pool.wait_ge(s_yw, NE * n + (e + 1))
                pool.tensor_tensor(acc[:], acc[:], yw[:, e % 2], ALU.add).then_inc(s_acc, 1)

            def fp8_copy(n):
                pool.wait_ge(s_ln["E"], NB * (n + 1))
                reach(pool, s_fdve, FDVE * n)
                carry_pool(1)
                halves(xf[:].rearrange("p b c -> p (b c)"), xe[:].rearrange("p b c -> p (b c)")).then_inc(s_fcopy, 1)

            def fp8_scaled(n):
                pool.wait_ge(s_fdve, FDVE * n + 3)
                pool.tensor_tensor(fq[:, 0], xf[:], fsc[:, 2, :].unsqueeze(2).to_broadcast([128, NB, 128]), ALU.mult)\
                    .then_inc(s_fpool, 1)

            def fp8_round(n):
                pool.wait_ge(s_fdve, FDVE * n + 5)
                pool.tensor_tensor(fq[:, 0], fq[:, 0], fq[:, 1], ALU.add).then_inc(s_fpool, 1)
                pool.wait_ge(s_fpool, 3 * n + 2)
                pool.tensor_tensor(fq[:, 2], fq[:, 0], fq[:, 1], ALU.subtract).then_inc(s_fpool, 1)

            def between(i, p, place):
                nC, nD, nCopy, nF = others_of(i)
                ending = nD if p <= 2 else nC
                at = (p, place)
                if isinstance(i, int) and i == 0 and place == 0:
                    if p == 4: split_weights(w1h, w1l, 0)
                    if p == 9: split_weights(v1h, v1l, 1)
                if nD is not None:
                    if at == (1, 3):
                        ffn_add(nD, NE - 1)
                        group_rstd("C", nD)
                    if at == (6, 0):
                        group_rstd("D", nD)
                if nCopy is not None and at == (11, 0):
                    fp8_copy(nCopy)
                if nF is not None:
                    if at == (0, 2):
                        fp8_scaled(nF)
                    if at == (1, 2):
                        fp8_round(nF)
                    if at == (4, 1):
                        group_rstd("F", nF)
                if nC is not None:
                    if at == (5, 2):
                        ffn_start(nC)
                    if at == (6, 2):
                        ffn_acc(nC)
                if ending is not None:
                    for c in CHUNKS_AT.get(at, ()):
                        if c > 0 and c % 3 == 0:
                            ffn_add(ending, c // 3 - 1)

            def step(i, p):
                f, g, v, b = (slot_at(i, p - lag) for lag in (0, 1, 3, 4))
                between(i, p, 0)
                if g: shift(g, 0)
                if g: shift(g, 1)
                if f: front_split(f)
                between(i, p, 1)
                between(i, p, 2)
                if v: carry_lo(v)
                if b: back_rstd(b)
                if g: shift(g, 2)
                if g: shift(g, 3)
                between(i, p, 3)

            program(pool, step)

        @block.vector
        def _(dve):
            def carry_dve(c):
                dve.memset(idle[:, c:c + 1], 0.0)

            done_setup = [0]

            def step(ins):
                done_setup[0] += 1
                ins.then_inc(s_setup_dve, 1)
                dve.wait_ge(s_setup_dve, done_setup[0])

            dve.memset(idle[:, 0:1], 0.0).then_inc(s_yout_free, 16)
            dve.wait_ge(s_const, n_const)
            dve.wait_ge(s_w, 32)
            dve.wait_ge(s_setup_act, 4)
            rs8 = 1.0 / float(np.sqrt(DH))
            for a in (0, 4, 8):
                dve.tensor_scalar(w[:, a, :], w[:, a, :], rs8, None, ALU.mult)
            dve.tensor_scalar(bias[:, 0, :], bias[:, 0, :], rs8, None, ALU.mult)
            step(dve.tensor_scalar(mask0[:], mask0[:], NEG, None, ALU.mult))
            step(dve.tensor_scalar(mix[:, 1:2], mix[:, 1:2], 1.0, None, ALU.add))
            step(dve.reciprocal(mix[:, 2:3], mix[:, 1:2]))
            step(dve.tensor_scalar(mix[:, 3:4], mix[:, 2:3], -1.0, 1.0, ALU.mult, ALU.add))
            step(dve.tensor_scalar(mega[:], mega[:], 0.0, 2.0, ALU.max, ALU.min))
            step(dve.tensor_scalar(mega[:], mega[:], 0.0, None, ALU.mult))
            step(dve.tensor_tensor(decay[:], decay[:], mega[:], ALU.add))
            step(dve.tensor_copy(w8i[:, 0, :], w8raw[:]))
            dve.tensor_scalar(w8i[:, 1, :], w8i[:, 0, :], 3, 15, ALU.logical_shift_right, ALU.bitwise_and)
            dve.tensor_scalar(w8i[:, 2, :], w8i[:, 0, :], 7, None, ALU.bitwise_and)
            step(dve.tensor_scalar(w8i[:, 3, :], w8i[:, 0, :], 7, None, ALU.logical_shift_right))
            dve.tensor_scalar(w8f[:, 0, :], w8i[:, 1, :], 0.0, 8.0, ALU.is_gt, ALU.mult)
            dve.tensor_scalar(w8i[:, 1, :], w8i[:, 1, :], 1.0, 117.0, ALU.max, ALU.add)
            step(dve.tensor_scalar(w8f[:, 1, :], w8i[:, 3, :], -2.0, 1.0, ALU.mult, ALU.add))
            dve.tensor_scalar(w8i[:, 1, :], w8i[:, 1, :], 23, None, ALU.logical_shift_left)
            step(dve.tensor_tensor(w8f[:, 0, :], w8f[:, 0, :], w8i[:, 2, :], ALU.add))
            step(dve.tensor_tensor(w8f[:, 0, :], w8f[:, 0, :], w8f[:, 1, :], ALU.mult))
            dve.tensor_tensor(w8[:], w8f[:, 0, :], w8i[:, 1, :].bitcast(F32), ALU.mult)
            dve.wait_ge(s_setup_pe, 1)
            step(dve.tensor_copy(u_col[:], pY[:, 0:1]))

            def front_proj(slot):
                st, b, n, k, u = slot
                if st != "B":
                    return
                dve.wait_ge(s_proj, k + 1)
                reach(dve, s_proj_out, k - DEEP + 1)
                dve.tensor_tensor(qk32[:, u % DEEP].rearrange("p a c -> p (a c)"), pM[:, 0:256],
                                  bias[:, 0:2, :].rearrange("p a c -> p (a c)"), ALU.add).then_inc(s_proj_ev, 1)
                dve.tensor_tensor(v32[:, u % DEEP, :], pM[:, 256:384], bias[:, 2, :], ALU.add).then_inc(s_proj_ev, 1)

            def scores(slot, j, old=None):
                st, b, n, k, u = slot
                m = mw(st)
                dve.wait_ge(s_score, 4 * k + (j + 1))
                if j == 0:
                    reach(dve, s_PTl, 4 * (k - PBUF + 1))
                    if old and old[0] == "A":
                        dve.wait_ge(s_pcl, old[2] * NB + (old[1] + 1))
                if st == "E" and j == 0:
                    dve.wait_ge(s_mask1, (n + 1) * 16)
                carry_dve(j % 2)
                mask = {"A": causal[:], "B": mask0[:], "E": mask1[:, b, :]}[st]
                for g in range(NQ):
                    last = dve.tensor_tensor_reduce(P[:, u % PBUF, j, g, 0:m], pS[j % 2][:, 128 * g:128 * g + m], mask,
                                                    1.0, -3e38, ALU.add, ALU.max, smax[:, u % PBUF, j, g:g + 1])
                last.then_inc(s_max, 1)

            def probs_lo(slot, j):
                st, b, n, k, u = slot
                dve.wait_ge(s_PTh, 4 * k + (j + 1))
                if j == 0:
                    reach(dve, s_pv, k - 1)
                dve.tensor_tensor(PTl[0:mw(st), u % 2, j, :, :], pT[0:mw(st), :].rearrange("p (g l) -> p g l", g=NQ),
                                  PTh[0:mw(st), u % 2, j, :, :], ALU.subtract).then_inc(s_PTl, 1)

            def oview():
                return pO[:, 0:H * (DH + 1)].rearrange("p (h d) -> p h d", h=H)

            def back_y(slot):
                st, b, n, k, u = slot
                i = u % 2
                na = n * NB + (b + 1)
                dve.wait_ge(s_pv, k + 1)
                dve.reciprocal(rz[:, i, :], oview()[:, :, DH]).then_inc(s_rz, 1)
                dve.wait_ge(s_rz, k + 1)
                if st == "A":
                    dve.tensor_tensor(carry_w[:], rz[0:SEG, i, :], decay[:], ALU.mult).then_inc(s_rl, 1)
                    dve.wait_ge(s_rl, na)
                    dve.tensor_scalar(rz[:, i, :], rz[:, i, :], mix[:, 2:3], None, ALU.mult).then_inc(s_rzt, 1)
                    dve.tensor_copy(carry_h[:], carry_w[:]).then_inc(s_rlh, 1)
                    dve.wait_ge(s_rzt, na)
                last = dve.tensor_tensor(yo[:, i, :].rearrange("p (h d) -> p h d", h=H), oview()[:, :, 0:DH],
                                         rz[:, i, :].unsqueeze(2).to_broadcast([128, H, DH]), ALU.mult)
                last.then_inc(s_yo, 1)
                if st == "A":
                    dve.wait_ge(s_rlh, na)
                    dve.tensor_tensor(carry_l[:], carry_w[:], carry_h[:], ALU.subtract).then_inc(s_rll, 1)

            def back_vp(slot):
                st, b, n, k, u = slot
                if st != "A":
                    return
                dve.wait_ge(s_pcs, n * NB + (b + 1))
                dve.tensor_tensor(vp[:].rearrange("p (h d) -> p h d", h=H),
                                  v32[0:SEG, u % DEEP, :].rearrange("p (h d) -> p h d", h=H),
                                  pO[0:SEG, 0:H].unsqueeze(2).to_broadcast([SEG, H, DH]), ALU.mult).then_inc(s_vp, 1)
                dve.tensor_copy(pcs[:], pO[0:SEG, 0:H]).then_inc(s_vp, 1)

            def back_kvm(slot):
                st, b, n, k, u = slot
                if st != "A":
                    return
                dve.wait_ge(s_kv, n * NB + (b + 1))
                dve.tensor_scalar(rsum[SEG:128, :], pO[SEG:128, 128:128 + H], EPS, None, ALU.add)\
                    .then_inc(s_kvm, 1)
                dve.tensor_tensor(kvm[:], pO[:, 0:128], block_diag[:], ALU.mult).then_inc(s_kvm, 1)
                na = n * NB + b
                dve.wait_ge(s_kvm, 2 * na + 1)
                dve.reciprocal(rsum[SEG:128, :], rsum[SEG:128, :]).then_inc(s_lin_ev, 1)
                dve.wait_ge(s_lin_ev, 3 * na + 1)
                dve.tensor_scalar(rsum[SEG:128, :], rsum[SEG:128, :], mix[SEG:128, 3:4], None, ALU.mult)\
                    .then_inc(s_lin_ev, 1)

            def back_ylin(slot):
                st, b, n, k, u = slot
                if st != "A":
                    return
                na = n * NB + b
                dve.wait_ge(s_lin_ev, 3 * na + 2)
                dve.wait_ge(s_lin, na + 1)
                dve.tensor_tensor(ylin[SEG:128, :].rearrange("p (h d) -> p h d", h=H),
                                  pO[SEG:128, 0:128].rearrange("p (h d) -> p h d", h=H),
                                  rsum[SEG:128, :].unsqueeze(2).to_broadcast([SEG, H, DH]), ALU.mult)\
                    .then_inc(s_lin_ev, 1)
                dve.wait_ge(s_lin_ev, 3 * na + 3)
                dve.tensor_tensor(yo[SEG:128, u % 2, :], yo[SEG:128, u % 2, :], ylin[SEG:128, :], ALU.add)\
                    .then_inc(s_y, 1)

            def back_res(slot):
                st, b, n, k, u = slot
                i = u % 2
                dve.wait_ge(s_proj_out, k + 1)
                dve.tensor_tensor(res[:, i, :], pO[:, 0:128], x_of[st][:, b, :], ALU.add).then_inc(s_res, 1)
                dve.wait_ge(s_res, k + 1)
                if st == "B":
                    dve.tensor_tensor(res[:, i, :], res[:, i, :], bias[:, 3, :], ALU.add).then_inc(s_resb, 1)
                    dve.wait_ge(s_resb, n * NB + (b + 1))
                dve.bn_stats(st6[:, i, :], res[:, i, :]).then_inc(s_st, 1)
                dve.wait_ge(s_st, k + 1)
                carry_dve(2)
                dve.bn_aggr(mv[:, i, :], st6[:, i, :]).then_inc(s_mv, 1)
                dve.wait_ge(s_mv, k + 1)
                dve.tensor_scalar(ve[:, i:i + 1], mv[:, i, 1:2], EPS, None, ALU.add).then_inc(s_ve, 1)

            def last_norm(slot):
                st, b, n, k, u = slot
                i = u % 2
                dve.wait_ge(s_rstd, k + 1)
                if st == "E":
                    reach(dve, s_fcopy, n)
                if st == "B":
                    reach(dve, s_acc, (NE + 1) * (n - 1) + 1)
                    reach(dve, s_gT, n)
                dve.tensor_scalar(dst_of[st][:, b, :], res[:, i, :], mv[:, i, 0:1], rstd[:, i:i + 1],
                                  ALU.subtract, ALU.mult).then_inc(s_ln[st], 1)

            def group_stats(s, n, src):
                for b in range(NB):
                    dve.bn_stats(gst[s][:, b, :], src[:, b, :]).then_inc(s_gst[s], 1)
                dve.wait_ge(s_gst[s], NB * n + NB)
                carry_dve(3)
                for b in range(NB):
                    dve.bn_aggr(gmv[s][:, b, :], gst[s][:, b, :]).then_inc(s_gmv[s], 1)
                dve.wait_ge(s_gmv[s], NB * n + NB)
                dve.tensor_scalar(gve[s][:], gmv[s][:, :, 1], EPS, None, ALU.add).then_inc(s_gve[s], 1)

            def group_norm(s, n, src, dst, tiles=range(NB)):
                dve.wait_ge(s_grs[s], n + 1)
                for b in tiles:
                    dve.tensor_scalar(dst[:, b, :], src[:, b, :], gmv[s][:, b, 0:1], grs[s][:, b:b + 1],
                                      ALU.subtract, ALU.mult).then_inc(s_gln[s], 1)

            def router_step(n, number, ins):
                ins.then_inc(s_rt_dve, 1)
                dve.wait_ge(s_rt_dve, RTD * n + number)

            def router_logits(n):
                dve.wait_ge(s_rt, n + 1)
                router_step(n, 1, dve.tensor_copy(rt[:, 0].rearrange("p b e -> p (b e)"), pY[:, 0:NB * NE]))
                router_step(n, 2, dve.tensor_reduce(rts[:, 0, :], rt[:, 0], AX.X, ALU.max))
                router_step(n, 3, dve.tensor_tensor(rt[:, 1], rt[:, 0],
                                                    rts[:, 0, :].unsqueeze(2).to_broadcast([128, NB, NE]), ALU.subtract))

            def router_probs(n):
                def over(t, a):
                    return t.unsqueeze(a).to_broadcast([128, NB, NE, NE])

                dve.wait_ge(s_rt_exp, n + 1)
                router_step(n, 4, dve.tensor_reduce(rts[:, 1, :], rt[:, 2], AX.X, ALU.add))
                router_step(n, 5, dve.reciprocal(rts[:, 2, :], rts[:, 1, :]))
                router_step(n, 6, dve.tensor_tensor(rt[:, 3], rt[:, 2],
                                                    rts[:, 2, :].unsqueeze(2).to_broadcast([128, NB, NE]), ALU.mult))
                router_step(n, 7, dve.tensor_tensor(rt64[:, 0], over(rt[:, 3], 2), over(rt[:, 3], 3), ALU.is_ge))
                router_step(n, 8, dve.tensor_tensor(rt64[:, 1], rt64[:, 0],
                                                    lower[:, 0:NE * NE].rearrange("p (a c) -> p a c", a=NE).unsqueeze(1)
                                                    .to_broadcast([128, NB, NE, NE]), ALU.mult))

            def router_gates(n):
                above = lower[:, NE * NE:].unsqueeze(1).to_broadcast([128, NB, NE])
                dve.tensor_reduce(rt[:, 4], rt64[:, 1], AX.X, ALU.add)
                router_step(n, 9, dve.tensor_reduce(rt[:, 5], rt64[:, 1].rearrange("p b a c -> p b c a"), AX.X, ALU.add))
                router_step(n, 10, dve.tensor_tensor(rt[:, 6], rt[:, 4], rt[:, 5], ALU.subtract))
                router_step(n, 11, dve.tensor_tensor(rt[:, 6], rt[:, 6], above, ALU.add))
                router_step(n, 12, dve.scalar_tensor_tensor(out=rt[:, 7], in0=rt[:, 6], scalar=1.5, in1=rt[:, 3],
                                                            op0=ALU.is_lt, op1=ALU.mult))

            def ffn_weigh(n, e):
                dve.wait_ge(s_y2, n * len(CH) + 3 * (e + 1))
                if e >= 2:
                    dve.wait_ge(s_acc, (NE + 1) * n + e)
                dve.tensor_tensor(yw[:, e % 2], pY[:].rearrange("p (b c) -> p b c", b=NB),
                                  rt[:, 7, :, e].unsqueeze(2).to_broadcast([128, NB, 128]), ALU.mult)\
                    .then_inc(s_yw, 1)

            def ffn_chunk(n, c):
                e, q, m = CH[c]
                dve.wait_ge(s_gelu, n * len(CH) + (c + 1))
                dve.wait_ge(s_val, n * len(CH) + (c + 1))
                if c >= 2:
                    dve.wait_ge(s_y2, n * len(CH) + (c - 1))
                dve.tensor_tensor(Hh[0:m, c % 2, :], pB[0:m, :], G[0:m, c % 2, :], ALU.mult).then_inc(s_h, 1)
                if q == 0 and e >= 1:
                    ffn_weigh(n, e - 1)

            def agent(n, part):
                def step(number, ins):
                    ins.then_inc(s_ddve, 1)
                    dve.wait_ge(s_ddve, DDVE * n + number)

                def product(i):
                    dve.wait_ge(s_dpe, DPE * n + i)

                def exped(i):
                    dve.wait_ge(s_dact, DACT * n + i)

                if part == 2:
                    product(2)
                    step(1, dve.tensor_scalar(dcol[:, 0, :], pY[:, 0:NB], float(D) ** -0.5, None, ALU.mult))
                    step(2, dve.tensor_tensor(dcol[:, 7, :], dcol[:, 0, :], dcol[:, 0, :], ALU.subtract))
                elif part == 3:
                    product(3)
                    step(3, dve.tensor_copy(dcol[:, 1, :], pY[:, 0:NB]))
                elif part == 4:
                    product(4)
                    step(4, dve.tensor_reduce(dstat[:, 0:1], pY[0:NB, 0:128], AX.X, ALU.max, negate=True))
                elif part == "softmax c":
                    exped(3)
                    step(5, dve.reciprocal(dstat[:, 1:2], dstat[:, 1:2]))
                    step(6, dve.tensor_scalar(drow[:, 1, :], drow[:, 0, :], dstat[:, 1:2], None, ALU.mult))
                elif part in (5, 6, 7):
                    product(part)
                    step(part + 2, dve.tensor_copy(dcol[:, part - 3, :], pY[:, 0:NB]))
                elif part == 8:
                    product(8)
                    step(10, dve.tensor_reduce(dstat[:, 2:3], pY[0:NB, 0:128], AX.X, ALU.max, negate=True))
                elif part == "softmax n":
                    exped(4)
                    step(11, dve.reciprocal(dstat[:, 3:4], dstat[:, 3:4]))
                    step(12, dve.tensor_scalar(drow[:, 3, :], drow[:, 2, :], dstat[:, 3:4], None, ALU.mult))
                elif part in (9, 10):
                    product(part)
                    step(part + 4, dve.tensor_copy(dcol[:, part - 4, :], pY[:, 0:NB]))
                elif part == 11:
                    product(11)
                    for b in range(NB):
                        dve.scalar_tensor_tensor(out=dacc[:, b, :], in0=pB[:, 128 * b:128 * b + 128],
                                                 scalar=dcol[:, 7, b:b + 1], in1=xc[:, b, :], op0=ALU.mult,
                                                 op1=ALU.add).then_inc(s_ddve, 1)

            def fp8_step(n, number, ins):
                ins.then_inc(s_fdve, 1)
                dve.wait_ge(s_fdve, FDVE * n + number)

            def fp8_scale(n):
                dve.wait_ge(s_fcopy, n + 1)
                fp8_step(n, 1, dve.tensor_reduce(fsc[:, 0, :], xf[:], AX.X, ALU.max, apply_absolute_value=True))
                fp8_step(n, 2, dve.tensor_scalar(fsc[:, 1, :], fsc[:, 0, :], 1e-12, 1.0 / 448.0, ALU.max, ALU.mult))
                dve.tensor_scalar(fsc[:, 3, :], fsc[:, 1, :], wscale[:, 0:1], None, ALU.mult)
                fp8_step(n, 3, dve.reciprocal(fsc[:, 2, :], fsc[:, 1, :]))

            def fp8_units(n):
                dve.wait_ge(s_fpool, 3 * n + 1)
                fp8_step(n, 4, dve.tensor_scalar(fq[:, 1].bitcast(I32), fq[:, 0].bitcast(I32), 0x7F800000, None,
                                                 ALU.bitwise_and))
                fp8_step(n, 5, dve.tensor_scalar(fq[:, 1], fq[:, 1], 2.0 ** -6, 1.5 * 2.0 ** 20, ALU.max, ALU.mult))

            def fp8_finish(n):
                dve.wait_ge(s_fpe, 2 * n + 2)
                for b in range(NB):
                    dve.scalar_tensor_tensor(out=facc[:, b, :], in0=pA[:, 128 * b:128 * b + 128],
                                             scalar=fsc[:, 3, b:b + 1], in1=bias[:, 5, :], op0=ALU.mult,
                                             op1=ALU.add).then_inc(s_fdve, 1)
                dve.wait_ge(s_fdve, FDVE * n + 9)
                fp8_step(n, 10, dve.tensor_tensor(facc[:], facc[:], xf[:], ALU.add))

            def between(i, p, place):
                nC, nD, _, nF = others_of(i)
                ending = nD if p <= 2 else nC
                at = (p, place)
                if nD is not None:
                    if at == (2, 0):
                        ffn_weigh(nD, NE - 1)
                        dve.wait_ge(s_acc, (NE + 1) * (nD + 1))
                        group_stats("C", nD, acc)
                    if at == (2, 1):
                        group_norm("C", nD, acc, xc)
                    for part in AGENT_DVE.get(at, ()):
                        agent(nD, part)
                    if at == (5, 3):
                        dve.wait_ge(s_ddve, DDVE * (nD + 1))
                        group_stats("D", nD, dacc)
                    if at == (6, 1):
                        group_norm("D", nD, dacc, xd, (0, 1))
                    if at == ((9, 3) if isinstance(nD, int) and nD == NG - 1 else (10, 1)):
                        group_norm("D", nD, dacc, xd, (2, 3))
                if nF is not None:
                    if at == (0, 2):
                        fp8_scale(nF)
                    if at == (1, 1):
                        fp8_units(nF)
                    if at == (2, 2):
                        fp8_finish(nF)
                    if at == (3, 3):
                        group_stats("F", nF, facc)
                    if at == (4, 3):
                        dve.wait_ge(s_yout_free, 16 * (nF + 1))
                        group_norm("F", nF, facc, yout)
                if nC is not None:
                    if at == (6, 0):
                        router_logits(nC)
                    if at == (7, 0):
                        router_gates(nC)
                if ending is not None:
                    for c in CHUNKS_AT.get(at, ()):
                        ffn_chunk(ending, c)
                if nC is not None:
                    if at == (6, 3):
                        router_probs(nC)

            def step(i, p):
                f, g, v, b, c = (slot_at(i, p - lag) for lag in (0, 1, 3, 4, 5))
                early = b and b[0] != "A"
                if b: back_y(b)
                if v: probs_lo(v, 0)
                between(i, p, 0)
                if b: back_vp(b)
                if g: scores(g, 0, slot_before(i, p - 1, PBUF))
                if v: probs_lo(v, 1)
                if g: scores(g, 1)
                if b: back_kvm(b)
                between(i, p, 1)
                if c: last_norm(c)
                if f: front_proj(f)
                if b: back_ylin(b)
                if early: back_res(b)
                if v: probs_lo(v, 2)
                between(i, p, 2)
                if g: scores(g, 2)
                if v: probs_lo(v, 3)
                if g: scores(g, 3)
                if b and not early: back_res(b)
                between(i, p, 3)

            dve.wait_ge(s_setup_pool, 1)
            program(dve, step)


def kernel(**inputs):
    import concourse.bacc as bacc
    from concourse.bass_utils import run_bass_kernel_spmd

    a = {k: np.ascontiguousarray(v) for k, v in inputs.items()}
    flat = lambda t: t.reshape(128, 128)
    l1 = a["L1_attn_w_qkv"]
    mats = [a["L0_attn_Wq"].T, a["L0_attn_Wk"].T, a["L0_attn_Wv"].T, a["L0_attn_Wc"].T,
            a["L0_xattn_Wq"], a["L0_xattn_Wk"], a["L0_xattn_Wv"], a["L0_xattn_Wo"],
            flat(a["L1_xattn_wq"]), flat(a["L1_xattn_wk"]), flat(a["L1_xattn_wv"]), flat(a["L1_xattn_wo"]),
            l1[0:128], l1[128:256].T, l1[256:384], l1[256:384].T]
    arrays = {
        "x": a["x"], "ctx": a["ctx_1024"], "mask0": a["mask_1x1xSxS2_fk1"], "mask1": a["mask_Bx1xSxS2_ff0"],
        "w": np.stack(mats),
        "bias": np.concatenate([a["L0_xattn_bq"], a["L0_xattn_bk"], a["L0_xattn_bv"], a["L0_xattn_bo"],
                                a["L0_ffn_bias"], a["L1_ffn_bias"]]),
        "terrace": a["L0_attn_terrace_mix"].reshape(SEG, 1),
        "decay": a["L0_attn_index_decays"].T, "mega": a["L0_attn_mega_decays"],
        "rw": a["L0_ffn_router_w"], "w1": a["L0_ffn_w1"], "v1": a["L0_ffn_v1"], "w2": a["L0_ffn_w2"],
        "conv": a["L1_attn_w_conv1"].reshape(128, 1),
        "w8": a["L1_ffn_weight"].view(np.uint8).T, "wscale": a["L1_ffn_weight_scale"].reshape(1),
        "ident": np.eye(128, dtype=np.float32),
        "causal": np.where(np.tril(np.ones((128, 128), bool)), 0.0, -1e30).astype(np.float32),
        "block": (np.kron(np.eye(H), np.ones((DH, DH))) * np.sqrt(DH)).astype(np.float32),
        "lower": np.tile(np.concatenate([np.tril(np.ones((NE, NE)), -1).ravel(), NE - 1.0 - np.arange(NE)]), (128, 1))
        .astype(np.float32),
    }
    nc = bacc.Bacc("TRN2", target_bir_lowering=False, num_devices=1)
    feeds, args = {}, []
    for name, t in arrays.items():
        t = np.ascontiguousarray(t)
        feeds[f"in_{name}"] = t
        args.append(nc.dram_tensor(f"in_{name}", t.shape, mybir.dt.from_np(t.dtype), kind="ExternalInput").ap())
    args.append(nc.dram_tensor("out_0", (NSEQ, S, D), F32, kind="ExternalOutput").ap())
    decoder(nc, *args)
    r = run_bass_kernel_spmd(nc, [feeds], core_ids=[0])
    return r.results[0]["out_0"]
```
